# Optimizing a Trainium2 kernel written in Bass

```python
import numpy as np
import jax
import jax.numpy as jnp

def _softmax(x, axis=-1):
    return jax.nn.softmax(x, axis=axis)

def _gelu(x):
    return jax.nn.gelu(x, approximate=True)

def _silu(x):
    return jax.nn.silu(x)

def _sigmoid(x):
    return jax.nn.sigmoid(x)

def _layernorm(x, axis=-1, eps=1e-05):
    m = jnp.mean(x, axis=axis, keepdims=True)
    v = jnp.var(x, axis=axis, keepdims=True)
    return (x - m) / jnp.sqrt(v + eps)

def _scatter_add(tgt, idx, src, axis=0):
    return tgt.at[idx].add(src)

def _segment_sum(src, seg, n):
    return jax.ops.segment_sum(src, seg, n)
kernel_name = 'mk_adj_ffn_d2_adj_r2_5f114c'

def setup_inputs(seed: int=0):
    np.random.seed(seed)
    _w = jnp.asarray

    def _rec_inputs():
        import jax
        import jax.numpy as jnp
        _gk = jax.random.key(seed)
        x = -0.0005207 + 1.001 * jax.random.normal(jax.random.fold_in(_gk, 1), (4096, 128), jnp.float32)
        _a = jax.random.bernoulli(jax.random.fold_in(_gk, 2), 0.000488281, (4096, 4096))
        adj = _a.astype(jnp.int32)
        return (x, adj)
    x, adj = _rec_inputs()

    def _L0_gnn_setup():
        import jax, jax.numpy as jnp
        import numpy as np
        N = 4096
        D = 128
        NEG = -1000.0
        SLOPE = 0.01
        key = jax.random.key(seed)
        k1, k2, k3, k4, k5, k6 = jax.random.split(key, 6)
        return {'query': jax.random.normal(k1, (N, D), dtype=jnp.float32), 'invocation_matrix': jax.random.randint(k2, (N, N), 0, 2, dtype=jnp.int32), 'Wq': jax.random.normal(k3, (D, D), dtype=jnp.float32) * (1.0 / np.sqrt(D)), 'Wk': jax.random.normal(k4, (D, D), dtype=jnp.float32) * (1.0 / np.sqrt(D)), 'Wv': jax.random.normal(k5, (D, D), dtype=jnp.float32) * (1.0 / np.sqrt(D)), 'a': jax.random.normal(k6, (1, 2 * D), dtype=jnp.float32)}
    _L0_gnn_all = _L0_gnn_setup()
    _L0_gnn_in = {k: v for k, v in _L0_gnn_all.items() if k in ('Wq', 'Wk', 'Wv', 'a')}
    del _L0_gnn_all

    def _L0_ffn_setup():
        import jax, jax.numpy as jnp
        import numpy as np
        C = 128
        EPS = 1e-05
        N_ITERS = 30

        def _layernorm(x, w, bias):
            mu = jnp.mean(x, axis=-1, keepdims=True)
            var = jnp.mean(jnp.square(x - mu), axis=-1, keepdims=True)
            return (x - mu) * jax.lax.rsqrt(var + EPS) * w + bias
        key = jax.random.key(seed)
        kx, kw, kb, klw, klb = jax.random.split(key, 5)
        x = jax.random.normal(kx, (8, 1024, C), dtype=jnp.float32)
        bound = 1.0 / np.sqrt(C)
        W = jax.random.uniform(kw, (C, C), minval=-bound, maxval=bound, dtype=jnp.float32)
        b = jax.random.uniform(kb, (C,), minval=-bound, maxval=bound, dtype=jnp.float32)
        ln_w = jnp.ones((C,), dtype=jnp.float32)
        ln_b = jnp.zeros((C,), dtype=jnp.float32)
        return {'x': x, 'ln_w': ln_w, 'ln_b': ln_b, 'W': W, 'b': b}
    _L0_ffn_all = _L0_ffn_setup()
    _L0_ffn_in = {k: v for k, v in _L0_ffn_all.items() if k in ('ln_w', 'ln_b', 'W', 'b')}
    del _L0_ffn_all

    def _L1_gnn_setup():
        import jax, jax.numpy as jnp
        import numpy as np
        N, FEAT = (4096, 128)
        NEG_SLOPE = 0.2
        MASK_VAL = jnp.float32(-9000000000000000.0)
        key = jax.random.key(seed)
        k1, k2, k3 = jax.random.split(key, 3)
        h = jax.random.normal(k1, (N, FEAT), dtype=jnp.float32)
        adj = jax.random.randint(k2, (N, N), 0, 2, dtype=jnp.int32)
        a = jax.random.normal(k3, (2 * FEAT, 1), dtype=jnp.float32) * 0.1
        return {'h': h, 'adj': adj, 'a': a}
    _L1_gnn_all = _L1_gnn_setup()
    _L1_gnn_in = {k: v for k, v in _L1_gnn_all.items() if k in ('a',)}
    del _L1_gnn_all

    def _L1_ffn_setup():
        import jax, jax.numpy as jnp
        import numpy as np
        D_MODEL = 128
        N_EXPERTS = 16
        HIDDEN = 256
        SCALE = 0.02
        key = jax.random.key(seed)
        ks = jax.random.split(key, 5)
        x = jax.random.normal(ks[0], (4, 4096, D_MODEL), dtype=jnp.float32)
        gate_w = jax.random.normal(ks[1], (D_MODEL, N_EXPERTS), dtype=jnp.float32) * SCALE
        gate_b = jnp.zeros((N_EXPERTS,), dtype=jnp.float32)
        w1 = jax.random.normal(ks[2], (N_EXPERTS, D_MODEL, HIDDEN), dtype=jnp.float32) * SCALE
        w2 = jax.random.normal(ks[3], (N_EXPERTS, D_MODEL, HIDDEN), dtype=jnp.float32) * SCALE
        w3 = jax.random.normal(ks[4], (N_EXPERTS, HIDDEN, D_MODEL), dtype=jnp.float32) * SCALE
        return {'x': x, 'gate_w': gate_w, 'gate_b': gate_b, 'w1': w1, 'w2': w2, 'w3': w3}
    _L1_ffn_all = _L1_ffn_setup()
    _L1_ffn_in = {k: v for k, v in _L1_ffn_all.items() if k in ('gate_w', 'gate_b', 'w1', 'w2', 'w3')}
    del _L1_ffn_all
    return {'x': x, 'adj': adj, 'L0_gnn_Wq': _L0_gnn_in['Wq'], 'L0_gnn_Wk': _L0_gnn_in['Wk'], 'L0_gnn_Wv': _L0_gnn_in['Wv'], 'L0_gnn_a': _L0_gnn_in['a'], 'L0_ffn_ln_w': _L0_ffn_in['ln_w'], 'L0_ffn_ln_b': _L0_ffn_in['ln_b'], 'L0_ffn_W': _L0_ffn_in['W'], 'L0_ffn_b': _L0_ffn_in['b'], 'L1_gnn_a': _L1_gnn_in['a'], 'L1_ffn_gate_w': _L1_ffn_in['gate_w'], 'L1_ffn_gate_b': _L1_ffn_in['gate_b'], 'L1_ffn_w1': _L1_ffn_in['w1'], 'L1_ffn_w2': _L1_ffn_in['w2'], 'L1_ffn_w3': _L1_ffn_in['w3']}

def reference(x, adj, L0_gnn_Wq, L0_gnn_Wk, L0_gnn_Wv, L0_gnn_a, L0_ffn_ln_w, L0_ffn_ln_b, L0_ffn_W, L0_ffn_b, L1_gnn_a, L1_ffn_gate_w, L1_ffn_gate_b, L1_ffn_w1, L1_ffn_w2, L1_ffn_w3):
    import jax
    import jax.numpy as jnp

    def _L0_gnn_ref(query, invocation_matrix, Wq, Wk, Wv, a):
        import jax, jax.numpy as jnp
        import numpy as np
        N = 4096
        D = 128
        NEG = -1000.0
        SLOPE = 0.01
        q = query @ Wq.T
        k = query @ Wk.T
        v = query @ Wv.T
        scores = jnp.concatenate([q, k], axis=1) @ a.T
        scores = jax.nn.leaky_relu(scores, negative_slope=SLOPE)
        scores = jnp.where(invocation_matrix == 0, jnp.float32(NEG), scores)
        attn = jax.nn.softmax(scores, axis=-1)
        return attn @ v

    def _L0_ffn_ref(x, ln_w, ln_b, W, b):
        import jax, jax.numpy as jnp
        import numpy as np
        C = 128
        EPS = 1e-05
        N_ITERS = 30

        def _layernorm(x, w, bias):
            mu = jnp.mean(x, axis=-1, keepdims=True)
            var = jnp.mean(jnp.square(x - mu), axis=-1, keepdims=True)
            return (x - mu) * jax.lax.rsqrt(var + EPS) * w + bias

        def step(h, _):
            h = h + 0.01 * jnp.tanh(h)
            h = h * jax.nn.sigmoid(h)
            h = _layernorm(h, ln_w, ln_b)
            h = jnp.einsum('bsc,dc->bsd', h, W) + b
            return (h, None)
        x, _ = jax.lax.scan(step, x, None, length=N_ITERS)
        return x

    def _L1_gnn_ref(h, adj, a):
        import jax, jax.numpy as jnp
        import numpy as np
        N, FEAT = (4096, 128)
        NEG_SLOPE = 0.2
        MASK_VAL = jnp.float32(-9000000000000000.0)
        f = h.shape[1]
        wh1 = h @ a[:f]
        wh2 = h @ a[f:]
        e = jax.nn.leaky_relu(wh1 + wh2.T, negative_slope=NEG_SLOPE)
        e = jnp.where(adj > 0, e, MASK_VAL)
        attention = jax.nn.softmax(e, axis=1)
        h_prime = attention @ h
        return h_prime

    def _L1_ffn_ref(x, gate_w, gate_b, w1, w2, w3):
        import jax, jax.numpy as jnp
        import numpy as np
        D_MODEL = 128
        N_EXPERTS = 16
        HIDDEN = 256
        SCALE = 0.02
        n_experts = w1.shape[0]
        logits = jnp.einsum('bsd,de->bse', x, gate_w) + gate_b
        probs = jax.nn.softmax(logits, axis=-1)
        top_probs, top_idx = jax.lax.top_k(probs, 2)
        top_probs = top_probs / jnp.sum(top_probs, axis=-1, keepdims=True)
        dispatch = jnp.sum(jax.nn.one_hot(top_idx, n_experts, dtype=x.dtype) * top_probs[..., None], axis=-2)
        h1 = jnp.einsum('bsd,edh->bseh', x, w1)
        h2 = jnp.einsum('bsd,edh->bseh', x, w2)
        hidden = jax.nn.silu(h1) * h2
        expert_out = jnp.einsum('bseh,eho->bseo', hidden, w3)
        return jnp.einsum('bseo,bse->bso', expert_out, dispatch)
    x = x + _L0_gnn_ref(_layernorm(x, axis=-1), adj, L0_gnn_Wq, L0_gnn_Wk, L0_gnn_Wv, L0_gnn_a)
    x = x + _L0_ffn_ref(_layernorm(x, axis=-1)[None], L0_ffn_ln_w, L0_ffn_ln_b, L0_ffn_W, L0_ffn_b)[0]
    x = x + _L1_gnn_ref(_layernorm(x, axis=-1), adj, L1_gnn_a)
    x = x + _L1_ffn_ref(_layernorm(x, axis=-1)[None], L1_ffn_gate_w, L1_ffn_gate_b, L1_ffn_w1, L1_ffn_w2, L1_ffn_w3)[0]
    return x

_drawn_inputs = setup_inputs


def setup_inputs(seed=0):
    import zlib

    import numpy as np

    out = dict(_drawn_inputs(seed))
    spreads = {'L0_ffn_ln_w': (1.0, 0.2), 'L0_ffn_ln_b': (0.0, 0.1), 'L1_ffn_gate_b': (0.0, 0.8)}
    factors = {'L1_ffn_gate_w': 8.0, 'L1_ffn_w1': 8.0, 'L1_ffn_w2': 8.0, 'L1_ffn_w3': 8.0}
    for name, (base, spread) in spreads.items():
        noise = np.random.default_rng([zlib.crc32(name.encode()), seed]).standard_normal(out[name].shape)
        drawn = base * np.exp(spread * noise) if base else spread * noise
        out[name] = jnp.asarray(drawn.astype(out[name].dtype))
    for name, factor in factors.items():
        out[name] = (out[name] * factor).astype(out[name].dtype)
    return out
```

```python
from contextlib import ExitStack

import concourse.bass as bass
from concourse import mybir

ALU = mybir.AluOpType
ACT = mybir.ActivationFunctionType
AX_X = mybir.AxisListType.X
F32 = mybir.dt.float32
BF16 = mybir.dt.bfloat16
I32 = mybir.dt.int32
U32 = mybir.dt.uint32
U8 = mybir.dt.uint8

P = 128
N = 4096
D = 128
NB = N // P
GB = 4
NG = NB // GB
GR = GB * P
JT = 2
NT = NB // JT
ITERS = 30
EPS = 1e-5
NEG = -1000.0
SLOPE0 = 0.01
SLOPE1 = 0.2
NPART = 3
VW = NPART * D + 1

RSQRT_MAGIC = float(0x5F1FFFF9)
RSQRT_K = 0.703952253
RSQRT_C = 2.38924456


class Chain:

    def __init__(self, eng, sem, base=0):
        self.eng, self.sem, self.base, self.n = eng, sem, base, 0

    def add(self, ins):
        self.n += 1
        ins.then_inc(self.sem, 1)

    def done(self):
        self.eng.wait_ge(self.sem, self.base + self.n)

    def link(self, ins):
        self.add(ins)
        self.done()


def rsqrt_start(v, y):
    return dict(out=y.bitcast(I32), in0=v.bitcast(I32), scalar1=-0.5, scalar2=RSQRT_MAGIC,
                op0=ALU.mult, op1=ALU.add)


LAG = 3


def back(it, g, lag):
    return (it, g - lag) if g >= lag else (it - 1, g - lag + NG)


assert NG == 8


def wait_use(eng, sem, it, g, slots, base=0):
    if isinstance(it, int) and it == 0 and g < slots:
        return
    eng.wait_ge(sem, it * NG + (base + g + 1 - slots))


def run(eng, step, iters=ITERS):
    for g in range(NG):
        step(0, g, first=True)
    with eng.Fori(1, iters) as it:
        for g in range(NG):
            step(it, g)
    for g in range(LAG):
        step(iters, g, last=True)


def emit_rsqrt(dve, link, v, y, t, u, newton):
    link(dve.tensor_scalar(**rsqrt_start(v, y)))
    for step in range(newton + 1):
        k, c = (RSQRT_K, RSQRT_K * RSQRT_C) if step == 0 else (0.5, 1.5)
        link(dve.tensor_tensor(t, y, y, ALU.mult))
        link(dve.scalar_tensor_tensor(u, t, -k, v, ALU.mult, ALU.mult))
        link(dve.scalar_tensor_tensor(y, u, c, y, ALU.add, ALU.mult))


def network(nc, x, adj_t, wq, wk, wv, a0, ln_w, ln_b, wf, bf, a1, gate_w, gate_b, w1, w2, w3, out,
            stop_after=9):
    with ExitStack() as ctx:
        def sb(name, shape, dt):
            return ctx.enter_context(nc.sbuf_tensor(name, shape, dt))

        def sem(name):
            return ctx.enter_context(nc.semaphore(name))

        mask_bytes = NG * NB * GR
        mask = sb("mask", [P, mask_bytes], U8)
        mask_v = mask[:, :].rearrange("p (g j i) -> p g j i", g=NG, j=NB)
        X = sb("X", [P, NB, D], F32)
        WORK = 51200
        work = sb("work", [P, WORK], U8)
        ps = ctx.enter_context(nc.psum_tensor("ps", [P, 8, 512], F32))

        def view(region, at, shape, dt, size):
            n = 1
            for s in shape:
                n *= s
            names = "abcd"[:len(shape)]
            flat = region[:, at:at + n * size].bitcast(dt)
            if len(shape) == 1:
                return flat
            return flat.rearrange(f"p ({' '.join(names)}) -> p {' '.join(names)}",
                                  **{names[i]: shape[i] for i in range(len(shape) - 1)})

        ident = sb("ident", [P, P], F32)
        ones = sb("ones", [P, P], F32)
        pool_mark = sb("pool_mark", [P, 4], F32)
        marks = sb("marks", [P, 16], F32)
        ones_bf = sb("ones_bf", [P, P], BF16)
        st6 = sb("st6", [P, NB, 6], F32)
        mv = sb("mv", [P, NB, 2], F32)
        NCOL = 16
        col = sb("col", [P, NCOL, NB], F32)
        wz = sb("wz", [P, D + 1], F32)
        wst = sb("wst", [P, D + 1], F32)
        c_col = sb("c_col", [P, 1], F32)
        c_nat = sb("c_nat", [P, D], F32)
        total = sb("total", [P, D], F32)

        v_col, y_col, t_col, u_col, s_col, cnt_col = (col[:, i, :] for i in range(6))
        e1_col, e0_col, al_col, be_col, p_col, q_col = (col[:, i, :] for i in range(6, 12))

        def dump():
            with nc.semaphore("dumped") as dumped, nc.Block() as block:
                @block.sync
                def _(sp):
                    sp.dma_start(out.rearrange("(b p) d -> p b d", p=P), X[:, :, :]).then_inc(dumped, 16)
                    sp.wait_ge(dumped, 16)

        split = view(work, 0, [NB, VW], BF16, 2)
        stage_at = (NB * VW * 2 + 63) // 64 * 64
        NS = 4
        stage = view(work, stage_at, [NS, JT, GR], I32, 4)
        M0N = 2
        conn = sb("conn", [P, M0N, JT, GR], BF16)
        xln = view(mask, 6 * NB * GR, [NB, D], F32, 4)
        xT = view(mask, 7 * NB * GR, [NB, D], F32, 4)
        rest = view(mask, 5 * NB * GR, [2, GB, D], F32, 4)
        w_in = view(mask, 4 * NB * GR, [8, D], F32, 4)
        sums = view(work, stage_at + NS * JT * GR * 4, [GB, D], F32, 4)
        sm = ctx.enter_context(nc.sbuf_tensor("small", [P, 12, 2, GB], F32))

        with ExitStack() as c1:
            def sem1(name):
                return c1.enter_context(nc.semaphore(name))

            x_in = sem1("x_in")
            w_in_s = sem1("w_in_s")
            landed = [sem1(f"landed{i}") for i in range(NS)]
            stage_free = sem1("stage_free")
            stage_free_odd = sem1("stage_free_odd")
            conn_ready = sem1("conn_ready")
            conn_free = sem1("conn_free")
            zeroed = sem1("zeroed")
            ident_ok = sem1("ident_ok")
            dchain = sem1("dchain")
            xln_ready = sem1("xln_ready")
            xT_psum = sem1("xT_psum")
            xT_ready = sem1("xT_ready")
            w_ps = sem1("w_ps")
            w_rdy = sem1("w_rdy")
            val_psum = sem1("val_psum")
            part1 = sem1("part1")
            split_ready = sem1("split_ready")
            total_psum = sem1("total_psum")
            sums_psum = sem1("sums_psum")
            sums_free = sem1("sums_free")
            a_cols = sem1("a_cols")
            exp_in = sem1("exp_in")
            exp_out = sem1("exp_out")
            achain = sem1("achain")

            evac = sem1("evac")
            EVAC = 29
            cnt, sc, sc2, mx, ncnt, w1c, w0c, al, be = (sm[:, i // 2, i % 2, :] for i in range(9))
            ind, t1, t2, ex = (sm[:, 6 + i, :, :] for i in range(4))

            def mask_at(g, c):
                return mask_v[:, bass.ds(g, 1), c * JT:(c + 1) * JT, :].rearrange("p o j i -> p (o j) i")

            block = c1.enter_context(nc.Block())
            wq_s, wk_s, wv_s, wf_s, lnw_s, lnb_s, wtmp, wtmp2 = (w_in[:, i, :] for i in range(8))
            a_col = view(mask, 4 * NB * GR + 8 * D * 4, [8], F32, 4)

            @block.sync
            def _(sp):
                sp.dma_start(X[:, :, :], x.rearrange("(b p) d -> p b d", p=P)).then_inc(x_in, 16)
                for dst, src in ((wq_s, wq), (wk_s, wk), (wv_s, wv), (wf_s, wf),
                                 (lnw_s, ln_w.partition_broadcast(P)),
                                 (lnb_s, ln_b.partition_broadcast(P)),
                                 (a_col[:, 0:2], a0),
                                 (a_col[:, 2:3], bf.rearrange("(p o) -> p o", o=1))):
                    sp.dma_start(dst, src).then_inc(w_in_s, 16)
                with sp.Fori(0, NG) as g:
                    for c in range(NT):
                        if c % 2 == 0:
                            sp.wait_ge(stage_free, g * (NT // 2) + c // 2 + 1)
                        else:
                            sp.wait_ge(stage_free_odd, g * (NT // 2) + c // 2 + 1)
                        sp.dma_start(stage[:, c % NS, :, :], adj_t[bass.ds(g, 1), c, :, :].rearrange(
                            "o p (j i) -> p (o j) i", j=JT)).then_inc(landed[c % NS], 16)

            @block.gpsimd
            def _(pool):
                pool.memset(ident[:, :], 0.0).then_inc(zeroed, 1)
                pool.wait_ge(zeroed, 1)
                pool.affine_select(out=ident[:, :], in_=ident[:, :], compare_op=ALU.not_equal, fill=1.0,
                                   base=0, pattern=[[-1, P]], channel_multiplier=1).then_inc(ident_ok, 1)
                for i in range(NS // 2):
                    pool.memset(pool_mark[:, i:i + 1], 0.0).then_inc(stage_free_odd, 1)
                for t in range(1, NG * NT, 2):
                    g, c = t // NT, t % NT
                    pool.wait_ge(conn_ready, t + 1 + NS)
                    if t == 1:
                        pool.wait_ge(sums_free, 1)
                    pool.tensor_scalar(mask_v[:, g, c * JT:(c + 1) * JT, :], stage[:, c % NS, :, :], 0.0, None,
                                       ALU.is_gt).then_inc(stage_free_odd, 1)

            @block.scalar
            def _(act):
                act.wait_ge(w_ps, 1)
                act.activation(wst[:, 0:D], ps[:, 7, 0:D], ACT.Copy).then_inc(w_rdy, 1)
                act.activation(wst[:, D:D + 1], ps[:, 6, 0:1], ACT.Copy).then_inc(w_rdy, 1)
                act.wait_ge(w_ps, 2)
                act.activation(wz[:, 0:D], ps[:, 5, 128:256], ACT.Copy).then_inc(w_rdy, 1)
                act.activation(c_nat[:, :], ps[:, 5, 256:384], ACT.Copy).then_inc(w_rdy, 1)
                for g in range(NG):
                    act.wait_ge(xT_psum, g + 1)
                    act.activation(xT[:, g * GB:(g + 1) * GB, :],
                                   ps[:, g % 2, :].rearrange("p (b d) -> p b d", b=GB),
                                   ACT.Copy).then_inc(xT_ready, 1)
                    act.wait_ge(val_psum, g + 1)
                    vals = ps[:, 2 + 2 * (g % 2):4 + 2 * (g % 2), :].rearrange("p k (h c) -> p (k h) c", h=2)
                    act.activation(split[:, g * GB:(g + 1) * GB, 0:D], vals[:, :, 0:D],
                                   ACT.Copy).then_inc(part1, 1)
                with act.Fori(0, NG) as g:
                    act.wait_ge(exp_in, g + 1)
                    act.activation(ex, t1, ACT.Exp).then_inc(exp_out, 1)

            @block.tensor
            def _(pe):
                pe.wait_ge(w_in_s, 16 * 8)
                pe.wait_ge(ident_ok, 1)
                pe.transpose(ps[:, 7, 0:D], wv_s, ident[:, :])
                pe.matmul(ps[:, 6, 0:1], wq_s, a_col[:, 0:1], start=True, stop=False)
                pe.matmul(ps[:, 6, 0:1], wk_s, a_col[:, 1:2], start=False, stop=True).then_inc(w_ps, 1)
                pe.wait_ge(a_cols, 1)
                pe.transpose(ps[:, 5, 128:256], wtmp, ident[:, :])
                pe.matmul(ps[:, 5, 256:384], c_col[:, 0:1].broadcast_to([P, P]), ident[:, :],
                          start=True, stop=True).then_inc(w_ps, 1)
                for g in range(NG):
                    pe.wait_ge(xln_ready, g + 1)
                    if g >= 2:
                        pe.wait_ge(xT_ready, g - 1)
                    for b in range(GB):
                        last = pe.transpose(ps[:, g % 2, b * P:(b + 1) * P], xln[:, g * GB + b, :],
                                            ident[:, :])
                    last.then_inc(xT_psum, 1)
                    pe.wait_ge(xT_ready, g + 1)
                    if g == 0:
                        pe.wait_ge(w_rdy, 4)
                    if g >= 2:
                        pe.wait_ge(split_ready, g - 1)
                    for b in range(GB):
                        last = pe.matmul(ps[:, 2 + 2 * (g % 2) + b // 2, (b % 2) * 256:(b % 2) * 256 + D + 1],
                                         xT[:, g * GB + b, :], wst[:, :], start=True, stop=True)
                    last.then_inc(val_psum, 1)
                pe.wait_ge(split_ready, NG)
                for b in range(NB):
                    last = pe.matmul(ps[:, 7, 0:VW], ones_bf[:, :], split[:, b, :],
                                     start=(b == 0), stop=(b == NB - 1))
                last.then_inc(total_psum, 1)
                with pe.Fori(0, NG) as g:
                    pe.wait_ge(sums_free, g + 1)
                    for c in range(NT):
                        pe.wait_ge(conn_ready, g * NT + c + 1 + NS)
                        for j in range(JT):
                            for b in range(GB):
                                last = pe.matmul(ps[:, b, 0:VW], conn[:, c % M0N, j, b * P:(b + 1) * P],
                                                 split[:, c * JT + j, :], start=(c + j == 0),
                                                 stop=(c == NT - 1 and j == JT - 1))
                        last.then_inc(conn_free, 1)

            @block.vector
            def _(dve):
                ch = Chain(dve, dchain)
                for i in range(NS // 2):
                    dve.memset(marks[:, i:i + 1], 0.0).then_inc(stage_free, 1)
                for i in range(NS):
                    dve.memset(marks[:, 4 + i:5 + i], 0.0).then_inc(conn_ready, 1)
                for i in range(M0N):
                    dve.memset(marks[:, 8 + i:9 + i], 0.0).then_inc(conn_free, 1)
                dve.memset(ones_bf[:, :], 1.0)
                dve.memset(ones[:, :], 1.0)
                dve.memset(wz[:, D:D + 1], 1.0 / D)
                ch.link(dve.memset(split[:, :, VW - 1:VW], 1.0))
                dve.wait_ge(w_in_s, 16 * 8)
                ch.add(dve.tensor_tensor(wtmp2, wf_s, lnb_s, ALU.mult))
                ch.link(dve.tensor_tensor(wtmp, wf_s, lnw_s, ALU.mult))
                ch.add(dve.tensor_reduce(a_col[:, 3:4], wtmp2, AX_X, ALU.add))
                ch.link(dve.tensor_reduce(a_col[:, 4:5], wtmp, AX_X, ALU.add))
                ch.add(dve.tensor_scalar(a_col[:, 5:6], a_col[:, 4:5], 1.0 / D, None, ALU.mult))
                ch.link(dve.tensor_tensor(c_col[:, :], a_col[:, 3:4], a_col[:, 2:3], ALU.add))
                dve.tensor_scalar(wtmp, wtmp, a_col[:, 5:6], None, ALU.subtract).then_inc(a_cols, 1)
                dve.wait_ge(x_in, 16)
                for b in range(NB):
                    ch.add(dve.bn_stats(st6[:, b, :], X[:, b, :]))
                ch.done()
                for b in range(NB):
                    ch.add(dve.bn_aggr(mv[:, b, :], st6[:, b, :]))
                ch.done()
                ch.link(dve.tensor_scalar(v_col, mv[:, :, 1], EPS, None, ALU.add))
                emit_rsqrt(dve, ch.link, v_col, y_col, t_col, u_col, 2)
                for b in range(NB):
                    ins = dve.tensor_scalar(xln[:, b, :], X[:, b, :], mv[:, b, 0:1], y_col[:, b:b + 1],
                                            ALU.subtract, ALU.mult)
                    if b % GB == GB - 1:
                        ins.then_inc(xln_ready, 1)
                for g in range(NG):
                    blocks = slice(g * GB, (g + 1) * GB)
                    vals = ps[:, 2 + 2 * (g % 2):4 + 2 * (g % 2), :].rearrange("p k (h c) -> p (k h) c", h=2)
                    dve.wait_ge(part1, g + 1)
                    ch.add(dve.tensor_copy(s_col[:, blocks], vals[:, :, D]))
                    ch.link(dve.tensor_tensor(rest[:, 0, :, :], vals[:, :, 0:D], split[:, blocks, 0:D], ALU.subtract))
                    ch.link(dve.tensor_copy(split[:, blocks, D:2 * D], rest[:, 0, :, :]))
                    ch.link(dve.tensor_tensor(rest[:, 1, :, :], rest[:, 0, :, :], split[:, blocks, D:2 * D],
                                              ALU.subtract))
                    dve.tensor_copy(split[:, blocks, 2 * D:3 * D], rest[:, 1, :, :]).then_inc(split_ready, 1)
                dve.wait_ge(total_psum, 1)
                ch.link(dve.tensor_reduce(total[:, :], ps[:, 7, 0:3 * D].rearrange("p (t d) -> p d t", t=3), AX_X,
                                          ALU.add))
                dve.memset(al_col, 0.0).then_inc(sums_free, 1)
                with dve.Fori(0, NG) as g:
                    for c in range(NT):
                        dve.wait_ge(landed[c % NS], (g * (NT // NS) + c // NS + 1) * 16)
                        dve.wait_ge(conn_free, g * NT + c + 1)
                        dve.tensor_scalar(conn[:, c % M0N, :, :], stage[:, c % NS, :, :], 0.0, None,
                                          ALU.not_equal).then_inc(conn_ready, 1)
                        if c % 2 == 0:
                            dve.tensor_scalar(mask_at(g, c), stage[:, c % NS, :, :], 0.0, None,
                                              ALU.is_gt).then_inc(stage_free, 1)
                    dve.wait_ge(conn_free, g * NT + NT + M0N)
                    lk = Chain(dve, evac, g * EVAC)
                    for b in range(GB):
                        lk.add(dve.tensor_reduce(sums[:, b, :], ps[:, b, 0:3 * D].rearrange("p (t d) -> p d t", t=3),
                                                 AX_X, ALU.add))
                    lk.add(dve.tensor_copy(cnt, ps[:, 0:GB, VW - 1]))
                    lk.done()
                    lk.add(dve.tensor_scalar(sc2, s_col[:, bass.ds(g * GB, GB)], SLOPE0, None, ALU.mult))
                    lk.add(dve.tensor_scalar(ind[:, 0, :], cnt, 0.0, None, ALU.is_gt))
                    lk.link(dve.tensor_scalar(ind[:, 1, :], cnt, float(N), None, ALU.is_ge))
                    dve.memset(sm[:, 11, :, :], 0.0).then_inc(sums_free, 1)
                    lk.add(dve.tensor_tensor(sc, s_col[:, bass.ds(g * GB, GB)], sc2, ALU.max))
                    lk.link(dve.tensor_scalar(t2, ind, -NEG, NEG, ALU.mult, ALU.add))
                    lk.link(dve.tensor_tensor(t1, ind, sc.unsqueeze(1).broadcast_to([P, 2, GB]), ALU.mult))
                    lk.link(dve.tensor_tensor(t1, t1, t2, ALU.add))
                    lk.link(dve.tensor_tensor(mx, t1[:, 0, :], t1[:, 1, :], ALU.max))
                    lk.add(dve.tensor_scalar(ncnt, cnt, -1.0, float(N), ALU.mult, ALU.add))
                    dve.tensor_tensor(t1, t1, mx.unsqueeze(1).broadcast_to([P, 2, GB]),
                                      ALU.subtract).then_inc(exp_in, 1)
                    dve.wait_ge(exp_out, g + 1)
                    lk.add(dve.tensor_tensor(w1c, ex[:, 0, :], cnt, ALU.mult))
                    lk.add(dve.tensor_tensor(al, ex[:, 0, :], ex[:, 1, :], ALU.subtract))
                    lk.link(dve.tensor_tensor(w0c, ex[:, 1, :], ncnt, ALU.mult))
                    lk.link(dve.tensor_tensor(w1c, w1c, w0c, ALU.add))
                    lk.link(dve.reciprocal(w1c, w1c))
                    lk.add(dve.tensor_tensor(al, al, w1c, ALU.mult))
                    lk.link(dve.tensor_tensor(be, ex[:, 1, :], w1c, ALU.mult))
                    for b in range(GB):
                        xb = X[:, bass.ds(g * GB + b, 1), :].rearrange("p o d -> p (o d)")
                        lk.add(dve.scalar_tensor_tensor(xb, sums[:, b, :], al[:, b:b + 1], xb, ALU.mult, ALU.add))
                    lk.done()
                    for b in range(GB):
                        xb = X[:, bass.ds(g * GB + b, 1), :].rearrange("p o d -> p (o d)")
                        lk.add(dve.scalar_tensor_tensor(xb, total[:, :], be[:, b:b + 1], xb, ALU.mult, ALU.add))
                    lk.done()
                    assert lk.n == EVAC, lk.n
        if stop_after <= 1:
            return dump()

        hN = view(work, 0, [NB, D], F32, 4)
        zeros = view(work, 40960, [16, D], F32, 4)
        SLOTS_E = 2 * N + 16 * P
        xs_d = nc.dram_tensor("xs_d", (SLOTS_E, D), F32, kind="Internal").ap()
        ys_d = nc.dram_tensor("ys_d", (SLOTS_E, D), F32, kind="Internal").ap()
        tT, gT = (view(work, (8 + i) * 4 * GR, [2, GR], F32, 4) for i in (0, 2))
        sT, qT = (view(work, (8 + i) * 4 * GR, [4, GR], F32, 4) for i in (4, 8))
        with ExitStack() as c2:
            def sem2(name):
                return c2.enter_context(nc.semaphore(name))

            dchain = sem2("f_dchain")
            h_ready = sem2("h_ready")
            hT_psum = sem2("hT_psum")
            t_ready = sem2("t_ready")
            g_ready = sem2("g_ready")
            s_ready = sem2("s_ready")
            q_ready = sem2("q_ready")
            z_psum = sem2("z_psum")
            var_psum = sem2("var_psum")
            m_ready = sem2("m_ready")
            rchain = sem2("rchain")
            RC = 8

            def z_bank(g):
                return ps[:, 2 * (g % 2):2 * (g % 2) + 2, :].rearrange("p k (h c) -> p (k h) c", h=2)

            zero_ok = sem2("zero_ok")
            zero_out = sem2("zero_out")
            fs = ctx.enter_context(nc.sbuf_tensor("fs", [P, 2, 5, GB], F32))
            block = c2.enter_context(nc.Block())

            @block.sync
            def _(sp):
                sp.wait_ge(zero_ok, 1)
                for i in range(SLOTS_E // (16 * P)):
                    sp.dma_start(xs_d[i * 16 * P:(i + 1) * 16 * P, :].rearrange("(p t) d -> p t d", p=P),
                                 zeros).then_inc(zero_out, 16)
                sp.wait_ge(zero_out, 16 * (SLOTS_E // (16 * P)))

            @block.tensor
            def _(pe):
                def turn(it, g):
                    pe.wait_ge(h_ready, it * NG + g + 1)
                    wait_use(pe, g_ready, it, g, 2)
                    for b in range(GB):
                        last = pe.transpose(ps[:, 4 + g % 2, b * P:(b + 1) * P], hN[:, g * GB + b, :], ident[:, :])
                    last.then_inc(hT_psum, 1)

                def squares(it, g):
                    pe.wait_ge(q_ready, it * NG + g + 1)
                    wait_use(pe, h_ready, it, g, 2, NG)
                    for b in range(GB):
                        last = pe.matmul(ps[:, 6 + g % 2, b:b + 1], qT[:, g % 4, b * P:(b + 1) * P], wz[:, D:D + 1],
                                         start=True, stop=True)
                    last.then_inc(var_psum, 1)

                def product(it, g):
                    pe.wait_ge(s_ready, it * NG + g + 1)
                    wait_use(pe, h_ready, it, g, 2, NG)
                    for b in range(GB):
                        last = pe.matmul(z_bank(g)[:, b, 0:D + 1], sT[:, g % 4, b * P:(b + 1) * P], wz[:, :],
                                         start=True, stop=True)
                    last.then_inc(z_psum, 1)

                def step(it, g, first=False, last=False):
                    if not last:
                        turn(it, g)
                    if not (first and g < 3):
                        squares(*back(it, g, 3))
                    if not (first and g < 2) and not (last and g >= 2):
                        product(*back(it, g, 2))

                run(pe, step)

            @block.scalar
            def _(act):
                def tanh(it, g):
                    act.wait_ge(hT_psum, it * NG + g + 1)
                    act.activation(tT[:, g % 2, :], ps[:, 4 + g % 2, :], ACT.Tanh, bias=c_col[:, :]).then_inc(t_ready, 1)

                def silu(it, g):
                    act.wait_ge(g_ready, it * NG + g + 1)
                    wait_use(act, z_psum, it, g, 4)
                    wait_use(act, q_ready, it, g, 4)
                    act.activation(sT[:, g % 4, :], gT[:, g % 2, :], ACT.Silu, bias=c_col[:, :]).then_inc(s_ready, 1)

                def mean2(it, g):
                    act.wait_ge(z_psum, it * NG + g + 1)
                    act.activation(fs[:, g % 2, 0, :], z_bank(g)[:, :, D], ACT.Square).then_inc(m_ready, 1)

                def step(it, g, first=False, last=False):
                    if not last:
                        tanh(it, g)
                    if not (first and g < 3):
                        mean2(*back(it, g, 3))
                    if not (first and g < 1) and not (last and g >= 1):
                        silu(*back(it, g, 1))

                run(act, step)

            @block.gpsimd
            def _(pool):
                pool.memset(zeros, 0.0).then_inc(zero_ok, 1)

                def square(it, g):
                    pool.wait_ge(s_ready, it * NG + g + 1)
                    wait_use(pool, var_psum, it, g, 4)
                    pool.tensor_tensor(qT[:, g % 4, :], sT[:, g % 4, :], sT[:, g % 4, :], ALU.mult).then_inc(q_ready, 1)

                for g in range(NG):
                    square(0, g)
                with pool.Fori(1, ITERS) as it:
                    for g in range(NG):
                        square(it, g)

            @block.vector
            def _(dve):
                ch = Chain(dve, dchain)
                for b in range(NB):
                    ch.add(dve.bn_stats(st6[:, b, :], X[:, b, :]))
                ch.done()
                for b in range(NB):
                    ch.add(dve.bn_aggr(mv[:, b, :], st6[:, b, :]))
                ch.done()
                ch.link(dve.tensor_scalar(v_col, mv[:, :, 1], EPS, None, ALU.add))
                emit_rsqrt(dve, ch.link, v_col, y_col, t_col, u_col, 2)
                for b in range(NB):
                    ch.add(dve.tensor_scalar(hN[:, b, :], X[:, b, :], mv[:, b, 0:1], y_col[:, b:b + 1],
                                             ALU.subtract, ALU.mult))
                ch.done()
                for g in range(NG):
                    hg = hN[:, g * GB:(g + 1) * GB, :]
                    dve.tensor_tensor(hg, hg, c_nat[:, :].unsqueeze(1).broadcast_to([P, GB, D]),
                                      ALU.subtract).then_inc(h_ready, 1)

                def sum_(it, g):
                    dve.wait_ge(t_ready, it * NG + g + 1)
                    wait_use(dve, s_ready, it, g, 2)
                    dve.scalar_tensor_tensor(gT[:, g % 2, :], tT[:, g % 2, :], 0.01, ps[:, 4 + g % 2, :],
                                             ALU.mult, ALU.add).then_inc(g_ready, 1)

                def scale(it, g):
                    m2, v, y, t, u = (fs[:, g % 2, i, :] for i in range(5))
                    lk = Chain(dve, rchain, it * (NG * RC) + g * RC)
                    dve.wait_ge(m_ready, it * NG + g + 1)
                    dve.wait_ge(var_psum, it * NG + g + 1)
                    lk.link(dve.scalar_tensor_tensor(v, ps[:, 6 + g % 2, 0:GB], EPS, m2, ALU.add, ALU.subtract))
                    emit_rsqrt(dve, lk.link, v, y, t, u, 1)
                    assert lk.n == RC
                    dve.tensor_tensor(hN[:, g * GB:(g + 1) * GB, :], z_bank(g)[:, :, 0:D],
                                      y.unsqueeze(2).broadcast_to([P, GB, D]), ALU.mult).then_inc(h_ready, 1)

                def step(it, g, first=False, last=False):
                    if not (first and g < 3):
                        scale(*back(it, g, 3))
                    if not last:
                        sum_(it, g)

                run(dve, step)
                dve.wait_ge(h_ready, (ITERS + 1) * NG)
                ch.add(dve.tensor_tensor(X[:, :, :], X[:, :, :], hN[:, :, :], ALU.add))
                ch.done()
                ch.link(dve.tensor_tensor(X[:, :, :], X[:, :, :],
                                          c_nat[:, :].unsqueeze(1).broadcast_to([P, NB, D]), ALU.add))
        if stop_after <= 2:
            return dump()

        HW = D + 1
        SB = 2
        SR = SB * P
        NSUB = NB // SB
        JC = 2
        NC = NB // JC
        SLOTS = 4
        rhs = view(work, 0, [2, NB, NPART, HW], BF16, 2)
        t_wide = view(work, 2 * NB * NPART * HW * 2, [NPART * HW], F32, 4)
        scr = conn[:, :, :, :].rearrange("p a b c -> p (a b c)").bitcast(F32)
        hT = scr[:, 0:2 * SR].rearrange("p (k i) -> p k i", k=2)
        f_w, r_w = (scr[:, (2 + i) * SR:(3 + i) * SR].rearrange("p (b d) -> p b d", b=SB) for i in range(2))
        a_bc = scr[:, 0:2 * SR].rearrange("p (k i) -> p k i", k=2)
        x_t = scr[:, 2 * SR:4 * SR].rearrange("p (k b d) -> p k b d", k=2, b=SB)
        tiles3 = X[:, 0:24, :].rearrange("p b d -> p (b d)").bitcast(BF16).rearrange(
            "p (f s j i) -> p f s j i", f=3, s=SLOTS, j=JC)
        m_bf, pairs = tiles3[:, 0], tiles3[:, 1:3]
        x2_d = nc.dram_tensor("x2_d", (N, D), F32, kind="Internal").ap()
        x3_d = nc.dram_tensor("x3_d", (N, D), F32, kind="Internal").ap()
        a_d = nc.dram_tensor("a_d", (NB, P), F32, kind="Internal").ap()
        aw = sb("aw", [P, 2], F32)
        ab = sb("ab", [P, 2, NB], F32)
        FF = sb("FF", [P, 2, NB], F32)
        CC = sb("CC", [P, 2, NB], F32)
        negb = sb("negb", [P, NB], F32)
        bm = sb("bm", [P, 4], F32)
        num = sb("num", [P, SB, HW], F32)
        a_rows = sb("a_rows", [NB, P], F32)
        dn = sb("dn", [P, 4, SB], F32)
        H = X
        with ExitStack() as c3:
            def sem3(name):
                return c3.enter_context(nc.semaphore(name))

            dchain = sem3("g_dchain")
            achain = sem3("g_achain")
            saved = sem3("saved")
            aw_in = sem3("aw_in")
            h_ready = sem3("g_h_ready")
            hT_psum = sem3("g_hT_psum")
            hT_ready = sem3("g_hT_ready")
            ab_psum = sem3("ab_psum")
            b_max = sem3("b_max")
            b_all = sem3("b_all")
            f_in = sem3("f_in")
            f_out = sem3("f_out")
            c_in = sem3("c_in")
            c_out = sem3("c_out")
            f_ready = sem3("f_ready")
            r_ready = sem3("r_ready")
            r2_ready = sem3("r2_ready")
            p1_ready = sem3("p1_ready")
            p2_ready = sem3("p2_ready")
            p3_ready = sem3("p3_ready")
            ones_col = sem3("ones_col")
            a_psum = sem3("a_psum")
            a_row = sem3("a_row")
            a_saved = sem3("a_saved")
            th_psum = sem3("th_psum")
            block = c3.enter_context(nc.Block())

            @block.sync
            def _(sp):
                sp.dma_start(x2_d.rearrange("(b p) d -> p b d", p=P), X[:, :, :]).then_inc(saved, 16)
                sp.dma_start(aw[:, :], a1).then_inc(aw_in, 16)
                sp.wait_ge(a_row, 1)
                sp.dma_start(a_d, a_rows[:, :]).then_inc(a_saved, 16)
                sp.wait_ge(a_saved, 16)

            @block.gpsimd
            def _(pool):
                pool.wait_ge(b_max, 1)
                pool.partition_all_reduce(bm[:, 1:2], bm[:, 0:1], P, bass.bass_isa.ReduceOp.max).then_inc(b_all, 1)

            @block.tensor
            def _(pe):
                pe.wait_ge(aw_in, 16)
                for u in range(NSUB):
                    pe.wait_ge(h_ready, u + 1)
                    if u >= 2:
                        pe.wait_ge(hT_ready, u - 1)
                    for b in range(SB):
                        last = pe.transpose(ps[:, u % 2, b * P:(b + 1) * P], H[:, u * SB + b, :], ident[:, :])
                    last.then_inc(hT_psum, 1)
                    for b in range(SB):
                        last = pe.matmul(ps[:, 3, 0:D], ones[:, :], H[:, u * SB + b, :], start=(u + b == 0),
                                         stop=(u == NSUB - 1 and b == SB - 1))
                    if u == NSUB - 1:
                        last.then_inc(th_psum, 1)
                    pe.wait_ge(hT_ready, u + 1)
                    for b in range(SB):
                        k = u * SB + b
                        last = pe.matmul(ps[:, 2, 2 * k:2 * k + 2], hT[:, u % 2, b * P:(b + 1) * P], aw[:, :],
                                         start=True, stop=True)
                    last.then_inc(ab_psum, 1)
                pe.wait_ge(f_in, 1)
                pe.transpose(ps[0:NB, 4, 0:P], ab[:, 0, :], ident[:, :]).then_inc(a_psum, 1)

            @block.scalar
            def _(act):
                for u in range(NSUB):
                    act.wait_ge(hT_psum, u + 1)
                    if u >= 2:
                        act.wait_ge(ab_psum, u - 1)
                    act.activation(hT[:, u % 2, :], ps[:, u % 2, 0:SR], ACT.Copy).then_inc(hT_ready, 1)
                act.wait_ge(a_psum, 1)
                act.activation(a_rows[:, :], ps[0:NB, 4, 0:P], ACT.Copy).then_inc(a_row, 1)
                act.wait_ge(f_in, 2)
                act.activation(FF[:, :, :], FF[:, :, :], ACT.Exp).then_inc(f_out, 1)
                act.wait_ge(c_in, 1)
                act.activation(CC[:, :, :], CC[:, :, :], ACT.Exp).then_inc(c_out, 1)
                for k in range(2 * NSUB):
                    u, f = k // 2, k % 2
                    blocks = slice(u * SB, (u + 1) * SB)
                    act.wait_ge(f_ready, k + 1)
                    act.activation(rhs[:, f, blocks, 0, 0:D], f_w, ACT.Copy).then_inc(p1_ready, 1)
                    act.wait_ge(r_ready, k + 1)
                    act.activation(rhs[:, f, blocks, 1, 0:D], r_w, ACT.Copy).then_inc(p2_ready, 1)
                    act.wait_ge(r2_ready, k + 1)
                    act.activation(rhs[:, f, blocks, 2, 0:D], r_w, ACT.Copy).then_inc(p3_ready, 1)

            @block.vector
            def _(dve):
                ch = Chain(dve, dchain)
                for b in range(NB):
                    ch.add(dve.bn_stats(st6[:, b, :], X[:, b, :]))
                ch.done()
                for b in range(NB):
                    ch.add(dve.bn_aggr(mv[:, b, :], st6[:, b, :]))
                ch.done()
                ch.link(dve.tensor_scalar(v_col, mv[:, :, 1], EPS, None, ALU.add))
                emit_rsqrt(dve, ch.link, v_col, y_col, t_col, u_col, 2)
                dve.wait_ge(saved, 16)
                for b in range(NB):
                    ins = dve.tensor_scalar(H[:, b, :], X[:, b, :], mv[:, b, 0:1], y_col[:, b:b + 1],
                                            ALU.subtract, ALU.mult)
                    if b % SB == SB - 1:
                        ins.then_inc(h_ready, 1)
                dve.wait_ge(ab_psum, NSUB)
                ch.link(dve.tensor_copy(ab[:, :, :], ps[:, 2, 0:2 * NB].rearrange("p (b k) -> p k b", k=2)))
                dve.tensor_reduce(bm[:, 0:1], ab[:, 1, :], AX_X, ALU.max).then_inc(b_max, 1)
                dve.tensor_scalar(negb[:, :], ab[:, 1, :], -1.0, None, ALU.mult).then_inc(f_in, 1)
                dve.wait_ge(b_all, 1)
                ch.link(dve.tensor_scalar(FF[:, 0, :], ab[:, 1, :], bm[:, 1:2], None, ALU.subtract))
                dve.tensor_scalar(FF[:, 1, :], FF[:, 0, :], SLOPE1, None, ALU.mult).then_inc(f_in, 1)
                ch.link(dve.tensor_scalar(CC[:, 0, :], ab[:, 0, :], bm[:, 1:2], None, ALU.add))
                ch.link(dve.tensor_scalar(CC[:, 1, :], CC[:, 0, :], SLOPE1, None, ALU.mult))
                ch.link(dve.tensor_tensor(t_col, CC[:, 0, :], CC[:, 1, :], ALU.max))
                dve.tensor_tensor(CC[:, :, :], CC[:, :, :], t_col.unsqueeze(1).broadcast_to([P, 2, NB]),
                                  ALU.subtract).then_inc(c_in, 1)
                dve.wait_ge(f_out, 1)
                ch.link(dve.tensor_copy(rhs[:, :, :, 0, D], FF[:, :, :]))
                rr = col[:, 0:2, :]
                ch.link(dve.tensor_tensor(rr, FF[:, :, :], rhs[:, :, :, 0, D], ALU.subtract))
                ch.link(dve.tensor_copy(rhs[:, :, :, 1, D], rr))
                ch.link(dve.tensor_tensor(rr, rr, rhs[:, :, :, 1, D], ALU.subtract))
                ch.link(dve.tensor_copy(rhs[:, :, :, 2, D], rr))
                dve.wait_ge(th_psum, 1)
                ch.link(dve.tensor_scalar(total[:, :], ps[:, 3, 0:D], 1.0 / N, None, ALU.mult))
                for k in range(2 * NSUB):
                    u, f = k // 2, k % 2
                    blocks = slice(u * SB, (u + 1) * SB)
                    if k >= 1:
                        dve.wait_ge(p3_ready, k)
                    dve.tensor_tensor(f_w, H[:, blocks, :], FF[:, f, blocks].unsqueeze(2).broadcast_to([P, SB, D]),
                                      ALU.mult).then_inc(f_ready, 1)
                    dve.wait_ge(p1_ready, k + 1)
                    dve.tensor_tensor(r_w, f_w, rhs[:, f, blocks, 0, 0:D], ALU.subtract).then_inc(r_ready, 1)
                    dve.wait_ge(p2_ready, k + 1)
                    dve.tensor_tensor(r_w, r_w, rhs[:, f, blocks, 1, 0:D], ALU.subtract).then_inc(r2_ready, 1)
                dve.wait_ge(p3_ready, 2 * NSUB)

        with ExitStack() as c4:
            def sem4(name):
                return c4.enter_context(nc.semaphore(name))

            mchain = sem4("mchain")
            up_ready = sem4("up_ready")
            m_ready = sem4("m_ready")
            low_dve = sem4("low_dve")
            low_pool = sem4("low_pool")
            used = sem4("used")
            banks_free = sem4("banks_free")
            low_sum = sem4("low_sum")
            wide_free = sem4("wide_free")
            a_in = [sem4(f"a_in{i}") for i in range(2)]
            x_in3 = [sem4(f"x_in3{i}") for i in range(2)]
            x_out = [sem4(f"x_out{i}") for i in range(2)]
            x_done = sem4("x_done")
            block = c4.enter_context(nc.Block())
            a_flat = a_d.rearrange("b p -> (b p)")
            EV = 9

            @block.sync
            def _(sp):
                for s in range(NSUB):
                    if s >= 2:
                        sp.wait_ge(up_ready, (s - 1) * NC)
                    sp.dma_start(a_bc[:, s % 2, :], a_flat[s * SR:(s + 1) * SR].partition_broadcast(P)).then_inc(
                        a_in[s % 2], 16)
                    if s >= 2:
                        sp.wait_ge(x_done, s - 1)
                        sp.dma_start(x3_d[(s - 2) * SR:(s - 1) * SR, :].rearrange("(b p) d -> p b d", p=P),
                                     x_t[:, s % 2, :, :]).then_inc(x_out[s % 2], 16)
                        sp.wait_ge(x_out[s % 2], (s // 2) * 16)
                    sp.dma_start(x_t[:, s % 2, :, :], x2_d[s * SR:(s + 1) * SR, :].rearrange(
                        "(b p) d -> p b d", p=P)).then_inc(x_in3[s % 2], 16)
                for s in (NSUB - 2, NSUB - 1):
                    sp.wait_ge(x_done, s + 1)
                    sp.dma_start(x3_d[s * SR:(s + 1) * SR, :].rearrange("(b p) d -> p b d", p=P),
                                 x_t[:, s % 2, :, :]).then_inc(x_out[s % 2], 16)
                for i in range(2):
                    sp.wait_ge(x_out[i], NSUB // 2 * 16)

            @block.gpsimd
            def _(pool):
                for k in range(3, NSUB * NC, 4):
                    pool.wait_ge(up_ready, k + 1)
                    pool.tensor_tensor(pairs[:, 1, k % SLOTS, :, :], m_bf[:, k % SLOTS, :, :],
                                       pairs[:, 0, k % SLOTS, :, :], ALU.subtract).then_inc(low_pool, 1)

            @block.tensor
            def _(pe):
                def chunk(g, h, c):
                    s = 2 * g + h
                    if c == 0:
                        pe.wait_ge(banks_free, s + 1)
                    pe.wait_ge(up_ready, s * NC + c + 1)
                    for f in range(2):
                        if f == 1:
                            if c % 4 == 3:
                                pe.wait_ge(low_pool, s * (NC // 4) + c // 4 + 1)
                            else:
                                pe.wait_ge(low_dve, s * (NC // 4 * 3) + c // 4 * 3 + c % 4 + 1)
                        for j in range(JC):
                            for b in range(SB):
                                last = pe.matmul(ps[:, 4 * h + 2 * f + b, 0:NPART * HW],
                                                 pairs[:, f, c % SLOTS, j, b * P:(b + 1) * P],
                                                 rhs[:, f, c * JC + j, :, :].rearrange("p t d -> p (t d)"),
                                                 start=(c + j == 0), stop=(c == NC - 1 and j == JC - 1))
                    last.then_inc(used, 1)

                with pe.Fori(0, NSUB // 2) as g:
                    for h in range(2):
                        for c in range(NC):
                            chunk(g, h, c)

            @block.scalar
            def _(act):
                def scale_low(g, h, b):
                    s = 2 * g + h
                    if b == 0:
                        act.wait_ge(used, (s + 1) * NC + SLOTS)
                    act.wait_ge(wide_free, s * SB + b + 1)
                    act.activation(t_wide, ps[:, 4 * h + 2 + b, 0:NPART * HW], ACT.Copy,
                                   scale=CC[:, 1, bass.ds(s * SB + b, 1)]).then_inc(low_sum, 1)

                def mask_chunk(g, h, c):
                    act.wait_ge(used, (2 * g + h) * NC + c + 1)
                    m = mask_v[:, bass.ds(g, 1), c * JC:(c + 1) * JC, h * SR:(h + 1) * SR].rearrange(
                        "p o j i -> p (o j) i")
                    act.activation(m_bf[:, c % SLOTS, :, :], m, ACT.Copy).then_inc(m_ready, 1)

                def body(g, first=False):
                    for h in range(2):
                        for c in range(NC):
                            mask_chunk(g, h, c)
                            if c == SLOTS and not (first and h == 0):
                                for b in range(SB):
                                    scale_low(*((g, 0) if h == 1 else (g - 1, 1)), b)

                body(0, first=True)
                with act.Fori(1, NSUB // 2) as g:
                    body(g)
                for b in range(SB):
                    scale_low(NSUB // 2 - 1, 1, b)

            @block.vector
            def _(dve):
                for i in range(SLOTS):
                    dve.memset(marks[:, i:i + 1], 0.0).then_inc(used, 1)
                for i in range(2):
                    dve.memset(marks[:, 4 + i:5 + i], 0.0).then_inc(banks_free, 1)
                dve.memset(marks[:, 8:9], 0.0).then_inc(wide_free, 1)

                def chunk(g, h, c):
                    s = 2 * g + h
                    if c == 0:
                        dve.wait_ge(a_in[h], (g + 1) * 16)
                    dve.wait_ge(m_ready, s * NC + c + 1)
                    for j in range(JC):
                        last = dve.scalar_tensor_tensor(pairs[:, 0, c % SLOTS, j, :], a_bc[:, h, :],
                                                        negb[:, c * JC + j:c * JC + j + 1], m_bf[:, c % SLOTS, j, :],
                                                        ALU.is_ge, ALU.mult)
                    last.then_inc(up_ready, 1)

                def chunk_low(g, h, c):
                    if c % 4 != 3:
                        dve.wait_ge(up_ready, (2 * g + h) * NC + c + 1)
                        dve.tensor_tensor(pairs[:, 1, c % SLOTS, :, :], m_bf[:, c % SLOTS, :, :],
                                          pairs[:, 0, c % SLOTS, :, :], ALU.subtract).then_inc(low_dve, 1)

                def finish(g, h):
                    s = 2 * g + h
                    lk = Chain(dve, mchain, s * EV)
                    dve.wait_ge(x_in3[h], (g + 1) * 16)
                    for b in range(SB):
                        dve.wait_ge(low_sum, s * SB + b + 1)
                        lk.link(dve.scalar_tensor_tensor(t_wide, ps[:, 4 * h + b, 0:NPART * HW],
                                                         CC[:, 0, bass.ds(s * SB + b, 1)], t_wide,
                                                         ALU.mult, ALU.add))
                        lk.link(dve.tensor_reduce(num[:, b, :], t_wide.rearrange("p (t d) -> p d t", t=NPART),
                                                  AX_X, ALU.add))
                        dve.memset(marks[:, 9 + b:10 + b], 0.0).then_inc(wide_free, 1)
                    dve.memset(marks[:, 11:12], 0.0).then_inc(banks_free, 1)
                    none, den, rden = dn[:, 0, :], dn[:, 1, :], dn[:, 2, :]
                    lk.link(dve.tensor_scalar(none, num[:, :, D], 0.0, None, ALU.is_equal))
                    lk.link(dve.tensor_tensor(den, num[:, :, D], none, ALU.add))
                    lk.link(dve.reciprocal(rden, den))
                    for b in range(SB):
                        lk.add(dve.scalar_tensor_tensor(num[:, b, 0:D], total[:, :], none[:, b:b + 1], num[:, b, 0:D],
                                                        ALU.mult, ALU.add))
                    lk.done()
                    for b in range(SB):
                        ins = dve.scalar_tensor_tensor(x_t[:, h, b, :], num[:, b, 0:D], rden[:, b:b + 1],
                                                       x_t[:, h, b, :], ALU.mult, ALU.add)
                    ins.then_inc(x_done, 1)
                    assert lk.n == EV, lk.n

                def body(g, first=False):
                    for h in range(2):
                        for c in range(NC):
                            chunk(g, h, c)
                            chunk_low(g, h, c)
                            if c == SLOTS and not (first and h == 0):
                                finish(*((g, 0) if h == 1 else (g - 1, 1)))

                body(0, first=True)
                with dve.Fori(1, NSUB // 2) as g:
                    body(g)
                finish(NSUB // 2 - 1, 1)

        with ExitStack() as c5, nc.semaphore("x_back") as x_back, nc.Block() as block:
            @block.sync
            def _(sp):
                sp.dma_start(X[:, :, :], x3_d.rearrange("(b p) d -> p b d", p=P)).then_inc(x_back, 16)
                sp.wait_ge(x_back, 16)
        if stop_after <= 3:
            return dump()

        NE = 16
        HID = 256
        K = 2
        KB = K * NB
        TILES = K * N // P + NE
        ROUNDS = TILES // NG
        at = [0]

        def m(shape, dt, size):
            n = size
            for x_ in shape:
                n *= x_
            v_ = view(mask, at[0], shape, dt, size)
            at[0] += (n + 63) // 64 * 64
            assert at[0] <= mask_bytes
            return v_

        w12 = m([NE, 2 * HID], F32, 4)
        w3_s = m([NE, 2, D], F32, 4)
        back_rows = m([K, NB, D], F32, 4)
        Y = view(work, 0, [NB, D], F32, 4)
        yT = m([2, GR], F32, 4)
        gw = m([NE], F32, 4)
        gb = m([NE], F32, 4)
        logit = m([NB, NE], F32, 4)
        top = m([NB, 8], F32, 4)
        top_i = m([NB, 8], U32, 4)
        idx = m([K, NB], F32, 4)
        pw = m([K, NB], F32, 4)
        iota_e = m([NE], F32, 4)
        iota_t = m([TILES], F32, 4)
        before = m([P], BF16, 2)
        hot = m([K, NB, NE], BF16, 2)
        tot = m([NE, KB], F32, 4)
        cum = m([NE, KB], F32, 4)
        one_row = m([NE * KB], F32, 4)
        n_e = m([NE], F32, 4)
        n_i = m([NE], I32, 4)
        t_e = m([NE], F32, 4)
        t_s = m([NE], F32, 4)
        off_e = m([NE], F32, 4)
        place = m([K, NB, NE], F32, 4)
        slot_f = m([K, NB], F32, 4)
        slot = m([KB], U32, 4)
        cmp_t = m([TILES, NE], F32, 4)
        eid_f = m([TILES], F32, 4)
        eid = m([TILES], I32, 4)
        xs = view(work, 16384, [2, 4, D], F32, 4)
        xT_s = m([2, P], F32, 4)
        sil = m([2, HID], F32, 4)
        hid = m([2, HID], F32, 4)
        hidT = m([2, 2, P], F32, 4)
        o_s = view(work, 16384 + 4096, [2, 4, D], F32, 4)
        with ExitStack() as c6:
            def sem6(name):
                return c6.enter_context(nc.semaphore(name))

            dchain = sem6("e_dchain")
            gate_in = sem6("gate_in")
            pchain = sem6("pchain")
            before_ok = sem6("before_ok")
            iota_ok = sem6("iota_ok")
            y_ready = sem6("y_ready")
            yT_psum = sem6("yT_psum")
            yT_ready = sem6("yT_ready")
            logit_psum = sem6("logit_psum")
            gap_ready = sem6("gap_ready")
            ratio = sem6("ratio")
            hot_ready = sem6("hot_ready")
            rank_psum = sem6("rank_psum")
            slot_ready = sem6("slot_ready")
            scattered = sem6("scattered")
            w_in6 = sem6("w_in6")
            block = c6.enter_context(nc.Block())

            @block.sync
            def _(sp):
                sp.dma_start(gw, gate_w).then_inc(gate_in, 16)
                sp.dma_start(gb, gate_b.partition_broadcast(P)).then_inc(gate_in, 16)
                sp.dma_start(w12[:, :, 0:HID], w1.rearrange("e d h -> d e h")).then_inc(w_in6, 16)
                sp.dma_start(w12[:, :, HID:2 * HID], w2.rearrange("e d h -> d e h")).then_inc(w_in6, 16)
                sp.dma_start(w3_s, w3.rearrange("e (c p) o -> p e c o", p=P)).then_inc(w_in6, 16)
                sp.wait_ge(w_in6, 48)

            @block.gpsimd
            def _(pool):
                pool.iota(iota_e, pattern=[[1, NE]], base=0, channel_multiplier=0,
                          allow_small_or_imprecise_dtypes=True).then_inc(iota_ok, 1)
                pool.iota(iota_t, pattern=[[1, TILES]], base=0, channel_multiplier=0,
                          allow_small_or_imprecise_dtypes=True).then_inc(iota_ok, 1)
                pool.memset(before, 1.0).then_inc(pchain, 1)
                pool.wait_ge(pchain, 1)
                pool.affine_select(out=before, in_=before, compare_op=ALU.is_gt, fill=0.0, base=0,
                                   pattern=[[1, P]], channel_multiplier=-1).then_inc(before_ok, 1)
                pool.wait_ge(slot_ready, 1)
                for k in range(K):
                    for b in range(NB):
                        pool.indirect_dma_start(
                            out=xs_d, out_offset=bass.IndirectOffsetOnAxis(
                                ap=slot[:, k * NB + b:k * NB + b + 1], axis=0),
                            in_=Y[:, b, :], in_offset=None).then_inc(scattered, 16)
                pool.wait_ge(scattered, KB * 16)

            @block.tensor
            def _(pe):
                pe.wait_ge(gate_in, 32)
                for g in range(NG):
                    pe.wait_ge(y_ready, g + 1)
                    if g >= 2:
                        pe.wait_ge(yT_ready, g - 1)
                    for b in range(GB):
                        last = pe.transpose(ps[:, g % 2, b * P:(b + 1) * P], Y[:, g * GB + b, :], ident[:, :])
                    last.then_inc(yT_psum, 1)
                    pe.wait_ge(yT_ready, g + 1)
                    for b in range(GB):
                        k = g * GB + b
                        last = pe.matmul(ps[:, 2, k * NE:(k + 1) * NE], yT[:, g % 2, b * P:(b + 1) * P], gw,
                                         start=True, stop=True)
                    last.then_inc(logit_psum, 1)
                pe.wait_ge(before_ok, 1)
                for k in range(K):
                    pe.wait_ge(hot_ready, k + 1)
                    h_k = hot[:, k, :, :].rearrange("p b e -> p (b e)")
                    pe.matmul(ps[:, 4 + k, :], before, h_k, start=True, stop=True)
                    pe.matmul(ps[:, 6 + k, :], ones_bf[:, :], h_k, start=True, stop=True).then_inc(rank_psum, 1)

            @block.scalar
            def _(act):
                for g in range(NG):
                    act.wait_ge(yT_psum, g + 1)
                    if g >= 2:
                        act.wait_ge(logit_psum, g - 1)
                    act.activation(yT[:, g % 2, :], ps[:, g % 2, :], ACT.Copy).then_inc(yT_ready, 1)
                act.wait_ge(gap_ready, 1)
                act.activation(pw[:, 1, :], pw[:, 1, :], ACT.Exp).then_inc(ratio, 1)

            @block.vector
            def _(dve):
                ch = Chain(dve, dchain)
                ch.add(dve.memset(one_row, 1.0))
                for b in range(NB):
                    ch.add(dve.bn_stats(st6[:, b, :], X[:, b, :]))
                ch.done()
                for b in range(NB):
                    ch.add(dve.bn_aggr(mv[:, b, :], st6[:, b, :]))
                ch.done()
                ch.link(dve.tensor_scalar(v_col, mv[:, :, 1], EPS, None, ALU.add))
                emit_rsqrt(dve, ch.link, v_col, y_col, t_col, u_col, 2)
                for b in range(NB):
                    ins = dve.tensor_scalar(Y[:, b, :], X[:, b, :], mv[:, b, 0:1], y_col[:, b:b + 1],
                                            ALU.subtract, ALU.mult)
                    if b % GB == GB - 1:
                        ins.then_inc(y_ready, 1)
                dve.wait_ge(logit_psum, NG)
                ch.link(dve.tensor_tensor(logit, ps[:, 2, :].rearrange("p (b e) -> p b e", e=NE),
                                          gb.unsqueeze(1).broadcast_to([P, NB, NE]), ALU.add))
                for b in range(NB):
                    ch.add(dve.max(top[:, b, :], logit[:, b, :]))
                ch.done()
                for b in range(NB):
                    ch.add(dve.max_index(top_i[:, b, :], top[:, b, :], logit[:, b, :]))
                dve.tensor_tensor(pw[:, 1, :], top[:, :, 1], top[:, :, 0], ALU.subtract).then_inc(gap_ready, 1)
                ch.done()
                ch.link(dve.tensor_copy(idx, top_i[:, :, 0:K].rearrange("p b k -> p k b")))
                dve.wait_ge(iota_ok, 2)
                for k in range(K):
                    dve.tensor_tensor(hot[:, k, :, :], idx[:, k, :].unsqueeze(2).broadcast_to([P, NB, NE]),
                                      iota_e.unsqueeze(1).broadcast_to([P, NB, NE]), ALU.is_equal).then_inc(hot_ready, 1)
                dve.wait_ge(ratio, 1)
                ch.link(dve.tensor_scalar(v_col, pw[:, 1, :], 1.0, None, ALU.add))
                ch.link(dve.reciprocal(pw[:, 0, :], v_col))
                ch.link(dve.tensor_tensor(pw[:, 1, :], pw[:, 1, :], pw[:, 0, :], ALU.mult))
                dve.wait_ge(rank_psum, K)
                for k in range(K):
                    ch.add(dve.tensor_copy(tot[:, :, k * NB:(k + 1) * NB],
                                           ps[:, 6 + k, :].rearrange("p (b e) -> p e b", e=NE)))
                ch.done()
                ch.link(dve.tensor_reduce(n_e, tot, AX_X, ALU.add))
                ch.link(dve.tensor_scalar(n_i, n_e, float(P - 1), None, ALU.add))
                ch.link(dve.tensor_scalar(n_i, n_i, 7, None, ALU.logical_shift_right))
                ch.link(dve.tensor_copy(t_e, n_i))
                ch.link(dve.tensor_tensor_scan(t_s, one_row[:, 0:NE], t_e, 0.0, ALU.mult, ALU.add))
                ch.link(dve.tensor_tensor(t_s, t_s, t_e, ALU.subtract))
                flat = lambda v_: v_.rearrange("p e k -> p (e k)")
                ch.link(dve.tensor_tensor_scan(flat(cum), one_row, flat(tot), 0.0, ALU.mult, ALU.add))
                ch.link(dve.tensor_tensor(cum, cum, tot, ALU.subtract))
                ch.link(dve.scalar_tensor_tensor(off_e, t_s, float(P), cum[:, :, 0], ALU.mult, ALU.subtract))
                ch.link(dve.tensor_tensor(cum, cum, off_e.unsqueeze(2).broadcast_to([P, NE, KB]), ALU.add))
                for k in range(K):
                    ch.add(dve.tensor_tensor(place[:, k, :, :], ps[:, 4 + k, :].rearrange("p (b e) -> p b e", e=NE),
                                             cum[:, :, k * NB:(k + 1) * NB].rearrange("p e b -> p b e"), ALU.add))
                ch.done()
                ch.link(dve.tensor_tensor(place, place, hot, ALU.mult))
                ch.link(dve.tensor_reduce(slot_f, place, AX_X, ALU.add))
                dve.tensor_copy(slot, slot_f.rearrange("p k b -> p (k b)")).then_inc(slot_ready, 1)
                ch.link(dve.tensor_tensor(cmp_t, t_s.unsqueeze(1).broadcast_to([P, TILES, NE]),
                                          iota_t.unsqueeze(2).broadcast_to([P, TILES, NE]), ALU.is_le))
                ch.link(dve.tensor_reduce(eid_f, cmp_t, AX_X, ALU.add))
                ch.link(dve.tensor_scalar(eid, eid_f, -1.0, None, ALU.add))

        with ExitStack() as c7:
            def sem7(name):
                return c7.enter_context(nc.semaphore(name))

            xs_in = [sem7(f"xs_in{i}") for i in range(2)]
            ys_out = [sem7(f"ys_out{i}") for i in range(2)]
            xsT_psum = sem7("xsT_psum")
            xsT_ready = sem7("xsT_ready")
            up_psum = sem7("up_psum")
            sil_ready = sem7("sil_ready")
            hid_ready = sem7("hid_ready")
            hidT_psum = sem7("hidT_psum")
            hidT_ready = sem7("hidT_ready")
            o_psum = sem7("o_psum")
            o_ready = sem7("o_ready")
            block = c7.enter_context(nc.Block())

            @block.sync
            def _(sp):
                def load(c):
                    if c >= 2:
                        sp.wait_ge(xsT_psum, 4 * (c - 1))
                    sp.dma_start(xs[:, c % 2, :, :], xs_d[c * 4 * P:(c + 1) * 4 * P, :].rearrange(
                        "(t p) d -> p t d", p=P)).then_inc(xs_in[c % 2], 16)

                load(0)
                for c in range(TILES // 4):
                    if c + 1 < TILES // 4:
                        load(c + 1)
                    sp.wait_ge(o_ready, 4 * (c + 1))
                    sp.dma_start(ys_d[c * 4 * P:(c + 1) * 4 * P, :].rearrange("(t p) d -> p t d", p=P),
                                 o_s[:, c % 2, :, :]).then_inc(ys_out[c % 2], 16)
                for i in range(2):
                    sp.wait_ge(ys_out[i], TILES // 8 * 16)

            @block.tensor
            def _(pe):
                def expert(it, t):
                    tile = it * NG + t
                    src = eid[0:1, tile:tile + 1] if isinstance(tile, int) else eid[0:1, bass.ds(tile, 1)]
                    return pe.value_load(src, min_val=0, max_val=NE - 1)

                def turn(it, t):
                    pe.wait_ge(xs_in[t // 4], it * 16 + 16)
                    wait_use(pe, xsT_ready, it, t, 2)
                    pe.transpose(ps[:, t % 2, 0:P], xs[:, t // 4, t % 4, :], ident[:, :]).then_inc(xsT_psum, 1)

                def up(it, t):
                    e = expert(it, t)
                    pe.wait_ge(xsT_ready, it * NG + t + 1)
                    wait_use(pe, hid_ready, it, t, 2)
                    pe.matmul(ps[:, 2 + t % 2, :], xT_s[:, t % 2, :],
                              w12[:, bass.ds(e, 1), :].rearrange("p o n -> p (o n)"),
                              start=True, stop=True).then_inc(up_psum, 1)

                def turn_hidden(it, t):
                    pe.wait_ge(hid_ready, it * NG + t + 1)
                    wait_use(pe, hidT_ready, it, t, 2)
                    for c in range(2):
                        last = pe.transpose(ps[:, 4 + t % 2, c * P:(c + 1) * P], hid[:, t % 2, c * P:(c + 1) * P],
                                            ident[:, :])
                    last.then_inc(hidT_psum, 1)

                def down(it, t):
                    e = expert(it, t)
                    pe.wait_ge(hidT_ready, it * NG + t + 1)
                    wait_use(pe, o_ready, it, t, 2)
                    for c in range(2):
                        last = pe.matmul(ps[:, 6 + t % 2, 0:D], hidT[:, t % 2, c, :],
                                         w3_s[:, bass.ds(e, 1), c, :].rearrange("p o n -> p (o n)"),
                                         start=(c == 0), stop=(c == 1))
                    last.then_inc(o_psum, 1)

                def step(it, t, first=False, last=False):
                    if not last:
                        turn(it, t)
                    if not (first and t < 1) and not (last and t >= 1):
                        up(*back(it, t, 1))
                    if not (first and t < 2) and not (last and t >= 2):
                        turn_hidden(*back(it, t, 2))
                    if not (first and t < 3):
                        down(*back(it, t, 3))

                run(pe, step, ROUNDS)

            @block.scalar
            def _(act):
                def take_x(it, t):
                    act.wait_ge(xsT_psum, it * NG + t + 1)
                    wait_use(act, up_psum, it, t, 2)
                    act.activation(xT_s[:, t % 2, :], ps[:, t % 2, 0:P], ACT.Copy).then_inc(xsT_ready, 1)

                def silu(it, t):
                    act.wait_ge(up_psum, it * NG + t + 1)
                    wait_use(act, hid_ready, it, t, 2)
                    act.activation(sil[:, t % 2, :], ps[:, 2 + t % 2, 0:HID], ACT.Silu).then_inc(sil_ready, 1)

                def take_out(it, t):
                    act.wait_ge(o_psum, it * NG + t + 1)
                    if t % 4 == 0 and not (isinstance(it, int) and it == 0):
                        act.wait_ge(ys_out[t // 4], it * 16)
                    act.activation(o_s[:, t // 4, t % 4, :], ps[:, 6 + t % 2, 0:D], ACT.Copy).then_inc(o_ready, 1)

                def step(it, t, first=False, last=False):
                    if not last:
                        take_x(it, t)
                    if not (first and t < 1) and not (last and t >= 1):
                        silu(*back(it, t, 1))
                    if not (first and t < 3):
                        take_out(*back(it, t, 3))

                run(act, step, ROUNDS)

            @block.vector
            def _(dve):
                def gate(it, t):
                    dve.wait_ge(sil_ready, it * NG + t + 1)
                    wait_use(dve, hidT_psum, it, t, 2)
                    dve.tensor_tensor(hid[:, t % 2, :], sil[:, t % 2, :], ps[:, 2 + t % 2, HID:2 * HID],
                                      ALU.mult).then_inc(hid_ready, 1)

                def take_hidden(it, t):
                    dve.wait_ge(hidT_psum, it * NG + t + 1)
                    wait_use(dve, o_psum, it, t, 2)
                    dve.tensor_copy(hidT[:, t % 2, :, :], ps[:, 4 + t % 2, 0:HID].rearrange(
                        "p (c i) -> p c i", c=2)).then_inc(hidT_ready, 1)

                def step(it, t, first=False, last=False):
                    if not (first and t < 1) and not (last and t >= 1):
                        gate(*back(it, t, 1))
                    if not (first and t < 2) and not (last and t >= 2):
                        take_hidden(*back(it, t, 2))

                run(dve, step, ROUNDS)

        with ExitStack() as c8:
            def sem8(name):
                return c8.enter_context(nc.semaphore(name))

            gathered = [sem8(f"gathered{i}") for i in range(NG)]
            summed = sem8("summed")
            first_sum = sem8("first_sum")
            out_done = sem8("out_done")
            block = c8.enter_context(nc.Block())

            @block.gpsimd
            def _(pool):
                for b in range(NB):
                    for k in range(K):
                        pool.indirect_dma_start(
                            out=back_rows[:, k, b, :], out_offset=None, in_=ys_d,
                            in_offset=bass.IndirectOffsetOnAxis(ap=slot[:, k * NB + b:k * NB + b + 1],
                                                                axis=0)).then_inc(gathered[b // GB], 16)

            @block.vector
            def _(dve):
                for g in range(NG):
                    dve.wait_ge(gathered[g], 16 * GB * K)
                    for k in range(K):
                        if k == 1:
                            dve.wait_ge(first_sum, g + 1)
                        for b in range(g * GB, (g + 1) * GB):
                            last = dve.scalar_tensor_tensor(X[:, b, :], back_rows[:, k, b, :], pw[:, k, b:b + 1],
                                                            X[:, b, :], ALU.mult, ALU.add)
                        last.then_inc(first_sum if k == 0 else summed, 1)

            @block.sync
            def _(sp):
                for g in range(NG):
                    sp.wait_ge(summed, g + 1)
                    sp.dma_start(out[g * GR:(g + 1) * GR, :].rearrange("(b p) d -> p b d", p=P),
                                 X[:, g * GB:(g + 1) * GB, :]).then_inc(out_done, 16)
                sp.wait_ge(out_done, 16 * NG)

_INS = ["x", "adj", "L0_gnn_Wq", "L0_gnn_Wk", "L0_gnn_Wv", "L0_gnn_a", "L0_ffn_ln_w", "L0_ffn_ln_b", "L0_ffn_W",
        "L0_ffn_b", "L1_gnn_a", "L1_ffn_gate_w", "L1_ffn_gate_b", "L1_ffn_w1", "L1_ffn_w2", "L1_ffn_w3"]


def build(nc, inputs, stop_after=9):
    import numpy as _np
    from concourse import mybir as _mybir

    arrays, args = {}, []
    for name in _INS:
        a = _np.asarray(inputs[name])
        if name == "adj":
            a = a.reshape(NG, GR, NT, JT, P).transpose(0, 2, 4, 3, 1).reshape(NG, NT, P, JT * GR)
        if name in ("L0_gnn_a", "L1_gnn_a"):
            a = a.reshape(2, D).T
        a = _np.ascontiguousarray(a)
        arrays[f"in_{name}_dram"] = a
        args.append(nc.dram_tensor(f"in_{name}_dram", a.shape, _mybir.dt.from_np(a.dtype), kind="ExternalInput").ap())
    out = nc.dram_tensor("out_0_dram", (N, D), _mybir.dt.float32, kind="ExternalOutput").ap()
    network(nc, *args, out, stop_after=stop_after)
    return arrays


def kernel(**inputs):
    import concourse.bacc as _bacc
    from concourse.bass_utils import run_bass_kernel_spmd as _run

    nc = _bacc.Bacc("TRN2", target_bir_lowering=False, num_devices=1)
    arrays = build(nc, inputs)
    r = _run(nc, [arrays], core_ids=[0])
    return r.results[0]["out_0_dram"]
```

```python
from contextlib import ExitStack

import concourse.bass as bass
from concourse import mybir

ALU = mybir.AluOpType
ACT = mybir.ActivationFunctionType
AX_X = mybir.AxisListType.X
F32 = mybir.dt.float32
BF16 = mybir.dt.bfloat16
I32 = mybir.dt.int32
U32 = mybir.dt.uint32
U8 = mybir.dt.uint8

P = 128
N = 4096
D = 128
NB = N // P
GB = 4
NG = NB // GB
GR = GB * P
JT = 2
NT = NB // JT
ITERS = 30
EPS = 1e-5
NEG = -1000.0
SLOPE0 = 0.01
SLOPE1 = 0.2
NPART = 3
VW = NPART * D + 1

RSQRT_MAGIC = float(0x5F1FFFF9)
RSQRT_K = 0.703952253
RSQRT_C = 2.38924456


class Chain:

    def __init__(self, eng, sem, base=0):
        self.eng, self.sem, self.base, self.n = eng, sem, base, 0

    def add(self, ins):
        self.n += 1
        ins.then_inc(self.sem, 1)

    def done(self):
        self.eng.wait_ge(self.sem, self.base + self.n)

    def link(self, ins):
        self.add(ins)
        self.done()


def rsqrt_start(v, y):
    return dict(out=y.bitcast(I32), in0=v.bitcast(I32), scalar1=-0.5, scalar2=RSQRT_MAGIC,
                op0=ALU.mult, op1=ALU.add)


def back(it, g, lag, per=NG):
    return (it, g - lag) if g >= lag else (it - 1, g - lag + per)


def wait_use(eng, sem, it, g, slots, base=0, per=NG):
    if isinstance(it, int) and it == 0 and g < slots:
        return
    eng.wait_ge(sem, it * per + (base + g + 1 - slots))


def run(eng, step, rounds, per=NG, lag=3):
    for g in range(per):
        step(0, g, first=True)
    with eng.Fori(1, rounds) as it:
        for g in range(per):
            step(it, g)
    for g in range(lag):
        step(rounds, g, last=True)


def emit_rsqrt(dve, link, v, y, t, u, newton):
    link(dve.tensor_scalar(**rsqrt_start(v, y)))
    for step in range(newton + 1):
        k, c = (RSQRT_K, RSQRT_K * RSQRT_C) if step == 0 else (0.5, 1.5)
        link(dve.tensor_tensor(t, y, y, ALU.mult))
        link(dve.scalar_tensor_tensor(u, t, -k, v, ALU.mult, ALU.mult))
        link(dve.scalar_tensor_tensor(y, u, c, y, ALU.add, ALU.mult))


def network(nc, x, adj_t, wq, wk, wv, a0, ln_w, ln_b, wf, bf, a1, gate_w, gate_b, w1, w2, w3, out,
            stop_after=9):
    with ExitStack() as ctx:
        def sb(name, shape, dt):
            return ctx.enter_context(nc.sbuf_tensor(name, shape, dt))

        def sem(name):
            return ctx.enter_context(nc.semaphore(name))

        mask_bytes = NG * NB * GR
        mask = sb("mask", [P, mask_bytes], U8)
        mask_v = mask[:, :].rearrange("p (g j i) -> p g j i", g=NG, j=NB)
        X = sb("X", [P, NB, D], F32)
        WORK = 51200
        work = sb("work", [P, WORK], U8)
        ps = ctx.enter_context(nc.psum_tensor("ps", [P, 8, 512], F32))

        def view(region, at, shape, dt, size):
            n = 1
            for s in shape:
                n *= s
            names = "abcd"[:len(shape)]
            flat = region[:, at:at + n * size].bitcast(dt)
            if len(shape) == 1:
                return flat
            return flat.rearrange(f"p ({' '.join(names)}) -> p {' '.join(names)}",
                                  **{names[i]: shape[i] for i in range(len(shape) - 1)})

        ident = sb("ident", [P, P], F32)
        ones = sb("ones", [P, P], F32)
        pool_mark = sb("pool_mark", [P, 4], F32)
        marks = sb("marks", [P, 16], F32)
        ones_bf = sb("ones_bf", [P, P], BF16)
        st6 = sb("st6", [P, NB, 6], F32)
        mv = sb("mv", [P, NB, 2], F32)
        NCOL = 16
        col = sb("col", [P, NCOL, NB], F32)
        wz = sb("wz", [P, D + 1], F32)
        wst = sb("wst", [P, D + 1], F32)
        c_col = sb("c_col", [P, 1], F32)
        c_nat = sb("c_nat", [P, D], F32)
        total = sb("total", [P, D], F32)

        v_col, y_col, t_col, u_col, s_col, cnt_col = (col[:, i, :] for i in range(6))
        e1_col, e0_col, al_col, be_col, p_col, q_col = (col[:, i, :] for i in range(6, 12))

        def dump():
            with nc.semaphore("dumped") as dumped, nc.Block() as block:
                @block.sync
                def _(sp):
                    sp.dma_start(out.rearrange("(b p) d -> p b d", p=P), X[:, :, :]).then_inc(dumped, 16)
                    sp.wait_ge(dumped, 16)

        split = view(work, 0, [NB, VW], BF16, 2)
        stage_at = (NB * VW * 2 + 63) // 64 * 64
        NS = 4
        stage = view(work, stage_at, [NS, JT, GR], I32, 4)
        M0N = 2
        conn = sb("conn", [P, M0N, JT, GR], BF16)
        xln = view(mask, 6 * NB * GR, [NB, D], F32, 4)
        xT = view(mask, 7 * NB * GR, [NB, D], F32, 4)
        rest = view(mask, 5 * NB * GR, [2, GB, D], F32, 4)
        w_in = view(mask, 4 * NB * GR, [8, D], F32, 4)
        sums = view(work, stage_at + NS * JT * GR * 4, [GB, D], F32, 4)
        sm = ctx.enter_context(nc.sbuf_tensor("small", [P, 12, 2, GB], F32))

        with ExitStack() as c1:
            def sem1(name):
                return c1.enter_context(nc.semaphore(name))

            x_in = sem1("x_in")
            w_in_s = sem1("w_in_s")
            landed = [sem1(f"landed{i}") for i in range(NS)]
            stage_free = sem1("stage_free")
            stage_free_odd = sem1("stage_free_odd")
            conn_ready = sem1("conn_ready")
            conn_free = sem1("conn_free")
            zeroed = sem1("zeroed")
            ident_ok = sem1("ident_ok")
            dchain = sem1("dchain")
            xln_ready = sem1("xln_ready")
            xT_psum = sem1("xT_psum")
            xT_ready = sem1("xT_ready")
            w_ps = sem1("w_ps")
            w_rdy = sem1("w_rdy")
            val_psum = sem1("val_psum")
            part1 = sem1("part1")
            split_ready = sem1("split_ready")
            total_psum = sem1("total_psum")
            sums_psum = sem1("sums_psum")
            sums_free = sem1("sums_free")
            a_cols = sem1("a_cols")
            exp_in = sem1("exp_in")
            exp_out = sem1("exp_out")
            achain = sem1("achain")

            evac = sem1("evac")
            EVAC = 29
            cnt, sc, sc2, mx, ncnt, w1c, w0c, al, be = (sm[:, i // 2, i % 2, :] for i in range(9))
            ind, t1, t2, ex = (sm[:, 6 + i, :, :] for i in range(4))

            def mask_at(g, c):
                return mask_v[:, bass.ds(g, 1), c * JT:(c + 1) * JT, :].rearrange("p o j i -> p (o j) i")

            block = c1.enter_context(nc.Block())
            wq_s, wk_s, wv_s, wf_s, lnw_s, lnb_s, wtmp, wtmp2 = (w_in[:, i, :] for i in range(8))
            a_col = view(mask, 4 * NB * GR + 8 * D * 4, [8], F32, 4)

            @block.sync
            def _(sp):
                sp.dma_start(X[:, :, :], x.rearrange("(b p) d -> p b d", p=P)).then_inc(x_in, 16)
                for dst, src in ((wq_s, wq), (wk_s, wk), (wv_s, wv), (wf_s, wf),
                                 (lnw_s, ln_w.partition_broadcast(P)),
                                 (lnb_s, ln_b.partition_broadcast(P)),
                                 (a_col[:, 0:2], a0),
                                 (a_col[:, 2:3], bf.rearrange("(p o) -> p o", o=1))):
                    sp.dma_start(dst, src).then_inc(w_in_s, 16)
                with sp.Fori(0, NG) as g:
                    for c in range(NT):
                        if c % 2 == 0:
                            sp.wait_ge(stage_free, g * (NT // 2) + c // 2 + 1)
                        else:
                            sp.wait_ge(stage_free_odd, g * (NT // 2) + c // 2 + 1)
                        sp.dma_start(stage[:, c % NS, :, :], adj_t[bass.ds(g, 1), c, :, :].rearrange(
                            "o p (j i) -> p (o j) i", j=JT)).then_inc(landed[c % NS], 16)

            @block.gpsimd
            def _(pool):
                pool.memset(ident[:, :], 0.0).then_inc(zeroed, 1)
                pool.wait_ge(zeroed, 1)
                pool.affine_select(out=ident[:, :], in_=ident[:, :], compare_op=ALU.not_equal, fill=1.0,
                                   base=0, pattern=[[-1, P]], channel_multiplier=1).then_inc(ident_ok, 1)
                for i in range(NS // 2):
                    pool.memset(pool_mark[:, i:i + 1], 0.0).then_inc(stage_free_odd, 1)
                for t in range(1, NG * NT, 2):
                    g, c = t // NT, t % NT
                    pool.wait_ge(conn_ready, t + 1 + NS)
                    if t == 1:
                        pool.wait_ge(sums_free, 1)
                    pool.tensor_scalar(mask_v[:, g, c * JT:(c + 1) * JT, :], stage[:, c % NS, :, :], 0.0, None,
                                       ALU.is_gt).then_inc(stage_free_odd, 1)

            @block.scalar
            def _(act):
                act.wait_ge(w_ps, 1)
                act.activation(wst[:, 0:D], ps[:, 7, 0:D], ACT.Copy).then_inc(w_rdy, 1)
                act.activation(wst[:, D:D + 1], ps[:, 6, 0:1], ACT.Copy).then_inc(w_rdy, 1)
                act.wait_ge(w_ps, 2)
                act.activation(wz[:, 0:D], ps[:, 5, 128:256], ACT.Copy).then_inc(w_rdy, 1)
                act.activation(c_nat[:, :], ps[:, 5, 256:384], ACT.Copy).then_inc(w_rdy, 1)
                for g in range(NG):
                    act.wait_ge(xT_psum, g + 1)
                    act.activation(xT[:, g * GB:(g + 1) * GB, :],
                                   ps[:, g % 2, :].rearrange("p (b d) -> p b d", b=GB),
                                   ACT.Copy).then_inc(xT_ready, 1)
                    act.wait_ge(val_psum, g + 1)
                    vals = ps[:, 2 + 2 * (g % 2):4 + 2 * (g % 2), :].rearrange("p k (h c) -> p (k h) c", h=2)
                    act.activation(split[:, g * GB:(g + 1) * GB, 0:D], vals[:, :, 0:D],
                                   ACT.Copy).then_inc(part1, 1)
                with act.Fori(0, NG) as g:
                    act.wait_ge(exp_in, g + 1)
                    act.activation(ex, t1, ACT.Exp).then_inc(exp_out, 1)

            @block.tensor
            def _(pe):
                pe.wait_ge(w_in_s, 16 * 8)
                pe.wait_ge(ident_ok, 1)
                pe.transpose(ps[:, 7, 0:D], wv_s, ident[:, :])
                pe.matmul(ps[:, 6, 0:1], wq_s, a_col[:, 0:1], start=True, stop=False)
                pe.matmul(ps[:, 6, 0:1], wk_s, a_col[:, 1:2], start=False, stop=True).then_inc(w_ps, 1)
                pe.wait_ge(a_cols, 1)
                pe.transpose(ps[:, 5, 128:256], wtmp, ident[:, :])
                pe.matmul(ps[:, 5, 256:384], c_col[:, 0:1].broadcast_to([P, P]), ident[:, :],
                          start=True, stop=True).then_inc(w_ps, 1)
                for g in range(NG):
                    pe.wait_ge(xln_ready, g + 1)
                    if g >= 2:
                        pe.wait_ge(xT_ready, g - 1)
                    for b in range(GB):
                        last = pe.transpose(ps[:, g % 2, b * P:(b + 1) * P], xln[:, g * GB + b, :],
                                            ident[:, :])
                    last.then_inc(xT_psum, 1)
                    pe.wait_ge(xT_ready, g + 1)
                    if g == 0:
                        pe.wait_ge(w_rdy, 4)
                    if g >= 2:
                        pe.wait_ge(split_ready, g - 1)
                    for b in range(GB):
                        last = pe.matmul(ps[:, 2 + 2 * (g % 2) + b // 2, (b % 2) * 256:(b % 2) * 256 + D + 1],
                                         xT[:, g * GB + b, :], wst[:, :], start=True, stop=True)
                    last.then_inc(val_psum, 1)
                pe.wait_ge(split_ready, NG)
                for b in range(NB):
                    last = pe.matmul(ps[:, 7, 0:VW], ones_bf[:, :], split[:, b, :],
                                     start=(b == 0), stop=(b == NB - 1))
                last.then_inc(total_psum, 1)
                with pe.Fori(0, NG) as g:
                    pe.wait_ge(sums_free, g + 1)
                    for c in range(NT):
                        pe.wait_ge(conn_ready, g * NT + c + 1 + NS)
                        for j in range(JT):
                            for b in range(GB):
                                last = pe.matmul(ps[:, b, 0:VW], conn[:, c % M0N, j, b * P:(b + 1) * P],
                                                 split[:, c * JT + j, :], start=(c + j == 0),
                                                 stop=(c == NT - 1 and j == JT - 1))
                        last.then_inc(conn_free, 1)

            @block.vector
            def _(dve):
                ch = Chain(dve, dchain)
                for i in range(NS // 2):
                    dve.memset(marks[:, i:i + 1], 0.0).then_inc(stage_free, 1)
                for i in range(NS):
                    dve.memset(marks[:, 4 + i:5 + i], 0.0).then_inc(conn_ready, 1)
                for i in range(M0N):
                    dve.memset(marks[:, 8 + i:9 + i], 0.0).then_inc(conn_free, 1)
                dve.memset(ones_bf[:, :], 1.0)
                dve.memset(ones[:, :], 1.0)
                dve.memset(wz[:, D:D + 1], 1.0 / D)
                ch.link(dve.memset(split[:, :, VW - 1:VW], 1.0))
                dve.wait_ge(w_in_s, 16 * 8)
                ch.add(dve.tensor_tensor(wtmp2, wf_s, lnb_s, ALU.mult))
                ch.link(dve.tensor_tensor(wtmp, wf_s, lnw_s, ALU.mult))
                ch.add(dve.tensor_reduce(a_col[:, 3:4], wtmp2, AX_X, ALU.add))
                ch.link(dve.tensor_reduce(a_col[:, 4:5], wtmp, AX_X, ALU.add))
                ch.add(dve.tensor_scalar(a_col[:, 5:6], a_col[:, 4:5], 1.0 / D, None, ALU.mult))
                ch.link(dve.tensor_tensor(c_col[:, :], a_col[:, 3:4], a_col[:, 2:3], ALU.add))
                dve.tensor_scalar(wtmp, wtmp, a_col[:, 5:6], None, ALU.subtract).then_inc(a_cols, 1)
                dve.wait_ge(x_in, 16)
                for b in range(NB):
                    ch.add(dve.bn_stats(st6[:, b, :], X[:, b, :]))
                ch.done()
                for b in range(NB):
                    ch.add(dve.bn_aggr(mv[:, b, :], st6[:, b, :]))
                ch.done()
                ch.link(dve.tensor_scalar(v_col, mv[:, :, 1], EPS, None, ALU.add))
                emit_rsqrt(dve, ch.link, v_col, y_col, t_col, u_col, 2)
                for b in range(NB):
                    ins = dve.tensor_scalar(xln[:, b, :], X[:, b, :], mv[:, b, 0:1], y_col[:, b:b + 1],
                                            ALU.subtract, ALU.mult)
                    if b % GB == GB - 1:
                        ins.then_inc(xln_ready, 1)
                for g in range(NG):
                    blocks = slice(g * GB, (g + 1) * GB)
                    vals = ps[:, 2 + 2 * (g % 2):4 + 2 * (g % 2), :].rearrange("p k (h c) -> p (k h) c", h=2)
                    dve.wait_ge(part1, g + 1)
                    ch.add(dve.tensor_copy(s_col[:, blocks], vals[:, :, D]))
                    ch.link(dve.tensor_tensor(rest[:, 0, :, :], vals[:, :, 0:D], split[:, blocks, 0:D], ALU.subtract))
                    ch.link(dve.tensor_copy(split[:, blocks, D:2 * D], rest[:, 0, :, :]))
                    ch.link(dve.tensor_tensor(rest[:, 1, :, :], rest[:, 0, :, :], split[:, blocks, D:2 * D],
                                              ALU.subtract))
                    dve.tensor_copy(split[:, blocks, 2 * D:3 * D], rest[:, 1, :, :]).then_inc(split_ready, 1)
                dve.wait_ge(total_psum, 1)
                ch.link(dve.tensor_reduce(total[:, :], ps[:, 7, 0:3 * D].rearrange("p (t d) -> p d t", t=3), AX_X,
                                          ALU.add))
                dve.memset(al_col, 0.0).then_inc(sums_free, 1)
                with dve.Fori(0, NG) as g:
                    for c in range(NT):
                        dve.wait_ge(landed[c % NS], (g * (NT // NS) + c // NS + 1) * 16)
                        dve.wait_ge(conn_free, g * NT + c + 1)
                        dve.tensor_scalar(conn[:, c % M0N, :, :], stage[:, c % NS, :, :], 0.0, None,
                                          ALU.not_equal).then_inc(conn_ready, 1)
                        if c % 2 == 0:
                            dve.tensor_scalar(mask_at(g, c), stage[:, c % NS, :, :], 0.0, None,
                                              ALU.is_gt).then_inc(stage_free, 1)
                    dve.wait_ge(conn_free, g * NT + NT + M0N)
                    lk = Chain(dve, evac, g * EVAC)
                    for b in range(GB):
                        lk.add(dve.tensor_reduce(sums[:, b, :], ps[:, b, 0:3 * D].rearrange("p (t d) -> p d t", t=3),
                                                 AX_X, ALU.add))
                    lk.add(dve.tensor_copy(cnt, ps[:, 0:GB, VW - 1]))
                    lk.done()
                    lk.add(dve.tensor_scalar(sc2, s_col[:, bass.ds(g * GB, GB)], SLOPE0, None, ALU.mult))
                    lk.add(dve.tensor_scalar(ind[:, 0, :], cnt, 0.0, None, ALU.is_gt))
                    lk.link(dve.tensor_scalar(ind[:, 1, :], cnt, float(N), None, ALU.is_ge))
                    dve.memset(sm[:, 11, :, :], 0.0).then_inc(sums_free, 1)
                    lk.add(dve.tensor_tensor(sc, s_col[:, bass.ds(g * GB, GB)], sc2, ALU.max))
                    lk.link(dve.tensor_scalar(t2, ind, -NEG, NEG, ALU.mult, ALU.add))
                    lk.link(dve.tensor_tensor(t1, ind, sc.unsqueeze(1).broadcast_to([P, 2, GB]), ALU.mult))
                    lk.link(dve.tensor_tensor(t1, t1, t2, ALU.add))
                    lk.link(dve.tensor_tensor(mx, t1[:, 0, :], t1[:, 1, :], ALU.max))
                    lk.add(dve.tensor_scalar(ncnt, cnt, -1.0, float(N), ALU.mult, ALU.add))
                    dve.tensor_tensor(t1, t1, mx.unsqueeze(1).broadcast_to([P, 2, GB]),
                                      ALU.subtract).then_inc(exp_in, 1)
                    dve.wait_ge(exp_out, g + 1)
                    lk.add(dve.tensor_tensor(w1c, ex[:, 0, :], cnt, ALU.mult))
                    lk.add(dve.tensor_tensor(al, ex[:, 0, :], ex[:, 1, :], ALU.subtract))
                    lk.link(dve.tensor_tensor(w0c, ex[:, 1, :], ncnt, ALU.mult))
                    lk.link(dve.tensor_tensor(w1c, w1c, w0c, ALU.add))
                    lk.link(dve.reciprocal(w1c, w1c))
                    lk.add(dve.tensor_tensor(al, al, w1c, ALU.mult))
                    lk.link(dve.tensor_tensor(be, ex[:, 1, :], w1c, ALU.mult))
                    for b in range(GB):
                        xb = X[:, bass.ds(g * GB + b, 1), :].rearrange("p o d -> p (o d)")
                        lk.add(dve.scalar_tensor_tensor(xb, sums[:, b, :], al[:, b:b + 1], xb, ALU.mult, ALU.add))
                    lk.done()
                    for b in range(GB):
                        xb = X[:, bass.ds(g * GB + b, 1), :].rearrange("p o d -> p (o d)")
                        lk.add(dve.scalar_tensor_tensor(xb, total[:, :], be[:, b:b + 1], xb, ALU.mult, ALU.add))
                    lk.done()
                    assert lk.n == EVAC, lk.n
        if stop_after <= 1:
            return dump()

        UP = 100.0
        NP = NG // 2
        PB = 2 * GB
        NH = 2
        HB = NB // NH
        hN = view(work, 0, [NB, D], F32, 4)
        tN = view(work, 16384, [2, GB, D], F32, 4)
        sN, sT = (view(work, 20480 + i * 8192, [4, GB, D], F32, 4) for i in range(2))
        zeros = view(work, 40960, [16, D], F32, 4)
        SLOTS_E = 2 * N + 16 * P
        xs_d = nc.dram_tensor("xs_d", (SLOTS_E, D), F32, kind="Internal").ap()
        ys_d = nc.dram_tensor("ys_d", (SLOTS_E, D), F32, kind="Internal").ap()
        with ExitStack() as c2:
            def sem2(name):
                return c2.enter_context(nc.semaphore(name))

            dchain = sem2("f_dchain")
            c_up = sem2("c_up")
            h_ready = sem2("h_ready")
            t_ready = sem2("t_ready")
            g_ready = sem2("g_ready")
            s_ready = sem2("s_ready")
            stats = sem2("stats")
            sT_psum = sem2("sT_psum")
            sT_ready = sem2("sT_ready")
            z_psum = sem2("z_psum")
            rchain = sem2("rchain")
            xc = sem2("xc")
            RC = 12
            zero_ok = sem2("zero_ok")
            zero_out = sem2("zero_out")
            fst = view(work, 36864, [NH, HB, 6], F32, 4)
            fs = view(work, 38400, [NH, 7, HB], F32, 4)
            c100 = view(work, 39936, [D], F32, 4)
            block = c2.enter_context(nc.Block())

            def rows(g):
                return slice(g * GB, (g + 1) * GB)

            @block.sync
            def _(sp):
                sp.wait_ge(zero_ok, 1)
                for i in range(SLOTS_E // (16 * P)):
                    sp.dma_start(xs_d[i * 16 * P:(i + 1) * 16 * P, :].rearrange("(p t) d -> p t d", p=P),
                                 zeros).then_inc(zero_out, 16)
                sp.wait_ge(zero_out, 16 * (SLOTS_E // (16 * P)))

            @block.tensor
            def _(pe):
                def turn(it, g):
                    pe.wait_ge(s_ready, it * NG + g + 1)
                    wait_use(pe, sT_ready, it, g, 4)
                    for b in range(GB):
                        last = pe.transpose(ps[:, 4 + g % 4, b * P:(b + 1) * P], sN[:, g % 4, b, :], ident[:, :])
                    last.then_inc(sT_psum, 1)

                def product(it, g):
                    pe.wait_ge(sT_ready, it * NG + g + 1)
                    wait_use(pe, h_ready, it, g, 4, NG)
                    for b in range(GB):
                        last = pe.matmul(ps[:, g % 4, b * D:(b + 1) * D], sT[:, g % 4, b, :], wz[:, 0:D],
                                         start=True, stop=True)
                    last.then_inc(z_psum, 1)

                def step(it, p, first=False, last=False):
                    for k in range(2):
                        if not (first and p < 1) and not (last and p >= 1):
                            it1, p1 = back(it, p, 1, NP)
                            turn(it1, 2 * p1 + k)
                    for k in range(2):
                        if not (first and p < 2):
                            it2, p2 = back(it, p, 2, NP)
                            product(it2, 2 * p2 + k)

                run(pe, step, ITERS, per=NP, lag=2)

            @block.scalar
            def _(act):
                def tanh(it, g):
                    act.wait_ge(h_ready, it * NG + g + 1)
                    wait_use(act, g_ready, it, g, 2)
                    act.activation(tN[:, g % 2, :, :], hN[:, rows(g), :], ACT.Tanh, scale=1.0 / UP).then_inc(
                        t_ready, 1)

                def silu(it, g):
                    act.wait_ge(g_ready, it * NG + g + 1)
                    wait_use(act, sT_psum, it, g, 4)
                    if not (isinstance(it, int) and it == 0 and g < 4):
                        act.wait_ge(stats, it * NB + (g - 3) * GB)
                    act.activation(sN[:, g % 4, :, :], hN[:, rows(g), :], ACT.Silu, scale=1.0 / UP).then_inc(
                        s_ready, 1)

                def take_turned(it, g):
                    act.wait_ge(sT_psum, it * NG + g + 1)
                    wait_use(act, z_psum, it, g, 4)
                    act.activation(sT[:, g % 4, :, :], ps[:, 4 + g % 4, :].rearrange("p (b i) -> p b i", b=GB),
                                   ACT.Copy).then_inc(sT_ready, 1)

                def step(it, p, first=False, last=False):
                    for k in range(2):
                        if not last:
                            tanh(it, 2 * p + k)
                    for k in range(2):
                        if not (first and p < 1):
                            it1, p1 = back(it, p, 1, NP)
                            take_turned(it1, 2 * p1 + k)
                    for k in range(2):
                        if not last:
                            silu(it, 2 * p + k)

                run(act, step, ITERS, per=NP, lag=1)

            @block.gpsimd
            def _(pool):
                pool.memset(zeros, 0.0).then_inc(zero_ok, 1)

                def sum_(it, g):
                    pool.wait_ge(t_ready, it * NG + g + 1)
                    pool.tensor_tensor(hN[:, rows(g), :], hN[:, rows(g), :], tN[:, g % 2, :, :],
                                       ALU.add).then_inc(g_ready, 1)

                for g in range(NG):
                    sum_(0, g)
                for g in range(NG):
                    pool.tensor_tensor(X[:, rows(g), :], X[:, rows(g), :],
                                       c_nat[:, :].unsqueeze(1).broadcast_to([P, GB, D]), ALU.add).then_inc(xc, 1)
                with pool.Fori(1, ITERS) as it:
                    for g in range(NG):
                        sum_(it, g)

            @block.vector
            def _(dve):
                ch = Chain(dve, dchain)
                dve.tensor_scalar(c100, c_nat[:, :], UP, None, ALU.mult).then_inc(c_up, 1)
                for b in range(NB):
                    ch.add(dve.bn_stats(st6[:, b, :], X[:, b, :]))
                ch.done()
                for b in range(NB):
                    ch.add(dve.bn_aggr(mv[:, b, :], st6[:, b, :]))
                ch.done()
                ch.link(dve.tensor_scalar(v_col, mv[:, :, 1], EPS, None, ALU.add))
                emit_rsqrt(dve, ch.link, v_col, y_col, t_col, u_col, 2)
                ch.link(dve.tensor_scalar(y_col, y_col, UP, None, ALU.mult))
                dve.wait_ge(c_up, 1)

                def normalise(g):
                    for b in range(g * GB, (g + 1) * GB):
                        last = dve.tensor_scalar(hN[:, b, :], X[:, b, :], mv[:, b, 0:1], y_col[:, b:b + 1],
                                                 ALU.subtract, ALU.mult)
                    last.then_inc(h_ready, 1)

                def affine(it, p, c):
                    g, b = 2 * p + c // GB, c % GB
                    it1 = it - 1
                    if c == 0:
                        dve.wait_ge(rchain, it1 * (NH * RC) + (p // 2 + 1) * RC)
                    if b == 0:
                        dve.wait_ge(z_psum, it1 * NG + g + 1)
                    cc = (p % 2) * PB + c
                    y = fs[:, p // 2, 5, cc:cc + 1]
                    ins = dve.scalar_tensor_tensor(hN[:, g * GB + b, :], ps[:, g % 4, b * D:(b + 1) * D], y,
                                                   c100, ALU.mult, ALU.add)
                    if b == GB - 1:
                        ins.then_inc(h_ready, 1)

                def result(p, c):
                    g, b = 2 * p + c // GB, c % GB
                    cc = (p % 2) * PB + c
                    if cc == 0:
                        dve.wait_ge(rchain, (ITERS - 1) * (NH * RC) + (p // 2 + 1) * RC)
                        ch.link(dve.tensor_scalar(fs[:, p // 2, 6, :], fs[:, p // 2, 5, :], 1.0 / UP, None, ALU.mult))
                        dve.wait_ge(xc, NG)
                    if b == 0:
                        dve.wait_ge(z_psum, (ITERS - 1) * NG + g + 1)
                    xb = X[:, g * GB + b, :]
                    ins = dve.scalar_tensor_tensor(xb, ps[:, g % 4, b * D:(b + 1) * D], fs[:, p // 2, 6, cc:cc + 1], xb,
                                                   ALU.mult, ALU.add)
                    if b == GB - 1:
                        ins.then_inc(h_ready, 1)

                def measure(it, p, c):
                    g, b = 2 * p + c // GB, c % GB
                    if b == 0:
                        dve.wait_ge(s_ready, it * NG + g + 1)
                    dve.bn_stats(fst[:, p // 2, (p % 2) * PB + c, :], sN[:, g % 4, b, :]).then_inc(stats, 1)

                def short(i, it, q):
                    d, dd, m2, v, t, y, u = (fs[:, q, k, :] for k in range(7))
                    st = fst[:, q, :, :]
                    if i == 0:
                        dve.wait_ge(stats, it * NB + (q + 1) * HB)
                    else:
                        dve.wait_ge(rchain, it * (NH * RC) + (q * RC + i))
                    if i == 0:
                        ins = dve.tensor_tensor(d, st[:, :, 1], st[:, :, 4], ALU.subtract)
                    if i == 1:
                        ins = dve.tensor_tensor(m2, st[:, :, 2], st[:, :, 5], ALU.add)
                    if i == 2:
                        ins = dve.tensor_tensor(dd, d, d, ALU.mult)
                    if i == 3:
                        ins = dve.scalar_tensor_tensor(m2, dd, D / 4, m2, ALU.mult, ALU.add)
                    if i == 4:
                        ins = dve.tensor_scalar(v, m2, 1.0 / D, EPS, ALU.mult, ALU.add)
                    if i == 5:
                        ins = dve.tensor_scalar(**rsqrt_start(v, y))
                    k, c = (RSQRT_K, RSQRT_K * RSQRT_C) if i < 9 else (0.5 * UP, 1.5 * UP)
                    if i in (6, 9):
                        ins = dve.tensor_tensor(t, y, y, ALU.mult)
                    if i in (7, 10):
                        ins = dve.scalar_tensor_tensor(u, t, -k, v, ALU.mult, ALU.mult)
                    if i in (8, 11):
                        ins = dve.scalar_tensor_tensor(y, u, c, y, ALU.add, ALU.mult)
                    ins.then_inc(rchain, 1)

                def step(it, p, first=False, last=False):
                    if first:
                        normalise(2 * p)
                        normalise(2 * p + 1)
                    for i in range(2 * PB):
                        if i < RC and p == 1 and not first:
                            short(i, it - 1, 1)
                        if i < RC and p == 3 and not last:
                            short(i, it, 0)
                        if i < PB:
                            if last:
                                result(p, i)
                            elif not first:
                                affine(it, p, i)
                        elif not (first and p < 1) and not (last and p >= 1):
                            it1, p1 = back(it, p, 1, NP)
                            measure(it1, p1, i - PB)

                run(dve, step, ITERS, per=NP, lag=NP)
        if stop_after <= 2:
            return dump()

        HW = D + 1
        SB = 2
        SR = SB * P
        NSUB = NB // SB
        JC = 2
        NC = NB // JC
        SLOTS = 4
        rhs = view(work, 0, [2, NB, NPART, HW], BF16, 2)
        t_wide = view(work, 2 * NB * NPART * HW * 2, [NPART * HW], F32, 4)
        scr = conn[:, :, :, :].rearrange("p a b c -> p (a b c)").bitcast(F32)
        hT = scr[:, 0:2 * SR].rearrange("p (k i) -> p k i", k=2)
        f_w, r_w = (scr[:, (2 + i) * SR:(3 + i) * SR].rearrange("p (b d) -> p b d", b=SB) for i in range(2))
        a_bc = scr[:, 0:2 * SR].rearrange("p (k i) -> p k i", k=2)
        x_t = scr[:, 2 * SR:4 * SR].rearrange("p (k b d) -> p k b d", k=2, b=SB)
        tiles3 = X[:, 0:24, :].rearrange("p b d -> p (b d)").bitcast(BF16).rearrange(
            "p (f s j i) -> p f s j i", f=3, s=SLOTS, j=JC)
        m_bf, pairs = tiles3[:, 0], tiles3[:, 1:3]
        x2_d = nc.dram_tensor("x2_d", (N, D), F32, kind="Internal").ap()
        x3_d = nc.dram_tensor("x3_d", (N, D), F32, kind="Internal").ap()
        ab_d = nc.dram_tensor("ab_d", (2 * NB, P), F32, kind="Internal").ap()
        h_d = nc.dram_tensor("h_d", (N, D), F32, kind="Internal").ap()
        aw = sb("aw", [P, 2], F32)
        ab = sb("ab", [P, 2, NB], F32)
        FF = sb("FF", [P, 2, NB], F32)
        CC = sb("CC", [P, 2, NB], F32)
        negb = sb("negb", [P, NB], F32)
        bm = sb("bm", [P, 4], F32)
        spread = sb("spread", [P, 1], F32)
        far = sb("far", [P, 1], I32)
        FAR = 64.0
        num = sb("num", [P, SB, HW], F32)
        ab_rows = sb("ab_rows", [2 * NB, P], F32)
        dn = sb("dn", [P, 4, SB], F32)
        H = X
        with ExitStack() as c3:
            def sem3(name):
                return c3.enter_context(nc.semaphore(name))

            dchain = sem3("g_dchain")
            achain = sem3("g_achain")
            saved = sem3("saved")
            aw_in = sem3("aw_in")
            h_ready = sem3("g_h_ready")
            hT_psum = sem3("g_hT_psum")
            hT_ready = sem3("g_hT_ready")
            ab_psum = sem3("ab_psum")
            b_max = sem3("b_max")
            b_all = sem3("b_all")
            f_in = sem3("f_in")
            f_out = sem3("f_out")
            c_in = sem3("c_in")
            c_out = sem3("c_out")
            f_ready = sem3("f_ready")
            r_ready = sem3("r_ready")
            r2_ready = sem3("r2_ready")
            p1_ready = sem3("p1_ready")
            p2_ready = sem3("p2_ready")
            p3_ready = sem3("p3_ready")
            ones_col = sem3("ones_col")
            a_psum = sem3("a_psum")
            ab_row = sem3("ab_row")
            a_saved = sem3("a_saved")
            th_psum = sem3("th_psum")
            block = c3.enter_context(nc.Block())

            @block.sync
            def _(sp):
                sp.dma_start(x2_d.rearrange("(b p) d -> p b d", p=P), X[:, :, :]).then_inc(saved, 16)
                sp.dma_start(aw[:, :], a1).then_inc(aw_in, 16)
                sp.wait_ge(h_ready, NSUB)
                sp.dma_start(h_d.rearrange("(b p) d -> p b d", p=P), H[:, :, :]).then_inc(saved, 16)
                sp.wait_ge(ab_row, 1)
                sp.dma_start(ab_d, ab_rows[:, :]).then_inc(a_saved, 16)
                sp.wait_ge(a_saved, 16)
                sp.wait_ge(saved, 32)

            @block.gpsimd
            def _(pool):
                pool.wait_ge(b_max, 2)
                pool.partition_all_reduce(bm[:, 2:4], bm[:, 0:2], P, bass.bass_isa.ReduceOp.max).then_inc(b_all, 1)

            @block.tensor
            def _(pe):
                pe.wait_ge(aw_in, 16)
                for u in range(NSUB):
                    pe.wait_ge(h_ready, u + 1)
                    if u >= 2:
                        pe.wait_ge(hT_ready, u - 1)
                    for b in range(SB):
                        last = pe.transpose(ps[:, u % 2, b * P:(b + 1) * P], H[:, u * SB + b, :], ident[:, :])
                    last.then_inc(hT_psum, 1)
                    for b in range(SB):
                        last = pe.matmul(ps[:, 3, 0:D], ones[:, :], H[:, u * SB + b, :], start=(u + b == 0),
                                         stop=(u == NSUB - 1 and b == SB - 1))
                    if u == NSUB - 1:
                        last.then_inc(th_psum, 1)
                    pe.wait_ge(hT_ready, u + 1)
                    for b in range(SB):
                        k = u * SB + b
                        last = pe.matmul(ps[:, 2, 2 * k:2 * k + 2], hT[:, u % 2, b * P:(b + 1) * P], aw[:, :],
                                         start=True, stop=True)
                    last.then_inc(ab_psum, 1)
                pe.wait_ge(f_in, 1)
                pe.transpose(ps[0:2 * NB, 4, 0:P], ab[:, :, :].rearrange("p k b -> p (k b)"), ident[:, :]).then_inc(a_psum, 1)

            @block.scalar
            def _(act):
                for u in range(NSUB):
                    act.wait_ge(hT_psum, u + 1)
                    if u >= 2:
                        act.wait_ge(ab_psum, u - 1)
                    act.activation(hT[:, u % 2, :], ps[:, u % 2, 0:SR], ACT.Copy).then_inc(hT_ready, 1)
                act.wait_ge(a_psum, 1)
                act.activation(ab_rows[:, :], ps[0:2 * NB, 4, 0:P], ACT.Copy).then_inc(ab_row, 1)
                act.wait_ge(f_in, 2)
                act.activation(FF[:, :, :], FF[:, :, :], ACT.Exp).then_inc(f_out, 1)
                act.wait_ge(c_in, 1)
                act.activation(CC[:, :, :], CC[:, :, :], ACT.Exp).then_inc(c_out, 1)
                for k in range(2 * NSUB):
                    u, f = k // 2, k % 2
                    blocks = slice(u * SB, (u + 1) * SB)
                    act.wait_ge(f_ready, k + 1)
                    act.activation(rhs[:, f, blocks, 0, 0:D], f_w, ACT.Copy).then_inc(p1_ready, 1)
                    act.wait_ge(r_ready, k + 1)
                    act.activation(rhs[:, f, blocks, 1, 0:D], r_w, ACT.Copy).then_inc(p2_ready, 1)
                    act.wait_ge(r2_ready, k + 1)
                    act.activation(rhs[:, f, blocks, 2, 0:D], r_w, ACT.Copy).then_inc(p3_ready, 1)

            @block.vector
            def _(dve):
                ch = Chain(dve, dchain)
                for b in range(NB):
                    ch.add(dve.bn_stats(st6[:, b, :], X[:, b, :]))
                ch.done()
                for b in range(NB):
                    ch.add(dve.bn_aggr(mv[:, b, :], st6[:, b, :]))
                ch.done()
                ch.link(dve.tensor_scalar(v_col, mv[:, :, 1], EPS, None, ALU.add))
                emit_rsqrt(dve, ch.link, v_col, y_col, t_col, u_col, 2)
                dve.wait_ge(saved, 16)
                for b in range(NB):
                    ins = dve.tensor_scalar(H[:, b, :], X[:, b, :], mv[:, b, 0:1], y_col[:, b:b + 1],
                                            ALU.subtract, ALU.mult)
                    if b % SB == SB - 1:
                        ins.then_inc(h_ready, 1)
                dve.wait_ge(ab_psum, NSUB)
                ch.link(dve.tensor_copy(ab[:, :, :], ps[:, 2, 0:2 * NB].rearrange("p (b k) -> p k b", k=2)))
                dve.tensor_reduce(bm[:, 0:1], ab[:, 1, :], AX_X, ALU.max).then_inc(b_max, 1)
                dve.tensor_scalar(negb[:, :], ab[:, 1, :], -1.0, None, ALU.mult).then_inc(f_in, 1)
                dve.wait_ge(f_in, 1)
                dve.tensor_reduce(bm[:, 1:2], negb[:, :], AX_X, ALU.max).then_inc(b_max, 1)
                dve.wait_ge(b_all, 1)
                ch.link(dve.tensor_tensor(spread[:, :], bm[:, 2:3], bm[:, 3:4], ALU.add))
                ch.link(dve.tensor_scalar(far[:, :], spread[:, :], FAR, None, ALU.is_gt))
                ch.link(dve.tensor_scalar(FF[:, 0, :], ab[:, 1, :], bm[:, 2:3], None, ALU.subtract))
                dve.tensor_scalar(FF[:, 1, :], FF[:, 0, :], SLOPE1, None, ALU.mult).then_inc(f_in, 1)
                ch.link(dve.tensor_scalar(CC[:, 0, :], ab[:, 0, :], bm[:, 2:3], None, ALU.add))
                ch.link(dve.tensor_scalar(CC[:, 1, :], CC[:, 0, :], SLOPE1, None, ALU.mult))
                ch.link(dve.tensor_tensor(t_col, CC[:, 0, :], CC[:, 1, :], ALU.max))
                dve.tensor_tensor(CC[:, :, :], CC[:, :, :], t_col.unsqueeze(1).broadcast_to([P, 2, NB]),
                                  ALU.subtract).then_inc(c_in, 1)
                dve.wait_ge(f_out, 1)
                ch.link(dve.tensor_copy(rhs[:, :, :, 0, D], FF[:, :, :]))
                rr = col[:, 0:2, :]
                ch.link(dve.tensor_tensor(rr, FF[:, :, :], rhs[:, :, :, 0, D], ALU.subtract))
                ch.link(dve.tensor_copy(rhs[:, :, :, 1, D], rr))
                ch.link(dve.tensor_tensor(rr, rr, rhs[:, :, :, 1, D], ALU.subtract))
                ch.link(dve.tensor_copy(rhs[:, :, :, 2, D], rr))
                dve.wait_ge(th_psum, 1)
                ch.link(dve.tensor_scalar(total[:, :], ps[:, 3, 0:D], 1.0 / N, None, ALU.mult))
                for k in range(2 * NSUB):
                    u, f = k // 2, k % 2
                    blocks = slice(u * SB, (u + 1) * SB)
                    if k >= 1:
                        dve.wait_ge(p3_ready, k)
                    dve.tensor_tensor(f_w, H[:, blocks, :], FF[:, f, blocks].unsqueeze(2).broadcast_to([P, SB, D]),
                                      ALU.mult).then_inc(f_ready, 1)
                    dve.wait_ge(p1_ready, k + 1)
                    dve.tensor_tensor(r_w, f_w, rhs[:, f, blocks, 0, 0:D], ALU.subtract).then_inc(r_ready, 1)
                    dve.wait_ge(p2_ready, k + 1)
                    dve.tensor_tensor(r_w, r_w, rhs[:, f, blocks, 1, 0:D], ALU.subtract).then_inc(r2_ready, 1)
                dve.wait_ge(p3_ready, 2 * NSUB)

        with ExitStack() as c4:
            def sem4(name):
                return c4.enter_context(nc.semaphore(name))

            mchain = sem4("mchain")
            up_ready = sem4("up_ready")
            m_ready = sem4("m_ready")
            low_dve = sem4("low_dve")
            low_pool = sem4("low_pool")
            used = sem4("used")
            banks_free = sem4("banks_free")
            low_sum = sem4("low_sum")
            wide_free = sem4("wide_free")
            a_in = [sem4(f"a_in{i}") for i in range(2)]
            x_in3 = [sem4(f"x_in3{i}") for i in range(2)]
            x_out = [sem4(f"x_out{i}") for i in range(2)]
            x_done = sem4("x_done")
            block = c4.enter_context(nc.Block())
            a_flat = ab_d.rearrange("b p -> (b p)")
            EV = 9

            @block.sync
            def _(sp):
                for s in range(NSUB):
                    if s >= 2:
                        sp.wait_ge(up_ready, (s - 1) * NC)
                    sp.dma_start(a_bc[:, s % 2, :], a_flat[s * SR:(s + 1) * SR].partition_broadcast(P)).then_inc(
                        a_in[s % 2], 16)
                    if s >= 2:
                        sp.wait_ge(x_done, s - 1)
                        sp.dma_start(x3_d[(s - 2) * SR:(s - 1) * SR, :].rearrange("(b p) d -> p b d", p=P),
                                     x_t[:, s % 2, :, :]).then_inc(x_out[s % 2], 16)
                        sp.wait_ge(x_out[s % 2], (s // 2) * 16)
                    sp.dma_start(x_t[:, s % 2, :, :], x2_d[s * SR:(s + 1) * SR, :].rearrange(
                        "(b p) d -> p b d", p=P)).then_inc(x_in3[s % 2], 16)
                for s in (NSUB - 2, NSUB - 1):
                    sp.wait_ge(x_done, s + 1)
                    sp.dma_start(x3_d[s * SR:(s + 1) * SR, :].rearrange("(b p) d -> p b d", p=P),
                                 x_t[:, s % 2, :, :]).then_inc(x_out[s % 2], 16)
                for i in range(2):
                    sp.wait_ge(x_out[i], NSUB // 2 * 16)

            @block.gpsimd
            def _(pool):
                for k in range(3, NSUB * NC, 4):
                    pool.wait_ge(up_ready, k + 1)
                    pool.tensor_tensor(pairs[:, 1, k % SLOTS, :, :], m_bf[:, k % SLOTS, :, :],
                                       pairs[:, 0, k % SLOTS, :, :], ALU.subtract).then_inc(low_pool, 1)

            @block.tensor
            def _(pe):
                def chunk(g, h, c):
                    s = 2 * g + h
                    if c == 0:
                        pe.wait_ge(banks_free, s + 1)
                    pe.wait_ge(up_ready, s * NC + c + 1)
                    for f in range(2):
                        if f == 1:
                            if c % 4 == 3:
                                pe.wait_ge(low_pool, s * (NC // 4) + c // 4 + 1)
                            else:
                                pe.wait_ge(low_dve, s * (NC // 4 * 3) + c // 4 * 3 + c % 4 + 1)
                        for j in range(JC):
                            for b in range(SB):
                                last = pe.matmul(ps[:, 4 * h + 2 * f + b, 0:NPART * HW],
                                                 pairs[:, f, c % SLOTS, j, b * P:(b + 1) * P],
                                                 rhs[:, f, c * JC + j, :, :].rearrange("p t d -> p (t d)"),
                                                 start=(c + j == 0), stop=(c == NC - 1 and j == JC - 1))
                    last.then_inc(used, 1)

                with pe.Fori(0, NSUB // 2) as g:
                    for h in range(2):
                        for c in range(NC):
                            chunk(g, h, c)

            @block.scalar
            def _(act):
                def scale_low(g, h, b):
                    s = 2 * g + h
                    if b == 0:
                        act.wait_ge(used, (s + 1) * NC + SLOTS)
                    act.wait_ge(wide_free, s * SB + b + 1)
                    act.activation(t_wide, ps[:, 4 * h + 2 + b, 0:NPART * HW], ACT.Copy,
                                   scale=CC[:, 1, bass.ds(s * SB + b, 1)]).then_inc(low_sum, 1)

                def mask_chunk(g, h, c):
                    act.wait_ge(used, (2 * g + h) * NC + c + 1)
                    m = mask_v[:, bass.ds(g, 1), c * JC:(c + 1) * JC, h * SR:(h + 1) * SR].rearrange(
                        "p o j i -> p (o j) i")
                    act.activation(m_bf[:, c % SLOTS, :, :], m, ACT.Copy).then_inc(m_ready, 1)

                def body(g, first=False):
                    for h in range(2):
                        for c in range(NC):
                            mask_chunk(g, h, c)
                            if c == SLOTS and not (first and h == 0):
                                for b in range(SB):
                                    scale_low(*((g, 0) if h == 1 else (g - 1, 1)), b)

                body(0, first=True)
                with act.Fori(1, NSUB // 2) as g:
                    body(g)
                for b in range(SB):
                    scale_low(NSUB // 2 - 1, 1, b)

            @block.vector
            def _(dve):
                for i in range(SLOTS):
                    dve.memset(marks[:, i:i + 1], 0.0).then_inc(used, 1)
                for i in range(2):
                    dve.memset(marks[:, 4 + i:5 + i], 0.0).then_inc(banks_free, 1)
                dve.memset(marks[:, 8:9], 0.0).then_inc(wide_free, 1)

                def chunk(g, h, c):
                    s = 2 * g + h
                    if c == 0:
                        dve.wait_ge(a_in[h], (g + 1) * 16)
                    dve.wait_ge(m_ready, s * NC + c + 1)
                    for j in range(JC):
                        last = dve.scalar_tensor_tensor(pairs[:, 0, c % SLOTS, j, :], a_bc[:, h, :],
                                                        negb[:, c * JC + j:c * JC + j + 1], m_bf[:, c % SLOTS, j, :],
                                                        ALU.is_ge, ALU.mult)
                    last.then_inc(up_ready, 1)

                def chunk_low(g, h, c):
                    if c % 4 != 3:
                        dve.wait_ge(up_ready, (2 * g + h) * NC + c + 1)
                        dve.tensor_tensor(pairs[:, 1, c % SLOTS, :, :], m_bf[:, c % SLOTS, :, :],
                                          pairs[:, 0, c % SLOTS, :, :], ALU.subtract).then_inc(low_dve, 1)

                def finish(g, h):
                    s = 2 * g + h
                    lk = Chain(dve, mchain, s * EV)
                    dve.wait_ge(x_in3[h], (g + 1) * 16)
                    for b in range(SB):
                        dve.wait_ge(low_sum, s * SB + b + 1)
                        lk.link(dve.scalar_tensor_tensor(t_wide, ps[:, 4 * h + b, 0:NPART * HW],
                                                         CC[:, 0, bass.ds(s * SB + b, 1)], t_wide,
                                                         ALU.mult, ALU.add))
                        lk.link(dve.tensor_reduce(num[:, b, :], t_wide.rearrange("p (t d) -> p d t", t=NPART),
                                                  AX_X, ALU.add))
                        dve.memset(marks[:, 9 + b:10 + b], 0.0).then_inc(wide_free, 1)
                    dve.memset(marks[:, 11:12], 0.0).then_inc(banks_free, 1)
                    none, den, rden = dn[:, 0, :], dn[:, 1, :], dn[:, 2, :]
                    lk.link(dve.tensor_scalar(none, num[:, :, D], 0.0, None, ALU.is_equal))
                    lk.link(dve.tensor_tensor(den, num[:, :, D], none, ALU.add))
                    lk.link(dve.reciprocal(rden, den))
                    for b in range(SB):
                        lk.add(dve.scalar_tensor_tensor(num[:, b, 0:D], total[:, :], none[:, b:b + 1], num[:, b, 0:D],
                                                        ALU.mult, ALU.add))
                    lk.done()
                    for b in range(SB):
                        ins = dve.scalar_tensor_tensor(x_t[:, h, b, :], num[:, b, 0:D], rden[:, b:b + 1],
                                                       x_t[:, h, b, :], ALU.mult, ALU.add)
                    ins.then_inc(x_done, 1)
                    assert lk.n == EV, lk.n

                def body(g, first=False):
                    for h in range(2):
                        for c in range(NC):
                            chunk(g, h, c)
                            chunk_low(g, h, c)
                            if c == SLOTS and not (first and h == 0):
                                finish(*((g, 0) if h == 1 else (g - 1, 1)))

                body(0, first=True)
                with dve.Fori(1, NSUB // 2) as g:
                    body(g)
                finish(NSUB // 2 - 1, 1)

        BIG = 1e30
        h_all = X
        b_bc = view(work, 0, [N], F32, 4)
        score = view(work, 4 * N, [N], F32, 4)
        far_m = view(work, 8 * N, [N], BF16, 2)
        pen = view(work, 8 * N, [N], F32, 4)
        prob_T = pen
        ident_bf = sb("ident_bf", [P, P], BF16)
        with ExitStack() as c5:
            def sem5(name):
                return c5.enter_context(nc.semaphore(name))

            far_in = sem5("far_in")
            far_ident = sem5("far_ident")
            far_x_in = sem5("far_x_in")
            far_x_out = sem5("far_x_out")
            far_mask = sem5("far_mask")
            far_turned = sem5("far_turned")
            far_max = sem5("far_max")
            far_exp = sem5("far_exp")
            far_pT_psum = sem5("far_pT_psum")
            far_pT = sem5("far_pT")
            far_sum = sem5("far_sum")
            far_rows = sem5("far_rows")
            far_done = sem5("far_done")
            far_chain = sem5("far_chain")
            x_back = sem5("x_back")
            FC = 8
            ps_all = ps[:, :, :].rearrange("p k c -> p (k c)")
            block = c5.enter_context(nc.Block())

            def is_far(eng):
                return eng.value_load(far[0:1, 0:1], min_val=0, max_val=1)

            def x_rows(t, r):
                return t.rearrange("(b p) d -> b p d", p=P)[bass.ds(r, 1), :, :].rearrange("o p d -> p (o d)")

            @block.sync
            def _(sp):
                with sp.If(is_far(sp) > 0):
                    sp.dma_start(h_all[:, :, :], h_d.rearrange("(b p) d -> p b d", p=P)).then_inc(far_in, 16)
                    sp.dma_start(b_bc, a_flat[N:2 * N].partition_broadcast(P)).then_inc(far_in, 16)
                    with sp.Fori(0, NB) as r:
                        sp.wait_ge(far_done, r + 1)
                        sp.dma_start(num[:, 0, 0:D], x_rows(x2_d, r)).then_inc(far_x_in, 16)
                        sp.wait_ge(far_rows, r + 1)
                        sp.dma_start(x_rows(x3_d, r), num[:, 1, 0:D]).then_inc(far_x_out, 16)
                    sp.wait_ge(far_x_out, NB * 16)
                sp.dma_start(X[:, :, :], x3_d.rearrange("(b p) d -> p b d", p=P)).then_inc(x_back, 16)
                sp.wait_ge(x_back, 16)

            @block.scalar
            def _(act):
                with act.If(is_far(act) > 0):
                    with act.Fori(0, NG) as g:
                        for b in range(GB):
                            r = g * GB + b
                            act.wait_ge(far_done, r + 1)
                            m = mask_v[:, bass.ds(g, 1), :, b * P:(b + 1) * P].rearrange("p o j i -> p (o j) i")
                            act.activation(far_m.rearrange("p (j i) -> p j i", j=NB), m, ACT.Copy).then_inc(
                                far_mask, 1)
                            act.wait_ge(far_max, r + 1)
                            act.activation(score, score, ACT.Exp, bias=dn[:, 0, 0:1]).then_inc(far_exp, 1)
                            act.wait_ge(far_pT_psum, r + 1)
                            act.activation(prob_T, ps_all, ACT.Copy).then_inc(far_pT, 1)

            @block.tensor
            def _(pe):
                with pe.If(is_far(pe) > 0):
                    pe.wait_ge(far_ident, 1)
                    pe.wait_ge(far_in, 32)
                    with pe.Fori(0, NB) as r:
                        pe.wait_ge(far_mask, r + 1)
                        for j in range(NB):
                            last = pe.matmul(ps_all[:, j * P:(j + 1) * P], far_m[:, j * P:(j + 1) * P],
                                             ident_bf[:, :], start=True, stop=True)
                        last.then_inc(far_turned, 1)
                        pe.wait_ge(far_exp, r + 1)
                        for j in range(NB):
                            last = pe.transpose(ps_all[:, j * P:(j + 1) * P], score[:, j * P:(j + 1) * P], ident[:, :])
                        last.then_inc(far_pT_psum, 1)
                        pe.wait_ge(far_pT, r + 1)
                        for j in range(NB):
                            last = pe.matmul(ps[:, 0, 0:D], prob_T[:, j * P:(j + 1) * P], h_all[:, j, :],
                                             start=(j == 0), stop=(j == NB - 1))
                        last.then_inc(far_sum, 1)

            @block.vector
            def _(dve):
                with dve.If(is_far(dve) > 0):
                    dve.tensor_copy(ident_bf[:, :], ident[:, :]).then_inc(far_ident, 1)
                    dve.memset(marks[:, 12:13], 0.0).then_inc(far_done, 1)
                    dve.wait_ge(far_in, 32)
                    with dve.Fori(0, NB) as r:
                        lk = Chain(dve, far_chain, r * FC)
                        dve.wait_ge(far_done, r + 1)
                        lk.link(dve.tensor_scalar(score, b_bc, ab[:, 0, bass.ds(r, 1)], None, ALU.add))
                        lk.link(dve.scalar_tensor_tensor(score, score, SLOPE1, score, ALU.mult, ALU.max))
                        dve.wait_ge(far_turned, r + 1)
                        lk.link(dve.tensor_scalar(pen, ps_all, BIG, -BIG, ALU.mult, ALU.add))
                        lk.link(dve.tensor_tensor(score, score, pen, ALU.add))
                        lk.link(dve.tensor_reduce(dn[:, 1, 0:1], score, AX_X, ALU.max))
                        dve.tensor_scalar(dn[:, 0, 0:1], dn[:, 1, 0:1], -1.0, None, ALU.mult).then_inc(far_max, 1)
                        dve.wait_ge(far_exp, r + 1)
                        lk.link(dve.tensor_reduce(dn[:, 2, 0:1], score, AX_X, ALU.add))
                        lk.link(dve.reciprocal(dn[:, 3, 0:1], dn[:, 2, 0:1]))
                        dve.wait_ge(far_sum, r + 1)
                        lk.link(dve.tensor_scalar(num[:, 1, 0:D], ps[:, 0, 0:D], dn[:, 3, 0:1], None, ALU.mult))
                        dve.wait_ge(far_x_in, (r + 1) * 16)
                        dve.tensor_tensor(num[:, 1, 0:D], num[:, 1, 0:D], num[:, 0, 0:D],
                                          ALU.add).then_inc(far_rows, 1)
                        assert lk.n == FC, lk.n
                        dve.wait_ge(far_x_out, (r + 1) * 16)
                        dve.memset(marks[:, 13:14], 0.0).then_inc(far_done, 1)
        if stop_after <= 3:
            return dump()

        NE = 16
        HID = 256
        K = 2
        KB = K * NB
        TILES = K * N // P + NE
        ROUNDS = TILES // NG
        at = [0]

        def m(shape, dt, size):
            n = size
            for x_ in shape:
                n *= x_
            v_ = view(mask, at[0], shape, dt, size)
            at[0] += (n + 63) // 64 * 64
            assert at[0] <= mask_bytes
            return v_

        w12 = m([NE, 2 * HID], F32, 4)
        w3_s = m([NE, 2, D], F32, 4)
        back_rows = m([K, NB, D], F32, 4)
        Y = view(work, 0, [NB, D], F32, 4)
        yT = m([2, GR], F32, 4)
        gw = m([NE], F32, 4)
        gb = m([NE], F32, 4)
        logit = m([NB, NE], F32, 4)
        top = m([NB, 8], F32, 4)
        top_i = m([NB, 8], U32, 4)
        idx = m([K, NB], F32, 4)
        pw = m([K, NB], F32, 4)
        iota_e = m([NE], F32, 4)
        iota_t = m([TILES], F32, 4)
        before = m([P], BF16, 2)
        hot = m([K, NB, NE], BF16, 2)
        tot = m([NE, KB], F32, 4)
        cum = m([NE, KB], F32, 4)
        one_row = m([NE * KB], F32, 4)
        n_e = m([NE], F32, 4)
        n_i = m([NE], I32, 4)
        t_e = m([NE], F32, 4)
        t_s = m([NE], F32, 4)
        off_e = m([NE], F32, 4)
        place = m([K, NB, NE], F32, 4)
        slot_f = m([K, NB], F32, 4)
        slot = m([KB], U32, 4)
        cmp_t = m([TILES, NE], F32, 4)
        eid_f = m([TILES], F32, 4)
        eid = m([TILES], I32, 4)
        xs = view(work, 16384, [2, 4, D], F32, 4)
        xT_s = m([2, P], F32, 4)
        sil = m([2, HID], F32, 4)
        hid = m([2, HID], F32, 4)
        hidT = m([2, 2, P], F32, 4)
        o_s = view(work, 16384 + 4096, [2, 4, D], F32, 4)
        with ExitStack() as c6:
            def sem6(name):
                return c6.enter_context(nc.semaphore(name))

            dchain = sem6("e_dchain")
            gate_in = sem6("gate_in")
            pchain = sem6("pchain")
            before_ok = sem6("before_ok")
            iota_ok = sem6("iota_ok")
            y_ready = sem6("y_ready")
            yT_psum = sem6("yT_psum")
            yT_ready = sem6("yT_ready")
            logit_psum = sem6("logit_psum")
            gap_ready = sem6("gap_ready")
            ratio = sem6("ratio")
            hot_ready = sem6("hot_ready")
            rank_psum = sem6("rank_psum")
            slot_ready = sem6("slot_ready")
            scattered = sem6("scattered")
            w_in6 = sem6("w_in6")
            block = c6.enter_context(nc.Block())

            @block.sync
            def _(sp):
                sp.dma_start(gw, gate_w).then_inc(gate_in, 16)
                sp.dma_start(gb, gate_b.partition_broadcast(P)).then_inc(gate_in, 16)
                sp.dma_start(w12[:, :, 0:HID], w1.rearrange("e d h -> d e h")).then_inc(w_in6, 16)
                sp.dma_start(w12[:, :, HID:2 * HID], w2.rearrange("e d h -> d e h")).then_inc(w_in6, 16)
                sp.dma_start(w3_s, w3.rearrange("e (c p) o -> p e c o", p=P)).then_inc(w_in6, 16)
                sp.wait_ge(w_in6, 48)

            @block.gpsimd
            def _(pool):
                pool.iota(iota_e, pattern=[[1, NE]], base=0, channel_multiplier=0,
                          allow_small_or_imprecise_dtypes=True).then_inc(iota_ok, 1)
                pool.iota(iota_t, pattern=[[1, TILES]], base=0, channel_multiplier=0,
                          allow_small_or_imprecise_dtypes=True).then_inc(iota_ok, 1)
                pool.memset(before, 1.0).then_inc(pchain, 1)
                pool.wait_ge(pchain, 1)
                pool.affine_select(out=before, in_=before, compare_op=ALU.is_gt, fill=0.0, base=0,
                                   pattern=[[1, P]], channel_multiplier=-1).then_inc(before_ok, 1)
                pool.wait_ge(slot_ready, 1)
                for k in range(K):
                    for b in range(NB):
                        pool.indirect_dma_start(
                            out=xs_d, out_offset=bass.IndirectOffsetOnAxis(
                                ap=slot[:, k * NB + b:k * NB + b + 1], axis=0),
                            in_=Y[:, b, :], in_offset=None).then_inc(scattered, 16)
                pool.wait_ge(scattered, KB * 16)

            @block.tensor
            def _(pe):
                pe.wait_ge(gate_in, 32)
                for g in range(NG):
                    pe.wait_ge(y_ready, g + 1)
                    if g >= 2:
                        pe.wait_ge(yT_ready, g - 1)
                    for b in range(GB):
                        last = pe.transpose(ps[:, g % 2, b * P:(b + 1) * P], Y[:, g * GB + b, :], ident[:, :])
                    last.then_inc(yT_psum, 1)
                    pe.wait_ge(yT_ready, g + 1)
                    for b in range(GB):
                        k = g * GB + b
                        last = pe.matmul(ps[:, 2, k * NE:(k + 1) * NE], yT[:, g % 2, b * P:(b + 1) * P], gw,
                                         start=True, stop=True)
                    last.then_inc(logit_psum, 1)
                pe.wait_ge(before_ok, 1)
                for k in range(K):
                    pe.wait_ge(hot_ready, k + 1)
                    h_k = hot[:, k, :, :].rearrange("p b e -> p (b e)")
                    pe.matmul(ps[:, 4 + k, :], before, h_k, start=True, stop=True)
                    pe.matmul(ps[:, 6 + k, :], ones_bf[:, :], h_k, start=True, stop=True).then_inc(rank_psum, 1)

            @block.scalar
            def _(act):
                for g in range(NG):
                    act.wait_ge(yT_psum, g + 1)
                    if g >= 2:
                        act.wait_ge(logit_psum, g - 1)
                    act.activation(yT[:, g % 2, :], ps[:, g % 2, :], ACT.Copy).then_inc(yT_ready, 1)
                act.wait_ge(gap_ready, 1)
                act.activation(pw[:, 1, :], pw[:, 1, :], ACT.Exp).then_inc(ratio, 1)

            @block.vector
            def _(dve):
                ch = Chain(dve, dchain)
                ch.add(dve.memset(one_row, 1.0))
                for b in range(NB):
                    ch.add(dve.bn_stats(st6[:, b, :], X[:, b, :]))
                ch.done()
                for b in range(NB):
                    ch.add(dve.bn_aggr(mv[:, b, :], st6[:, b, :]))
                ch.done()
                ch.link(dve.tensor_scalar(v_col, mv[:, :, 1], EPS, None, ALU.add))
                emit_rsqrt(dve, ch.link, v_col, y_col, t_col, u_col, 2)
                for b in range(NB):
                    ins = dve.tensor_scalar(Y[:, b, :], X[:, b, :], mv[:, b, 0:1], y_col[:, b:b + 1],
                                            ALU.subtract, ALU.mult)
                    if b % GB == GB - 1:
                        ins.then_inc(y_ready, 1)
                dve.wait_ge(logit_psum, NG)
                ch.link(dve.tensor_tensor(logit, ps[:, 2, :].rearrange("p (b e) -> p b e", e=NE),
                                          gb.unsqueeze(1).broadcast_to([P, NB, NE]), ALU.add))
                for b in range(NB):
                    ch.add(dve.max(top[:, b, :], logit[:, b, :]))
                ch.done()
                for b in range(NB):
                    ch.add(dve.max_index(top_i[:, b, :], top[:, b, :], logit[:, b, :]))
                dve.tensor_tensor(pw[:, 1, :], top[:, :, 1], top[:, :, 0], ALU.subtract).then_inc(gap_ready, 1)
                ch.done()
                ch.link(dve.tensor_copy(idx, top_i[:, :, 0:K].rearrange("p b k -> p k b")))
                dve.wait_ge(iota_ok, 2)
                for k in range(K):
                    dve.tensor_tensor(hot[:, k, :, :], idx[:, k, :].unsqueeze(2).broadcast_to([P, NB, NE]),
                                      iota_e.unsqueeze(1).broadcast_to([P, NB, NE]), ALU.is_equal).then_inc(hot_ready, 1)
                dve.wait_ge(ratio, 1)
                ch.link(dve.tensor_scalar(v_col, pw[:, 1, :], 1.0, None, ALU.add))
                ch.link(dve.reciprocal(pw[:, 0, :], v_col))
                ch.link(dve.tensor_tensor(pw[:, 1, :], pw[:, 1, :], pw[:, 0, :], ALU.mult))
                dve.wait_ge(rank_psum, K)
                for k in range(K):
                    ch.add(dve.tensor_copy(tot[:, :, k * NB:(k + 1) * NB],
                                           ps[:, 6 + k, :].rearrange("p (b e) -> p e b", e=NE)))
                ch.done()
                ch.link(dve.tensor_reduce(n_e, tot, AX_X, ALU.add))
                ch.link(dve.tensor_scalar(n_i, n_e, float(P - 1), None, ALU.add))
                ch.link(dve.tensor_scalar(n_i, n_i, 7, None, ALU.logical_shift_right))
                ch.link(dve.tensor_copy(t_e, n_i))
                ch.link(dve.tensor_tensor_scan(t_s, one_row[:, 0:NE], t_e, 0.0, ALU.mult, ALU.add))
                ch.link(dve.tensor_tensor(t_s, t_s, t_e, ALU.subtract))
                flat = lambda v_: v_.rearrange("p e k -> p (e k)")
                ch.link(dve.tensor_tensor_scan(flat(cum), one_row, flat(tot), 0.0, ALU.mult, ALU.add))
                ch.link(dve.tensor_tensor(cum, cum, tot, ALU.subtract))
                ch.link(dve.scalar_tensor_tensor(off_e, t_s, float(P), cum[:, :, 0], ALU.mult, ALU.subtract))
                ch.link(dve.tensor_tensor(cum, cum, off_e.unsqueeze(2).broadcast_to([P, NE, KB]), ALU.add))
                for k in range(K):
                    ch.add(dve.tensor_tensor(place[:, k, :, :], ps[:, 4 + k, :].rearrange("p (b e) -> p b e", e=NE),
                                             cum[:, :, k * NB:(k + 1) * NB].rearrange("p e b -> p b e"), ALU.add))
                ch.done()
                ch.link(dve.tensor_tensor(place, place, hot, ALU.mult))
                ch.link(dve.tensor_reduce(slot_f, place, AX_X, ALU.add))
                dve.tensor_copy(slot, slot_f.rearrange("p k b -> p (k b)")).then_inc(slot_ready, 1)
                ch.link(dve.tensor_tensor(cmp_t, t_s.unsqueeze(1).broadcast_to([P, TILES, NE]),
                                          iota_t.unsqueeze(2).broadcast_to([P, TILES, NE]), ALU.is_le))
                ch.link(dve.tensor_reduce(eid_f, cmp_t, AX_X, ALU.add))
                ch.link(dve.tensor_scalar(eid, eid_f, -1.0, None, ALU.add))

        with ExitStack() as c7:
            def sem7(name):
                return c7.enter_context(nc.semaphore(name))

            xs_in = [sem7(f"xs_in{i}") for i in range(2)]
            ys_out = [sem7(f"ys_out{i}") for i in range(2)]
            xsT_psum = sem7("xsT_psum")
            xsT_ready = sem7("xsT_ready")
            up_psum = sem7("up_psum")
            sil_ready = sem7("sil_ready")
            hid_ready = sem7("hid_ready")
            hidT_psum = sem7("hidT_psum")
            hidT_ready = sem7("hidT_ready")
            o_psum = sem7("o_psum")
            o_ready = sem7("o_ready")
            block = c7.enter_context(nc.Block())

            @block.sync
            def _(sp):
                def load(c):
                    if c >= 2:
                        sp.wait_ge(xsT_psum, 4 * (c - 1))
                    sp.dma_start(xs[:, c % 2, :, :], xs_d[c * 4 * P:(c + 1) * 4 * P, :].rearrange(
                        "(t p) d -> p t d", p=P)).then_inc(xs_in[c % 2], 16)

                load(0)
                for c in range(TILES // 4):
                    if c + 1 < TILES // 4:
                        load(c + 1)
                    sp.wait_ge(o_ready, 4 * (c + 1))
                    sp.dma_start(ys_d[c * 4 * P:(c + 1) * 4 * P, :].rearrange("(t p) d -> p t d", p=P),
                                 o_s[:, c % 2, :, :]).then_inc(ys_out[c % 2], 16)
                for i in range(2):
                    sp.wait_ge(ys_out[i], TILES // 8 * 16)

            @block.tensor
            def _(pe):
                def expert(it, t):
                    tile = it * NG + t
                    src = eid[0:1, tile:tile + 1] if isinstance(tile, int) else eid[0:1, bass.ds(tile, 1)]
                    return pe.value_load(src, min_val=0, max_val=NE - 1)

                def turn(it, t):
                    pe.wait_ge(xs_in[t // 4], it * 16 + 16)
                    wait_use(pe, xsT_ready, it, t, 2)
                    pe.transpose(ps[:, t % 2, 0:P], xs[:, t // 4, t % 4, :], ident[:, :]).then_inc(xsT_psum, 1)

                def up(it, t):
                    e = expert(it, t)
                    pe.wait_ge(xsT_ready, it * NG + t + 1)
                    wait_use(pe, hid_ready, it, t, 2)
                    pe.matmul(ps[:, 2 + t % 2, :], xT_s[:, t % 2, :],
                              w12[:, bass.ds(e, 1), :].rearrange("p o n -> p (o n)"),
                              start=True, stop=True).then_inc(up_psum, 1)

                def turn_hidden(it, t):
                    pe.wait_ge(hid_ready, it * NG + t + 1)
                    wait_use(pe, hidT_ready, it, t, 2)
                    for c in range(2):
                        last = pe.transpose(ps[:, 4 + t % 2, c * P:(c + 1) * P], hid[:, t % 2, c * P:(c + 1) * P],
                                            ident[:, :])
                    last.then_inc(hidT_psum, 1)

                def down(it, t):
                    e = expert(it, t)
                    pe.wait_ge(hidT_ready, it * NG + t + 1)
                    wait_use(pe, o_ready, it, t, 2)
                    for c in range(2):
                        last = pe.matmul(ps[:, 6 + t % 2, 0:D], hidT[:, t % 2, c, :],
                                         w3_s[:, bass.ds(e, 1), c, :].rearrange("p o n -> p (o n)"),
                                         start=(c == 0), stop=(c == 1))
                    last.then_inc(o_psum, 1)

                def step(it, t, first=False, last=False):
                    if not last:
                        turn(it, t)
                    if not (first and t < 1) and not (last and t >= 1):
                        up(*back(it, t, 1))
                    if not (first and t < 2) and not (last and t >= 2):
                        turn_hidden(*back(it, t, 2))
                    if not (first and t < 3):
                        down(*back(it, t, 3))

                run(pe, step, ROUNDS)

            @block.scalar
            def _(act):
                def take_x(it, t):
                    act.wait_ge(xsT_psum, it * NG + t + 1)
                    wait_use(act, up_psum, it, t, 2)
                    act.activation(xT_s[:, t % 2, :], ps[:, t % 2, 0:P], ACT.Copy).then_inc(xsT_ready, 1)

                def silu(it, t):
                    act.wait_ge(up_psum, it * NG + t + 1)
                    wait_use(act, hid_ready, it, t, 2)
                    act.activation(sil[:, t % 2, :], ps[:, 2 + t % 2, 0:HID], ACT.Silu).then_inc(sil_ready, 1)

                def take_out(it, t):
                    act.wait_ge(o_psum, it * NG + t + 1)
                    if t % 4 == 0 and not (isinstance(it, int) and it == 0):
                        act.wait_ge(ys_out[t // 4], it * 16)
                    act.activation(o_s[:, t // 4, t % 4, :], ps[:, 6 + t % 2, 0:D], ACT.Copy).then_inc(o_ready, 1)

                def step(it, t, first=False, last=False):
                    if not last:
                        take_x(it, t)
                    if not (first and t < 1) and not (last and t >= 1):
                        silu(*back(it, t, 1))
                    if not (first and t < 3):
                        take_out(*back(it, t, 3))

                run(act, step, ROUNDS)

            @block.vector
            def _(dve):
                def gate(it, t):
                    dve.wait_ge(sil_ready, it * NG + t + 1)
                    wait_use(dve, hidT_psum, it, t, 2)
                    dve.tensor_tensor(hid[:, t % 2, :], sil[:, t % 2, :], ps[:, 2 + t % 2, HID:2 * HID],
                                      ALU.mult).then_inc(hid_ready, 1)

                def take_hidden(it, t):
                    dve.wait_ge(hidT_psum, it * NG + t + 1)
                    wait_use(dve, o_psum, it, t, 2)
                    dve.tensor_copy(hidT[:, t % 2, :, :], ps[:, 4 + t % 2, 0:HID].rearrange(
                        "p (c i) -> p c i", c=2)).then_inc(hidT_ready, 1)

                def step(it, t, first=False, last=False):
                    if not (first and t < 1) and not (last and t >= 1):
                        gate(*back(it, t, 1))
                    if not (first and t < 2) and not (last and t >= 2):
                        take_hidden(*back(it, t, 2))

                run(dve, step, ROUNDS)

        with ExitStack() as c8:
            def sem8(name):
                return c8.enter_context(nc.semaphore(name))

            gathered = [sem8(f"gathered{i}") for i in range(NG)]
            summed = sem8("summed")
            first_sum = sem8("first_sum")
            out_done = sem8("out_done")
            block = c8.enter_context(nc.Block())

            @block.gpsimd
            def _(pool):
                for b in range(NB):
                    for k in range(K):
                        pool.indirect_dma_start(
                            out=back_rows[:, k, b, :], out_offset=None, in_=ys_d,
                            in_offset=bass.IndirectOffsetOnAxis(ap=slot[:, k * NB + b:k * NB + b + 1],
                                                                axis=0)).then_inc(gathered[b // GB], 16)

            @block.vector
            def _(dve):
                for g in range(NG):
                    dve.wait_ge(gathered[g], 16 * GB * K)
                    for k in range(K):
                        if k == 1:
                            dve.wait_ge(first_sum, g + 1)
                        for b in range(g * GB, (g + 1) * GB):
                            last = dve.scalar_tensor_tensor(X[:, b, :], back_rows[:, k, b, :], pw[:, k, b:b + 1],
                                                            X[:, b, :], ALU.mult, ALU.add)
                        last.then_inc(first_sum if k == 0 else summed, 1)

            @block.sync
            def _(sp):
                for g in range(NG):
                    sp.wait_ge(summed, g + 1)
                    sp.dma_start(out[g * GR:(g + 1) * GR, :].rearrange("(b p) d -> p b d", p=P),
                                 X[:, g * GB:(g + 1) * GB, :]).then_inc(out_done, 16)
                sp.wait_ge(out_done, 16 * NG)

_INS = ["x", "adj", "L0_gnn_Wq", "L0_gnn_Wk", "L0_gnn_Wv", "L0_gnn_a", "L0_ffn_ln_w", "L0_ffn_ln_b", "L0_ffn_W",
        "L0_ffn_b", "L1_gnn_a", "L1_ffn_gate_w", "L1_ffn_gate_b", "L1_ffn_w1", "L1_ffn_w2", "L1_ffn_w3"]


def build(nc, inputs, stop_after=9):
    import numpy as _np
    from concourse import mybir as _mybir

    arrays, args = {}, []
    for name in _INS:
        a = _np.asarray(inputs[name])
        if name == "adj":
            a = a.reshape(NG, GR, NT, JT, P).transpose(0, 2, 4, 3, 1).reshape(NG, NT, P, JT * GR)
        if name in ("L0_gnn_a", "L1_gnn_a"):
            a = a.reshape(2, D).T
        a = _np.ascontiguousarray(a)
        arrays[f"in_{name}_dram"] = a
        args.append(nc.dram_tensor(f"in_{name}_dram", a.shape, _mybir.dt.from_np(a.dtype), kind="ExternalInput").ap())
    out = nc.dram_tensor("out_0_dram", (N, D), _mybir.dt.float32, kind="ExternalOutput").ap()
    network(nc, *args, out, stop_after=stop_after)
    return arrays


def kernel(**inputs):
    import concourse.bacc as _bacc
    from concourse.bass_utils import run_bass_kernel_spmd as _run

    nc = _bacc.Bacc("TRN2", target_bir_lowering=False, num_devices=1)
    arrays = build(nc, inputs)
    r = _run(nc, [arrays], core_ids=[0])
    return r.results[0]["out_0_dram"]
```

```python
from contextlib import ExitStack

import concourse.bass as bass
from concourse import mybir

ALU = mybir.AluOpType
ACT = mybir.ActivationFunctionType
AX_X = mybir.AxisListType.X
F32 = mybir.dt.float32
BF16 = mybir.dt.bfloat16
I32 = mybir.dt.int32
U32 = mybir.dt.uint32
U8 = mybir.dt.uint8
I8 = mybir.dt.int8

P = 128
N = 4096
D = 128
NB = N // P
GB = 4
NG = NB // GB
GR = GB * P
JT = 2
NT = NB // JT
ITERS = 30
EPS = 1e-5
NEG = -1000.0
SLOPE0 = 0.01
SLOPE1 = 0.2
NPART = 3
VW = NPART * D + 1

RSQRT_MAGIC = float(0x5F1FFFF9)
RSQRT_K = 0.703952253
RSQRT_C = 2.38924456


class Chain:

    def __init__(self, eng, sem, base=0):
        self.eng, self.sem, self.base, self.n = eng, sem, base, 0

    def add(self, ins):
        self.n += 1
        ins.then_inc(self.sem, 1)

    def done(self):
        self.eng.wait_ge(self.sem, self.base + self.n)

    def link(self, ins):
        self.add(ins)
        self.done()


def rsqrt_start(v, y):
    return dict(out=y.bitcast(I32), in0=v.bitcast(I32), scalar1=-0.5, scalar2=RSQRT_MAGIC,
                op0=ALU.mult, op1=ALU.add)


def back(it, g, lag, per=NG):
    return (it, g - lag) if g >= lag else (it - 1, g - lag + per)


def wait_use(eng, sem, it, g, slots, base=0, per=NG):
    if isinstance(it, int) and it == 0 and g < slots:
        return
    eng.wait_ge(sem, it * per + (base + g + 1 - slots))


def run(eng, step, rounds, per=NG, lag=3):
    for g in range(per):
        step(0, g, first=True)
    with eng.Fori(1, rounds) as it:
        for g in range(per):
            step(it, g)
    for g in range(lag):
        step(rounds, g, last=True)


def emit_rsqrt(dve, link, v, y, t, u, newton):
    link(dve.tensor_scalar(**rsqrt_start(v, y)))
    for step in range(newton + 1):
        k, c = (RSQRT_K, RSQRT_K * RSQRT_C) if step == 0 else (0.5, 1.5)
        link(dve.tensor_tensor(t, y, y, ALU.mult))
        link(dve.scalar_tensor_tensor(u, t, -k, v, ALU.mult, ALU.mult))
        link(dve.scalar_tensor_tensor(y, u, c, y, ALU.add, ALU.mult))


def network(nc, x, adj_t, wq, wk, wv, a0, ln_w, ln_b, wf, bf, a1, gate_w, gate_b, w1, w2, w3, out):
    with ExitStack() as ctx:
        def sb(name, shape, dt):
            return ctx.enter_context(nc.sbuf_tensor(name, shape, dt))

        mask_bytes = NG * NB * GR
        mask = sb("mask", [P, mask_bytes], U8)
        mask_v = mask[:, :].bitcast(I8).rearrange("p (g j i) -> p g j i", g=NG, j=NB)
        X = sb("X", [P, NB, D], F32)
        WORK = 51200
        work = sb("work", [P, WORK], U8)
        ps = ctx.enter_context(nc.psum_tensor("ps", [P, 8, 512], F32))

        def view(region, at, shape, dt, size):
            n = 1
            for s in shape:
                n *= s
            names = "abcd"[:len(shape)]
            flat = region[:, at:at + n * size].bitcast(dt)
            if len(shape) == 1:
                return flat
            return flat.rearrange(f"p ({' '.join(names)}) -> p {' '.join(names)}",
                                  **{names[i]: shape[i] for i in range(len(shape) - 1)})

        ident = sb("ident", [P, P], F32)
        ones = sb("ones", [P, P], F32)
        marks = sb("marks", [P, 16], F32)
        ones_bf = sb("ones_bf", [P, P], BF16)
        st6 = sb("st6", [P, NB, 6], F32)
        mv = sb("mv", [P, NB, 2], F32)
        col = sb("col", [P, 5, NB], F32)
        wz = sb("wz", [P, D], F32)
        wst = sb("wst", [P, D + 1], F32)
        c_col = sb("c_col", [P, 1], F32)
        c_nat = sb("c_nat", [P, D], F32)
        total = sb("total", [P, D], F32)

        v_col, y_col, t_col, u_col, s_col = (col[:, i, :] for i in range(5))

        split = view(work, 0, [NB, VW], BF16, 2)
        stage_at = (NB * VW * 2 + 63) // 64 * 64
        NS = 4
        stage = view(work, stage_at, [NS, JT, GR], I32, 4)
        NCONN = 2
        conn = sb("conn", [P, NCONN, JT, GR], BF16)
        xln = view(mask, 6 * NB * GR, [NB, D], F32, 4)
        xT = view(mask, 7 * NB * GR, [NB, D], F32, 4)
        rest = view(mask, 5 * NB * GR, [2, GB, D], F32, 4)
        w_in = view(mask, 4 * NB * GR, [8, D], F32, 4)
        sums = view(work, stage_at + NS * JT * GR * 4, [GB, D], F32, 4)
        sm = ctx.enter_context(nc.sbuf_tensor("small", [P, 12, 2, GB], F32))

        with ExitStack() as c1:
            def sem1(name):
                return c1.enter_context(nc.semaphore(name))

            x_in = sem1("x_in")
            weights_in = sem1("weights_in")
            landed = [sem1(f"landed{i}") for i in range(NS)]
            stage_free = sem1("stage_free")
            conn_ready = sem1("conn_ready")
            conn_free = sem1("conn_free")
            zeroed = sem1("zeroed")
            ident_ok = sem1("ident_ok")
            dchain = sem1("dchain")
            xln_ready = sem1("xln_ready")
            xT_psum = sem1("xT_psum")
            xT_ready = sem1("xT_ready")
            weights_psum = sem1("weights_psum")
            weights_ready = sem1("weights_ready")
            val_psum = sem1("val_psum")
            part1 = sem1("part1")
            split_ready = sem1("split_ready")
            total_psum = sem1("total_psum")
            sums_free = sem1("sums_free")
            ffn_folded = sem1("ffn_folded")
            exp_in = sem1("exp_in")
            exp_out = sem1("exp_out")

            finish_chain = sem1("finish_chain")
            stats = sem1("row_stats")
            PARTS = (2, 3, 3, 2, 1, 1, 1, 3, 1, 1, 1, 2, 4, 4)
            FINISH = sum(PARTS)
            cnt, sc, sc2, mx, ncnt, w1c, w0c, al, be = (sm[:, i // 2, i % 2, :] for i in range(9))
            ind, t1, t2, ex = (sm[:, 6 + i, :, :] for i in range(4))

            def mask_at(g, c):
                return mask_v[:, bass.ds(g, 1), c * JT:(c + 1) * JT, :].rearrange("p o j i -> p (o j) i")

            block = c1.enter_context(nc.Block())
            wq_s, wk_s, wv_s, wf_s, lnw_s, lnb_s, wtmp, wtmp2 = (w_in[:, i, :] for i in range(8))
            a_col = view(mask, 4 * NB * GR + 8 * D * 4, [8], F32, 4)

            @block.sync
            def _(sp):
                sp.dma_start(X[:, :, :], x.rearrange("(b p) d -> p b d", p=P)).then_inc(x_in, 16)
                for dst, src in ((wq_s, wq), (wk_s, wk), (wv_s, wv), (wf_s, wf),
                                 (lnw_s, ln_w.partition_broadcast(P)),
                                 (lnb_s, ln_b.partition_broadcast(P)),
                                 (a_col[:, 0:2], a0),
                                 (a_col[:, 2:3], bf.rearrange("(p o) -> p o", o=1))):
                    sp.dma_start(dst, src).then_inc(weights_in, 16)
                with sp.Fori(0, NG) as g:
                    for c in range(NT):
                        sp.wait_ge(stage_free, g * NT + c + 1)
                        sp.dma_start(stage[:, c % NS, :, :], adj_t[bass.ds(g, 1), c, :, :].rearrange(
                            "o p (j i) -> p (o j) i", j=JT)).then_inc(landed[c % NS], 16)

            @block.gpsimd
            def _(pool):
                pool.memset(ident[:, :], 0.0).then_inc(zeroed, 1)
                pool.wait_ge(zeroed, 1)
                pool.affine_select(out=ident[:, :], in_=ident[:, :], compare_op=ALU.not_equal, fill=1.0,
                                   base=0, pattern=[[-1, P]], channel_multiplier=1).then_inc(ident_ok, 1)

            @block.scalar
            def _(act):
                act.wait_ge(weights_psum, 1)
                act.activation(wst[:, 0:D], ps[:, 7, 0:D], ACT.Copy).then_inc(weights_ready, 1)
                act.activation(wst[:, D:D + 1], ps[:, 6, 0:1], ACT.Copy).then_inc(weights_ready, 1)
                act.wait_ge(weights_psum, 2)
                act.activation(wz[:, :], ps[:, 5, 128:256], ACT.Copy).then_inc(weights_ready, 1)
                act.activation(c_nat[:, :], ps[:, 5, 256:384], ACT.Copy).then_inc(weights_ready, 1)
                for g in range(NG):
                    act.wait_ge(xT_psum, g + 1)
                    act.activation(xT[:, g * GB:(g + 1) * GB, :],
                                   ps[:, g % 2, :].rearrange("p (b d) -> p b d", b=GB),
                                   ACT.Copy).then_inc(xT_ready, 1)
                    act.wait_ge(val_psum, g + 1)
                    vals = ps[:, 2 + 2 * (g % 2):4 + 2 * (g % 2), :].rearrange("p k (h c) -> p (k h) c", h=2)
                    act.activation(split[:, g * GB:(g + 1) * GB, 0:D], vals[:, :, 0:D],
                                   ACT.Copy).then_inc(part1, 1)

                def sign(g, c):
                    act.wait_ge(conn_ready, g * NT + c + 1)
                    act.activation(mask_at(g, c), stage[:, c % NS, :, :], ACT.Sign).then_inc(stage_free, 1)

                def weights(g):
                    act.wait_ge(exp_in, g + 1)
                    act.activation(ex, t1, ACT.Exp).then_inc(exp_out, 1)

                def body(gg, first=False):
                    for h in range(2):
                        for c in range(NT):
                            sign(2 * gg + h, c)
                            if c == 7 and not (first and h == 0):
                                weights(2 * gg + h - 1)

                body(0, first=True)
                with act.Fori(1, NG // 2) as gg:
                    body(gg)
                weights(NG - 1)

            @block.tensor
            def _(pe):
                pe.wait_ge(weights_in, 16 * 8)
                pe.wait_ge(ident_ok, 1)
                pe.transpose(ps[:, 7, 0:D], wv_s, ident[:, :])
                pe.matmul(ps[:, 6, 0:1], wq_s, a_col[:, 0:1], start=True, stop=False)
                pe.matmul(ps[:, 6, 0:1], wk_s, a_col[:, 1:2], start=False, stop=True).then_inc(weights_psum, 1)
                pe.wait_ge(ffn_folded, 1)
                pe.transpose(ps[:, 5, 128:256], wtmp, ident[:, :])
                pe.matmul(ps[:, 5, 256:384], c_col[:, 0:1].broadcast_to([P, P]), ident[:, :],
                          start=True, stop=True).then_inc(weights_psum, 1)
                for g in range(NG + 1):
                    if g < NG:
                        pe.wait_ge(xln_ready, g + 1)
                        if g >= 2:
                            pe.wait_ge(xT_ready, g - 1)
                        for b in range(GB):
                            last = pe.transpose(ps[:, g % 2, b * P:(b + 1) * P], xln[:, g * GB + b, :],
                                                ident[:, :])
                        last.then_inc(xT_psum, 1)
                    if g >= 1:
                        v = g - 1
                        pe.wait_ge(xT_ready, g)
                        if v == 0:
                            pe.wait_ge(weights_ready, 4)
                        if v >= 2:
                            pe.wait_ge(split_ready, v - 1)
                        for b in range(GB):
                            last = pe.matmul(ps[:, 2 + 2 * (v % 2) + b // 2, (b % 2) * 256:(b % 2) * 256 + D + 1],
                                             xT[:, v * GB + b, :], wst[:, :], start=True, stop=True)
                        last.then_inc(val_psum, 1)
                pe.wait_ge(split_ready, NG)

                def group(g, h):
                    pe.wait_ge(sums_free, g + 1)
                    for c in range(NT):
                        pe.wait_ge(conn_ready, g * NT + c + 1)
                        for j in range(JT):
                            for b in range(GB):
                                last = pe.matmul(ps[:, 4 * h + b, 0:VW], conn[:, c % NCONN, j, b * P:(b + 1) * P],
                                                 split[:, c * JT + j, :], start=(c + j == 0),
                                                 stop=(c == NT - 1 and j == JT - 1))
                        last.then_inc(conn_free, 1)

                group(0, 0)
                for b in range(NB):
                    last = pe.matmul(ps[:, 7, 0:VW], ones_bf[:, :], split[:, b, :],
                                     start=(b == 0), stop=(b == NB - 1))
                last.then_inc(total_psum, 1)
                group(1, 1)
                with pe.Fori(1, NG // 2) as gg:
                    for h in range(2):
                        group(2 * gg + h, h)

            @block.vector
            def _(dve):
                ch = Chain(dve, dchain)
                for i in range(NS):
                    dve.memset(marks[:, i:i + 1], 0.0).then_inc(stage_free, 1)
                for i in range(NCONN):
                    dve.memset(marks[:, 8 + i:9 + i], 0.0).then_inc(conn_free, 1)
                dve.memset(ones_bf[:, :], 1.0)
                dve.memset(ones[:, :], 1.0)
                ch.link(dve.memset(split[:, :, VW - 1:VW], 1.0))
                dve.wait_ge(weights_in, 16 * 8)
                ch.add(dve.tensor_tensor(wtmp2, wf_s, lnb_s, ALU.mult))
                ch.link(dve.tensor_tensor(wtmp, wf_s, lnw_s, ALU.mult))
                ch.add(dve.tensor_reduce(a_col[:, 3:4], wtmp2, AX_X, ALU.add))
                ch.link(dve.tensor_reduce(a_col[:, 4:5], wtmp, AX_X, ALU.add))
                ch.add(dve.tensor_scalar(a_col[:, 5:6], a_col[:, 4:5], 1.0 / D, None, ALU.mult))
                ch.link(dve.tensor_tensor(c_col[:, :], a_col[:, 3:4], a_col[:, 2:3], ALU.add))
                dve.tensor_scalar(wtmp, wtmp, a_col[:, 5:6], None, ALU.subtract).then_inc(ffn_folded, 1)
                dve.wait_ge(x_in, 16)
                for b in range(NB):
                    ch.add(dve.bn_stats(st6[:, b, :], X[:, b, :]))
                ch.done()
                for b in range(NB):
                    ch.add(dve.bn_aggr(mv[:, b, :], st6[:, b, :]))
                ch.done()
                ch.link(dve.tensor_scalar(v_col, mv[:, :, 1], EPS, None, ALU.add))
                emit_rsqrt(dve, ch.link, v_col, y_col, t_col, u_col, 2)
                for b in range(NB):
                    ins = dve.tensor_scalar(xln[:, b, :], X[:, b, :], mv[:, b, 0:1], y_col[:, b:b + 1],
                                            ALU.subtract, ALU.mult)
                    if b % GB == GB - 1:
                        ins.then_inc(xln_ready, 1)
                for g in range(NG):
                    blocks = slice(g * GB, (g + 1) * GB)
                    vals = ps[:, 2 + 2 * (g % 2):4 + 2 * (g % 2), :].rearrange("p k (h c) -> p (k h) c", h=2)
                    dve.wait_ge(part1, g + 1)
                    ch.add(dve.tensor_copy(s_col[:, blocks], vals[:, :, D]))
                    ch.link(dve.tensor_tensor(rest[:, 0, :, :], vals[:, :, 0:D], split[:, blocks, 0:D], ALU.subtract))
                    ch.link(dve.tensor_copy(split[:, blocks, D:2 * D], rest[:, 0, :, :]))
                    ch.link(dve.tensor_tensor(rest[:, 1, :, :], rest[:, 0, :, :], split[:, blocks, D:2 * D],
                                              ALU.subtract))
                    dve.tensor_copy(split[:, blocks, 2 * D:3 * D], rest[:, 1, :, :]).then_inc(split_ready, 1)
                dve.wait_ge(split_ready, NG)
                dve.memset(marks[:, 10:11], 0.0).then_inc(sums_free, 1)

                def connected(g, c):
                    dve.wait_ge(landed[c % NS], (g * (NT // NS) + c // NS + 1) * 16)
                    dve.wait_ge(conn_free, g * NT + c + 1)
                    dve.tensor_scalar(conn[:, c % NCONN, :, :], stage[:, c % NS, :, :], 0.0, None,
                                      ALU.not_equal).then_inc(conn_ready, 1)

                def finish(g, h, i):
                    scored = s_col[:, bass.ds(g * GB, GB)]
                    lk = Chain(dve, finish_chain, g * FINISH + sum(PARTS[:i]))
                    if i == 0:
                        dve.wait_ge(conn_free, g * NT + NT + NCONN)
                    else:
                        lk.done()
                    if i in (0, 1):
                        for b in (2 * i, 2 * i + 1):
                            lk.add(dve.tensor_reduce(sums[:, b, :], ps[:, 4 * h + b, 0:3 * D].rearrange(
                                "p (t d) -> p d t", t=3), AX_X, ALU.add))
                    if i == 1:
                        lk.add(dve.tensor_copy(cnt, ps[:, 4 * h:4 * h + GB, VW - 1]))
                    if i == 2:
                        dve.memset(sm[:, 11, 0, 0:1], 0.0).then_inc(sums_free, 1)
                        lk.add(dve.tensor_scalar(sc2, scored, SLOPE0, None, ALU.mult))
                        lk.add(dve.tensor_scalar(ind[:, 0, :], cnt, 0.0, None, ALU.is_gt))
                        lk.add(dve.tensor_scalar(ind[:, 1, :], cnt, float(N), None, ALU.is_ge))
                    if i == 3:
                        lk.add(dve.tensor_tensor(sc, scored, sc2, ALU.max))
                        lk.add(dve.tensor_scalar(t2, ind, -NEG, NEG, ALU.mult, ALU.add))
                    if i == 4:
                        lk.add(dve.tensor_tensor(t1, ind, sc.unsqueeze(1).broadcast_to([P, 2, GB]), ALU.mult))
                    if i == 5:
                        lk.add(dve.tensor_tensor(t1, t1, t2, ALU.add))
                    if i == 6:
                        lk.add(dve.tensor_tensor(mx, t1[:, 0, :], t1[:, 1, :], ALU.max))
                        lk.done()
                        dve.tensor_tensor(t1, t1, mx.unsqueeze(1).broadcast_to([P, 2, GB]),
                                          ALU.subtract).then_inc(exp_in, 1)
                    if i == 7:
                        dve.wait_ge(exp_out, g + 1)
                        lk.add(dve.tensor_scalar(ncnt, cnt, -1.0, float(N), ALU.mult, ALU.add))
                        lk.add(dve.tensor_tensor(w1c, ex[:, 0, :], cnt, ALU.mult))
                        lk.add(dve.tensor_tensor(al, ex[:, 0, :], ex[:, 1, :], ALU.subtract))
                    if i == 8:
                        lk.add(dve.tensor_tensor(w0c, ex[:, 1, :], ncnt, ALU.mult))
                    if i == 9:
                        lk.add(dve.tensor_tensor(w1c, w1c, w0c, ALU.add))
                    if i == 10:
                        lk.add(dve.reciprocal(w1c, w1c))
                    if i == 11:
                        lk.add(dve.tensor_tensor(al, al, w1c, ALU.mult))
                        lk.add(dve.tensor_tensor(be, ex[:, 1, :], w1c, ALU.mult))
                    if i in (12, 13):
                        of, by = ((sums[:, b, :] for b in range(GB)), al) if i == 12 else ([total[:, :]] * GB, be)
                        for b, what in enumerate(of):
                            xb = X[:, bass.ds(g * GB + b, 1), :].rearrange("p o d -> p (o d)")
                            lk.add(dve.scalar_tensor_tensor(xb, what, by[:, b:b + 1], xb, ALU.mult, ALU.add))
                    assert lk.n == PARTS[i]

                def measure(g):
                    dve.wait_ge(finish_chain, (g + 1) * FINISH)
                    for b in range(GB):
                        dve.bn_stats(st6[:, bass.ds(g * GB + b, 1), :].rearrange("p o k -> p (o k)"),
                                     X[:, bass.ds(g * GB + b, 1), :].rearrange("p o d -> p (o d)")).then_inc(stats, 1)

                def body(gg, first=False):
                    for h in range(2):
                        for c in range(NT):
                            connected(2 * gg + h, c)
                            if first and h == 1 and c == 0:
                                dve.wait_ge(total_psum, 1)
                                ch.link(dve.tensor_reduce(total[:, :], ps[:, 7, 0:3 * D].rearrange(
                                    "p (t d) -> p d t", t=3), AX_X, ALU.add))
                                dve.memset(marks[:, 11:12], 0.0).then_inc(sums_free, 1)
                            if c == 0 and not first:
                                measure(2 * gg + h - 2)
                            part = c - 1 if c < 8 else c - 2
                            if part >= 0 and c != 8 and not (first and h == 0):
                                finish(2 * gg + h - 1, 1 - h, part)

                body(0, first=True)
                with dve.Fori(1, NG // 2) as gg:
                    body(gg)
                measure(NG - 2)
                for i in range(len(PARTS)):
                    finish(NG - 1, 1, i)
                measure(NG - 1)
                dve.wait_ge(stats, NB)

        UP = 100.0
        NP = NG // 2
        PB = 2 * GB
        NH = 2
        HB = NB // NH
        hN = view(work, 0, [NB, D], F32, 4)
        tN = view(work, 16384, [2, GB, D], F32, 4)
        sN, sT = (view(work, 20480 + i * 8192, [4, GB, D], F32, 4) for i in range(2))
        DW = D + 2
        FILL = 16
        SLOTS_E = 2 * N + 16 * P
        unused = view(work, 40960, [FILL, DW], F32, 4)
        xs_d = nc.dram_tensor("xs_d", (SLOTS_E, DW), F32, kind="Internal").ap()
        y_d = nc.dram_tensor("y_d", (2 * N + FILL * P, D), F32, kind="Internal").ap()
        with ExitStack() as c2:
            def sem2(name):
                return c2.enter_context(nc.semaphore(name))

            dchain = sem2("f_dchain")
            c_up = sem2("c_up")
            h_ready = sem2("h_ready")
            t_ready = sem2("t_ready")
            g_ready = sem2("g_ready")
            s_ready = sem2("s_ready")
            stats = sem2("stats")
            sT_psum = sem2("sT_psum")
            sT_ready = sem2("sT_ready")
            z_psum = sem2("z_psum")
            root_chain = sem2("root_chain")
            xc = sem2("xc")
            ROOT = 11
            zero_ok = sem2("zero_ok")
            zero_out = sem2("zero_out")
            fst = view(work, 36864, [NH, HB, 6], F32, 4)
            fs = view(work, 38400, [NH, 7, HB], F32, 4)
            c100 = view(work, 39936, [D], F32, 4)
            block = c2.enter_context(nc.Block())

            def rows(g):
                return slice(g * GB, (g + 1) * GB)

            @block.sync
            def _(sp):
                sp.wait_ge(zero_ok, 2)
                for i in range(SLOTS_E // (FILL * P)):
                    sp.dma_start(xs_d[i * FILL * P:(i + 1) * FILL * P, :].rearrange("(t p) d -> p t d", p=P),
                                 unused).then_inc(zero_out, 16)
                sp.wait_ge(zero_out, 16 * (SLOTS_E // (FILL * P)))

            @block.tensor
            def _(pe):
                def turn(it, g):
                    pe.wait_ge(s_ready, it * NG + g + 1)
                    wait_use(pe, sT_ready, it, g, 4)
                    for b in range(GB):
                        last = pe.transpose(ps[:, 4 + g % 4, b * P:(b + 1) * P], sN[:, g % 4, b, :], ident[:, :])
                    last.then_inc(sT_psum, 1)

                def product(it, g):
                    pe.wait_ge(sT_ready, it * NG + g + 1)
                    wait_use(pe, h_ready, it, g, 4, NG)
                    for b in range(GB):
                        last = pe.matmul(ps[:, g % 4, b * D:(b + 1) * D], sT[:, g % 4, b, :], wz[:, :],
                                         start=True, stop=True)
                    last.then_inc(z_psum, 1)

                def step(it, p, first=False, last=False):
                    for k in range(2):
                        if not (first and p < 1) and not (last and p >= 1):
                            it1, p1 = back(it, p, 1, NP)
                            turn(it1, 2 * p1 + k)
                    for k in range(2):
                        if not (first and p < 2):
                            it2, p2 = back(it, p, 2, NP)
                            product(it2, 2 * p2 + k)

                run(pe, step, ITERS, per=NP, lag=2)

            @block.scalar
            def _(act):
                def tanh(it, g):
                    act.wait_ge(h_ready, it * NG + g + 1)
                    wait_use(act, g_ready, it, g, 2)
                    act.activation(tN[:, g % 2, :, :], hN[:, rows(g), :], ACT.Tanh, scale=1.0 / UP).then_inc(
                        t_ready, 1)

                def silu(it, g):
                    act.wait_ge(g_ready, it * NG + g + 1)
                    wait_use(act, sT_psum, it, g, 4)
                    if not (isinstance(it, int) and it == 0 and g < 4):
                        act.wait_ge(stats, it * NB + (g - 3) * GB)
                    act.activation(sN[:, g % 4, :, :], hN[:, rows(g), :], ACT.Silu, scale=1.0 / UP).then_inc(
                        s_ready, 1)

                def take_turned(it, g):
                    act.wait_ge(sT_psum, it * NG + g + 1)
                    wait_use(act, z_psum, it, g, 4)
                    act.activation(sT[:, g % 4, :, :], ps[:, 4 + g % 4, :].rearrange("p (b i) -> p b i", b=GB),
                                   ACT.Copy).then_inc(sT_ready, 1)

                def step(it, p, first=False, last=False):
                    for k in range(2):
                        if not last:
                            tanh(it, 2 * p + k)
                    for k in range(2):
                        if not (first and p < 1):
                            it1, p1 = back(it, p, 1, NP)
                            take_turned(it1, 2 * p1 + k)
                    for k in range(2):
                        if not last:
                            silu(it, 2 * p + k)

                run(act, step, ITERS, per=NP, lag=1)

            @block.gpsimd
            def _(pool):
                pool.memset(unused, 0.0).then_inc(zero_ok, 1)
                pool.wait_ge(zero_ok, 1)
                pool.iota(unused[:, :, D:D + 1].bitcast(U32), pattern=[[P, FILL]], base=2 * N,
                          channel_multiplier=1).then_inc(zero_ok, 1)

                def sum_(it, g):
                    pool.wait_ge(t_ready, it * NG + g + 1)
                    pool.tensor_tensor(hN[:, rows(g), :], hN[:, rows(g), :], tN[:, g % 2, :, :],
                                       ALU.add).then_inc(g_ready, 1)

                for g in range(NG):
                    sum_(0, g)
                for g in range(NG):
                    pool.tensor_tensor(X[:, rows(g), :], X[:, rows(g), :],
                                       c_nat[:, :].unsqueeze(1).broadcast_to([P, GB, D]), ALU.add).then_inc(xc, 1)
                with pool.Fori(1, ITERS) as it:
                    for g in range(NG):
                        sum_(it, g)

            @block.vector
            def _(dve):
                ch = Chain(dve, dchain)
                dve.tensor_scalar(c100, c_nat[:, :], UP, None, ALU.mult).then_inc(c_up, 1)
                for b in range(NB):
                    ch.add(dve.bn_aggr(mv[:, b, :], st6[:, b, :]))
                ch.done()
                ch.link(dve.tensor_scalar(v_col, mv[:, :, 1], EPS, None, ALU.add))
                emit_rsqrt(dve, ch.link, v_col, y_col, t_col, u_col, 2)
                ch.link(dve.tensor_scalar(y_col, y_col, UP, None, ALU.mult))
                dve.wait_ge(c_up, 1)

                def normalise(g):
                    for b in range(g * GB, (g + 1) * GB):
                        last = dve.tensor_scalar(hN[:, b, :], X[:, b, :], mv[:, b, 0:1], y_col[:, b:b + 1],
                                                 ALU.subtract, ALU.mult)
                    last.then_inc(h_ready, 1)

                def affine(it, p, c):
                    g, b = 2 * p + c // GB, c % GB
                    it1 = it - 1
                    if c == 0:
                        dve.wait_ge(root_chain, it1 * (NH * ROOT) + (p // 2 + 1) * ROOT)
                    if b == 0:
                        dve.wait_ge(z_psum, it1 * NG + g + 1)
                    cc = (p % 2) * PB + c
                    y = fs[:, p // 2, 5, cc:cc + 1]
                    ins = dve.scalar_tensor_tensor(hN[:, g * GB + b, :], ps[:, g % 4, b * D:(b + 1) * D], y,
                                                   c100, ALU.mult, ALU.add)
                    if b == GB - 1:
                        ins.then_inc(h_ready, 1)

                def result(p, c):
                    g, b = 2 * p + c // GB, c % GB
                    cc = (p % 2) * PB + c
                    if cc == 0:
                        dve.wait_ge(root_chain, (ITERS - 1) * (NH * ROOT) + (p // 2 + 1) * ROOT)
                        ch.link(dve.tensor_scalar(fs[:, p // 2, 6, :], fs[:, p // 2, 5, :], 1.0 / UP, None, ALU.mult))
                        dve.wait_ge(xc, NG)
                    if b == 0:
                        dve.wait_ge(z_psum, (ITERS - 1) * NG + g + 1)
                    xb = X[:, g * GB + b, :]
                    ins = dve.scalar_tensor_tensor(xb, ps[:, g % 4, b * D:(b + 1) * D], fs[:, p // 2, 6, cc:cc + 1], xb,
                                                   ALU.mult, ALU.add)
                    if b == GB - 1:
                        ins.then_inc(h_ready, 1)

                def measure(it, p, c):
                    g, b = 2 * p + c // GB, c % GB
                    if b == 0:
                        dve.wait_ge(s_ready, it * NG + g + 1)
                    dve.bn_stats(fst[:, p // 2, (p % 2) * PB + c, :], sN[:, g % 4, b, :]).then_inc(stats, 1)

                def short(i, it, q):
                    d, dd, m2, v, t, y, u = (fs[:, q, k, :] for k in range(7))
                    st = fst[:, q, :, :]
                    if i == 0:
                        dve.wait_ge(stats, it * NB + (q + 1) * HB)
                    else:
                        dve.wait_ge(root_chain, it * (NH * ROOT) + (q * ROOT + i))
                    if i == 0:
                        ins = dve.tensor_tensor(d, st[:, :, 1], st[:, :, 4], ALU.subtract)
                    if i == 1:
                        ins = dve.scalar_tensor_tensor(m2, st[:, :, 2], D * EPS, st[:, :, 5], ALU.add, ALU.add)
                    if i == 2:
                        ins = dve.tensor_tensor(dd, d, d, ALU.mult)
                    if i == 3:
                        ins = dve.scalar_tensor_tensor(v, dd, D / 4, m2, ALU.mult, ALU.add)
                    if i == 4:
                        ins = dve.tensor_scalar(**rsqrt_start(v, y))
                    up = UP * D ** 0.5
                    k, c = (RSQRT_K, RSQRT_K * RSQRT_C) if i < 8 else (0.5 * up, 1.5 * up)
                    if i in (5, 8):
                        ins = dve.tensor_tensor(t, y, y, ALU.mult)
                    if i in (6, 9):
                        ins = dve.scalar_tensor_tensor(u, t, -k, v, ALU.mult, ALU.mult)
                    if i in (7, 10):
                        ins = dve.scalar_tensor_tensor(y, u, c, y, ALU.add, ALU.mult)
                    ins.then_inc(root_chain, 1)

                def step(it, p, first=False, last=False):
                    if first:
                        normalise(2 * p)
                        normalise(2 * p + 1)
                    for i in range(2 * PB):
                        if i < ROOT and p == 1 and not first:
                            short(i, it - 1, 1)
                        if i < ROOT and p == 3 and not last:
                            short(i, it, 0)
                        if i < PB:
                            if last:
                                result(p, i)
                            elif not first:
                                affine(it, p, i)
                        elif not (first and p < 1) and not (last and p >= 1):
                            it1, p1 = back(it, p, 1, NP)
                            measure(it1, p1, i - PB)

                run(dve, step, ITERS, per=NP, lag=NP)

        HW = D + 1
        SB = 2
        SR = SB * P
        NSUB = NB // SB
        JC = 2
        NC = NB // JC
        SLOTS = 4
        rhs = view(work, 0, [2, NB, NPART, HW], BF16, 2)
        t_wide = view(work, 2 * NB * NPART * HW * 2, [NPART * HW], F32, 4)
        scr = conn[:, :, :, :].rearrange("p a b c -> p (a b c)").bitcast(F32)
        hT = scr.rearrange("p (k i) -> p k i", k=2)
        f_w, r_w = (scr[:, 2 * i * SR:2 * (i + 1) * SR].rearrange("p (k b d) -> p k b d", k=2, b=SB)
                    for i in range(2))
        a_bc = scr[:, 0:2 * SR].rearrange("p (k i) -> p k i", k=2)
        x_t = scr[:, 2 * SR:4 * SR].rearrange("p (k b d) -> p k b d", k=2, b=SB)
        tiles3 = X[:, :, :].rearrange("p b d -> p (b d)").bitcast(BF16).rearrange(
            "p (f s j i) -> p f s j i", f=4, s=SLOTS, j=JC)
        m_bf, above, pairs = tiles3[:, 0], tiles3[:, 1], tiles3[:, 2:4]
        BIGGER = float(2 ** 60)
        x2_d = nc.dram_tensor("x2_d", (N, D), F32, kind="Internal").ap()
        x3_d = nc.dram_tensor("x3_d", (N, D), F32, kind="Internal").ap()
        ab_d = nc.dram_tensor("ab_d", (2 * NB, P), F32, kind="Internal").ap()
        h_d = nc.dram_tensor("h_d", (N, D), F32, kind="Internal").ap()
        aw = sb("aw", [P, 2], F32)
        ab = sb("ab", [P, 2, NB], F32)
        FF = sb("FF", [P, 2, NB], F32)
        CC = sb("CC", [P, 2, NB], F32)
        negb = sb("negb", [P, NB], F32)
        bigb = sb("bigb", [P, NB], F32)
        bm = sb("bm", [P, 4], F32)
        spread = sb("spread", [P, 1], F32)
        far = sb("far", [P, 1], I32)
        FAR = 64.0
        num = sb("num", [P, SB, HW], F32)
        ab_rows = sb("ab_rows", [2 * NB, P], F32)
        dn = sb("dn", [P, 4, SB], F32)
        H = X
        with ExitStack() as c3:
            def sem3(name):
                return c3.enter_context(nc.semaphore(name))

            dchain = sem3("g_dchain")
            saved = sem3("saved")
            aw_in = sem3("aw_in")
            h_ready = sem3("g_h_ready")
            hT_psum = sem3("g_hT_psum")
            hT_ready = sem3("g_hT_ready")
            ab_psum = sem3("ab_psum")
            b_max = sem3("b_max")
            b_all = sem3("b_all")
            f_in = sem3("f_in")
            f_out = sem3("f_out")
            c_in = sem3("c_in")
            c_out = sem3("c_out")
            f_ready = sem3("f_ready")
            r_ready = sem3("r_ready")
            p1_ready = sem3("p1_ready")
            p2_ready = sem3("p2_ready")
            p3_ready = sem3("p3_ready")
            a_psum = sem3("a_psum")
            ab_row = sem3("ab_row")
            a_saved = sem3("a_saved")
            th_psum = sem3("th_psum")
            block = c3.enter_context(nc.Block())

            def part(k, t):
                u, f = k // 2, k % 2
                return rhs[:, f, u * SB:(u + 1) * SB, t, 0:D]

            @block.sync
            def _(sp):
                sp.dma_start(x2_d.rearrange("(b p) d -> p b d", p=P), X[:, :, :]).then_inc(saved, 16)
                sp.dma_start(aw[:, :], a1).then_inc(aw_in, 16)
                sp.wait_ge(h_ready, NG)
                sp.dma_start(h_d.rearrange("(b p) d -> p b d", p=P), H[:, :, :]).then_inc(saved, 16)
                sp.wait_ge(ab_row, 1)
                sp.dma_start(ab_d, ab_rows[:, :]).then_inc(a_saved, 16)
                sp.wait_ge(a_saved, 16)
                sp.wait_ge(saved, 32)

            @block.gpsimd
            def _(pool):
                pool.wait_ge(b_max, 2)
                pool.partition_all_reduce(bm[:, 2:4], bm[:, 0:2], P, bass.bass_isa.ReduceOp.max).then_inc(b_all, 1)
                pool.wait_ge(f_out, 1)
                for k in range(2 * NSUB):
                    if k >= 2:
                        pool.wait_ge(r_ready, k - 1)
                    u, f = k // 2, k % 2
                    blocks = slice(u * SB, (u + 1) * SB)
                    pool.tensor_tensor(f_w[:, k % 2, :, :], H[:, blocks, :],
                                       FF[:, f, blocks].unsqueeze(2).broadcast_to([P, SB, D]),
                                       ALU.mult).then_inc(f_ready, 1)

            @block.tensor
            def _(pe):
                pe.wait_ge(aw_in, 16)
                for u in range(NG + 1):
                    if u < NG:
                        pe.wait_ge(h_ready, u + 1)
                        if u >= 2:
                            pe.wait_ge(hT_ready, u - 1)
                        for b in range(GB):
                            last = pe.transpose(ps[:, u % 2, b * P:(b + 1) * P], H[:, u * GB + b, :], ident[:, :])
                        last.then_inc(hT_psum, 1)
                    if u >= 1:
                        pe.wait_ge(hT_ready, u)
                        for b in range(GB):
                            k = (u - 1) * GB + b
                            last = pe.matmul(ps[:, 2, 2 * k:2 * k + 2], hT[:, (u - 1) % 2, b * P:(b + 1) * P],
                                             aw[:, :], start=True, stop=True)
                        last.then_inc(ab_psum, 1)
                pe.wait_ge(f_in, 1)
                pe.transpose(ps[0:2 * NB, 4, 0:P], ab[:, :, :].rearrange("p k b -> p (k b)"),
                             ident[:, :]).then_inc(a_psum, 1)
                for b in range(NB):
                    last = pe.matmul(ps[:, 3, 0:D], ones[:, :], H[:, b, :], start=(b == 0), stop=(b == NB - 1))
                last.then_inc(th_psum, 1)

            @block.scalar
            def _(act):
                for u in range(NG):
                    act.wait_ge(hT_psum, u + 1)
                    if u >= 2:
                        act.wait_ge(ab_psum, u - 1)
                    act.activation(hT[:, u % 2, :], ps[:, u % 2, :], ACT.Copy).then_inc(hT_ready, 1)
                act.wait_ge(a_psum, 1)
                act.activation(ab_rows[:, :], ps[0:2 * NB, 4, 0:P], ACT.Copy).then_inc(ab_row, 1)
                act.wait_ge(f_in, 2)
                act.activation(FF[:, :, :], FF[:, :, :], ACT.Exp).then_inc(f_out, 1)
                act.wait_ge(c_in, 1)
                act.activation(CC[:, :, :], CC[:, :, :], ACT.Exp).then_inc(c_out, 1)
                for k in range(2 * NSUB + 1):
                    if k < 2 * NSUB:
                        act.wait_ge(f_ready, k + 1)
                        act.activation(part(k, 0), f_w[:, k % 2, :, :], ACT.Copy).then_inc(p1_ready, 1)
                    if k >= 1:
                        act.wait_ge(r_ready, k)
                        act.activation(part(k - 1, 1), r_w[:, (k - 1) % 2, :, :], ACT.Copy).then_inc(p2_ready, 1)

            @block.vector
            def _(dve):
                ch = Chain(dve, dchain)
                for b in range(NB):
                    ch.add(dve.bn_stats(st6[:, b, :], X[:, b, :]))
                ch.done()
                for b in range(NB):
                    ch.add(dve.bn_aggr(mv[:, b, :], st6[:, b, :]))
                ch.done()
                ch.link(dve.tensor_scalar(v_col, mv[:, :, 1], EPS, None, ALU.add))
                emit_rsqrt(dve, ch.link, v_col, y_col, t_col, u_col, 2)
                dve.wait_ge(saved, 16)
                for b in range(NB):
                    ins = dve.tensor_scalar(H[:, b, :], X[:, b, :], mv[:, b, 0:1], y_col[:, b:b + 1],
                                            ALU.subtract, ALU.mult)
                    if b % GB == GB - 1:
                        ins.then_inc(h_ready, 1)
                dve.wait_ge(ab_psum, NG)
                ch.link(dve.tensor_copy(ab[:, :, :], ps[:, 2, 0:2 * NB].rearrange("p (b k) -> p k b", k=2)))
                dve.tensor_reduce(bm[:, 0:1], ab[:, 1, :], AX_X, ALU.max).then_inc(b_max, 1)
                dve.tensor_scalar(negb[:, :], ab[:, 1, :], -1.0, None, ALU.mult).then_inc(f_in, 1)
                ch.link(dve.tensor_scalar(bigb[:, :], ab[:, 1, :], BIGGER, None, ALU.mult))
                dve.wait_ge(f_in, 1)
                dve.tensor_reduce(bm[:, 1:2], negb[:, :], AX_X, ALU.max).then_inc(b_max, 1)
                dve.wait_ge(b_all, 1)
                ch.link(dve.tensor_tensor(spread[:, :], bm[:, 2:3], bm[:, 3:4], ALU.add))
                ch.link(dve.tensor_scalar(far[:, :], spread[:, :], FAR, None, ALU.is_gt))
                ch.link(dve.tensor_scalar(FF[:, 0, :], ab[:, 1, :], bm[:, 2:3], None, ALU.subtract))
                dve.tensor_scalar(FF[:, 1, :], FF[:, 0, :], SLOPE1, None, ALU.mult).then_inc(f_in, 1)
                ch.link(dve.tensor_scalar(CC[:, 0, :], ab[:, 0, :], bm[:, 2:3], None, ALU.add))
                ch.link(dve.tensor_scalar(CC[:, 1, :], CC[:, 0, :], SLOPE1, None, ALU.mult))
                ch.link(dve.tensor_tensor(t_col, CC[:, 0, :], CC[:, 1, :], ALU.max))
                dve.tensor_tensor(CC[:, :, :], CC[:, :, :], t_col.unsqueeze(1).broadcast_to([P, 2, NB]),
                                  ALU.subtract).then_inc(c_in, 1)
                dve.wait_ge(f_out, 1)
                ch.link(dve.tensor_copy(rhs[:, :, :, 0, D], FF[:, :, :]))
                rr = col[:, 0:2, :]
                ch.link(dve.tensor_tensor(rr, FF[:, :, :], rhs[:, :, :, 0, D], ALU.subtract))
                ch.link(dve.tensor_copy(rhs[:, :, :, 1, D], rr))
                ch.link(dve.tensor_tensor(rr, rr, rhs[:, :, :, 1, D], ALU.subtract))
                ch.link(dve.tensor_copy(rhs[:, :, :, 2, D], rr))
                for k in range(2 * NSUB + 1):
                    if k < 2 * NSUB:
                        dve.wait_ge(p1_ready, k + 1)
                        if k >= 2:
                            dve.wait_ge(p3_ready, k - 1)
                        dve.tensor_tensor(r_w[:, k % 2, :, :], f_w[:, k % 2, :, :], part(k, 0),
                                          ALU.subtract).then_inc(r_ready, 1)
                    if k >= 1:
                        dve.wait_ge(p2_ready, k)
                        dve.tensor_tensor(part(k - 1, 2), r_w[:, (k - 1) % 2, :, :], part(k - 1, 1),
                                          ALU.subtract).then_inc(p3_ready, 1)
                dve.wait_ge(th_psum, 1)
                ch.link(dve.tensor_scalar(total[:, :], ps[:, 3, 0:D], 1.0 / N, None, ALU.mult))
                dve.wait_ge(p3_ready, 2 * NSUB)

        with ExitStack() as c4:
            def sem4(name):
                return c4.enter_context(nc.semaphore(name))

            step_chain = sem4("step_chain")
            above_ready = sem4("above_ready")
            m_act = sem4("m_act")
            m_dve = sem4("m_dve")
            up_ready = sem4("up_ready")
            low_ready = sem4("low_ready")
            used = sem4("used")
            banks_free = sem4("banks_free")
            low_sum = sem4("low_sum")
            wide_free = sem4("wide_free")
            a_in = [sem4(f"a_in{i}") for i in range(2)]
            x_in3 = [sem4(f"x_in3{i}") for i in range(2)]
            x_out = [sem4(f"x_out{i}") for i in range(2)]
            x_done = sem4("x_done")
            block = c4.enter_context(nc.Block())
            a_flat = ab_d.rearrange("b p -> (b p)")
            PARTS3 = (1, 1, 1, 1, 1, 1, 1, SB, SB)
            STEP = sum(PARTS3)

            def mask_chunk(g, h, c):
                return mask_v[:, bass.ds(g, 1), c * JC:(c + 1) * JC, h * SR:(h + 1) * SR].rearrange(
                    "p o j i -> p (o j) i")

            @block.sync
            def _(sp):
                for s in range(NSUB):
                    if s >= 2:
                        sp.wait_ge(above_ready, (s - 1) * NC)
                    sp.dma_start(a_bc[:, s % 2, :], a_flat[s * SR:(s + 1) * SR].partition_broadcast(P)).then_inc(
                        a_in[s % 2], 16)
                    if s >= 2:
                        sp.wait_ge(x_done, s - 1)
                        sp.dma_start(x3_d[(s - 2) * SR:(s - 1) * SR, :].rearrange("(b p) d -> p b d", p=P),
                                     x_t[:, s % 2, :, :]).then_inc(x_out[s % 2], 16)
                        sp.wait_ge(x_out[s % 2], (s // 2) * 16)
                    sp.dma_start(x_t[:, s % 2, :, :], x2_d[s * SR:(s + 1) * SR, :].rearrange(
                        "(b p) d -> p b d", p=P)).then_inc(x_in3[s % 2], 16)
                for s in (NSUB - 2, NSUB - 1):
                    sp.wait_ge(x_done, s + 1)
                    sp.dma_start(x3_d[s * SR:(s + 1) * SR, :].rearrange("(b p) d -> p b d", p=P),
                                 x_t[:, s % 2, :, :]).then_inc(x_out[s % 2], 16)
                for i in range(2):
                    sp.wait_ge(x_out[i], NSUB // 2 * 16)

            @block.tensor
            def _(pe):
                def chunk(g, h, c):
                    s = 2 * g + h
                    if c == 0:
                        pe.wait_ge(banks_free, s + 1)
                    pe.wait_ge(up_ready, s * NC + c + 1)
                    for f in range(2):
                        if f == 1:
                            pe.wait_ge(low_ready, s * NC + c + 1)
                        for j in range(JC):
                            for b in range(SB):
                                last = pe.matmul(ps[:, 4 * h + 2 * f + b, 0:NPART * HW],
                                                 pairs[:, f, c % SLOTS, j, b * P:(b + 1) * P],
                                                 rhs[:, f, c * JC + j, :, :].rearrange("p t d -> p (t d)"),
                                                 start=(c + j == 0), stop=(c == NC - 1 and j == JC - 1))
                    last.then_inc(used, 1)

                with pe.Fori(0, NSUB // 2) as g:
                    for h in range(2):
                        for c in range(NC):
                            chunk(g, h, c)

            @block.scalar
            def _(act):
                def scale_low(g, h, b):
                    s = 2 * g + h
                    if b == 0:
                        act.wait_ge(used, (s + 1) * NC + SLOTS)
                    act.wait_ge(wide_free, s * SB + b + 1)
                    act.activation(t_wide, ps[:, 4 * h + 2 + b, 0:NPART * HW], ACT.Copy,
                                   scale=CC[:, 1, bass.ds(s * SB + b, 1)]).then_inc(low_sum, 1)

                def chunk(g, h, c):
                    s = 2 * g + h
                    if c == 0:
                        act.wait_ge(a_in[h], (g + 1) * 16)
                    act.wait_ge(used, s * NC + c + 1)
                    for j in range(JC):
                        last = act.activation(above[:, c % SLOTS, j, :], a_bc[:, h, :], ACT.Relu, scale=BIGGER,
                                              bias=bigb[:, c * JC + j:c * JC + j + 1])
                    last.then_inc(above_ready, 1)
                    if c % 4 != 3:
                        act.activation(m_bf[:, c % SLOTS, :, :], mask_chunk(g, h, c), ACT.Relu).then_inc(m_act, 1)

                def body(g, first=False):
                    for h in range(2):
                        for c in range(NC):
                            chunk(g, h, c)
                            if c in (SLOTS, 2 * SLOTS) and not (first and h == 0):
                                scale_low(*((g, 0) if h == 1 else (g - 1, 1)), c // SLOTS - 1)

                body(0, first=True)
                with act.Fori(1, NSUB // 2) as g:
                    body(g)
                for b in range(SB):
                    scale_low(NSUB // 2 - 1, 1, b)

            @block.vector
            def _(dve):
                for i in range(SLOTS):
                    dve.memset(marks[:, i:i + 1], 0.0).then_inc(used, 1)
                for i in range(2):
                    dve.memset(marks[:, 4 + i:5 + i], 0.0).then_inc(banks_free, 1)
                dve.memset(marks[:, 8:9], 0.0).then_inc(wide_free, 1)

                def chunk(g, h, c):
                    s = 2 * g + h
                    if c % 4 == 3:
                        dve.wait_ge(used, s * NC + c + 1)
                        dve.tensor_scalar(m_bf[:, c % SLOTS, :, :], mask_chunk(g, h, c), 0.0, None,
                                          ALU.max).then_inc(m_dve, 1)
                        dve.wait_ge(m_dve, s * (NC // 4) + c // 4 + 1)
                    else:
                        dve.wait_ge(m_act, s * (NC // 4 * 3) + c // 4 * 3 + c % 4 + 1)
                    dve.wait_ge(above_ready, s * NC + c + 1)
                    dve.tensor_tensor(pairs[:, 0, c % SLOTS, :, :], above[:, c % SLOTS, :, :],
                                      m_bf[:, c % SLOTS, :, :], ALU.min).then_inc(up_ready, 1)

                def chunk_low(g, h, c):
                    dve.wait_ge(up_ready, (2 * g + h) * NC + c + 1)
                    dve.tensor_tensor(pairs[:, 1, c % SLOTS, :, :], m_bf[:, c % SLOTS, :, :],
                                      pairs[:, 0, c % SLOTS, :, :], ALU.subtract).then_inc(low_ready, 1)

                def free_wide(g, h):
                    dve.wait_ge(step_chain, (2 * g + h) * STEP + 2)
                    dve.memset(marks[:, 9:10], 0.0).then_inc(wide_free, 1)

                def finish(g, h, i):
                    s = 2 * g + h
                    none, den, rden = dn[:, 0, :], dn[:, 1, :], dn[:, 2, :]
                    lk = Chain(dve, step_chain, s * STEP + sum(PARTS3[:i]))
                    if i > 0:
                        lk.done()
                    b = i // 2
                    if i in (0, 2):
                        dve.wait_ge(low_sum, s * SB + b + 1)
                        lk.add(dve.scalar_tensor_tensor(t_wide, ps[:, 4 * h + b, 0:NPART * HW],
                                                        CC[:, 0, bass.ds(s * SB + b, 1)], t_wide,
                                                        ALU.mult, ALU.add))
                    if i in (1, 3):
                        lk.add(dve.tensor_reduce(num[:, b, :], t_wide.rearrange("p (t d) -> p d t", t=NPART),
                                                 AX_X, ALU.add))
                    if i == 3:
                        dve.memset(marks[:, 11:12], 0.0).then_inc(banks_free, 1)
                    if i == 4:
                        dve.memset(marks[:, 10:11], 0.0).then_inc(wide_free, 1)
                    if i == 4:
                        lk.add(dve.tensor_scalar(none, num[:, :, D], 0.0, None, ALU.is_equal))
                    if i == 5:
                        lk.add(dve.tensor_tensor(den, num[:, :, D], none, ALU.add))
                    if i == 6:
                        lk.add(dve.reciprocal(rden, den))
                    if i == 7:
                        for b in range(SB):
                            lk.add(dve.scalar_tensor_tensor(num[:, b, 0:D], total[:, :], none[:, b:b + 1],
                                                            num[:, b, 0:D], ALU.mult, ALU.add))
                    if i == 8:
                        dve.wait_ge(x_in3[h], (g + 1) * 16)
                        for b in range(SB):
                            lk.add(dve.scalar_tensor_tensor(x_t[:, h, b, :], num[:, b, 0:D], rden[:, b:b + 1],
                                                            x_t[:, h, b, :], ALU.mult, ALU.add))
                        lk.done()
                        for b in range(SB):
                            ins = dve.bn_stats(st6[:, bass.ds(s * SB + b, 1), :].rearrange("p o k -> p (o k)"),
                                               x_t[:, h, b, :])
                        ins.then_inc(x_done, 1)
                    assert lk.n == PARTS3[i]

                def body(g, first=False):
                    for h in range(2):
                        for c in range(NC):
                            chunk(g, h, c)
                            chunk_low(g, h, c)
                            part = {5: 0, 6: 1, 9: 2, 10: 3, 11: 4, 12: 5, 13: 6, 14: 7, 15: 8}.get(c)
                            if part is not None and not (first and h == 0):
                                finish(*((g, 0) if h == 1 else (g - 1, 1)), part)
                            if c == 7 and not (first and h == 0):
                                free_wide(*((g, 0) if h == 1 else (g - 1, 1)))

                body(0, first=True)
                with dve.Fori(1, NSUB // 2) as g:
                    body(g)
                for i in range(len(PARTS3)):
                    finish(NSUB // 2 - 1, 1, i)
                    if i == 1:
                        free_wide(NSUB // 2 - 1, 1)

        BIG = 1e30
        h_all = X
        b_bc = view(work, 0, [N], F32, 4)
        score = view(work, 4 * N, [N], F32, 4)
        far_m = view(work, 8 * N, [N], BF16, 2)
        pen = view(work, 8 * N, [N], F32, 4)
        prob_T = pen
        ident_bf = sb("ident_bf", [P, P], BF16)
        with ExitStack() as c5:
            def sem5(name):
                return c5.enter_context(nc.semaphore(name))

            far_in = sem5("far_in")
            far_ident = sem5("far_ident")
            far_x_in = sem5("far_x_in")
            far_x_out = sem5("far_x_out")
            far_mask = sem5("far_mask")
            far_turned = sem5("far_turned")
            far_max = sem5("far_max")
            far_exp = sem5("far_exp")
            far_pT_psum = sem5("far_pT_psum")
            far_pT = sem5("far_pT")
            far_sum = sem5("far_sum")
            far_rows = sem5("far_rows")
            far_done = sem5("far_done")
            far_chain = sem5("far_chain")
            x_back = sem5("x_back")
            FC = 8
            ps_all = ps[:, :, :].rearrange("p k c -> p (k c)")
            block = c5.enter_context(nc.Block())

            def is_far(eng):
                return eng.value_load(far[0:1, 0:1], min_val=0, max_val=1)

            def x_rows(t, r):
                return t.rearrange("(b p) d -> b p d", p=P)[bass.ds(r, 1), :, :].rearrange("o p d -> p (o d)")

            @block.sync
            def _(sp):
                with sp.If(is_far(sp) > 0):
                    sp.dma_start(h_all[:, :, :], h_d.rearrange("(b p) d -> p b d", p=P)).then_inc(far_in, 16)
                    sp.dma_start(b_bc, a_flat[N:2 * N].partition_broadcast(P)).then_inc(far_in, 16)
                    with sp.Fori(0, NB) as r:
                        sp.wait_ge(far_done, r + 1)
                        sp.dma_start(num[:, 0, 0:D], x_rows(x2_d, r)).then_inc(far_x_in, 16)
                        sp.wait_ge(far_rows, r + 1)
                        sp.dma_start(x_rows(x3_d, r), num[:, 1, 0:D]).then_inc(far_x_out, 16)
                    sp.wait_ge(far_x_out, NB * 16)
                sp.dma_start(X[:, :, :], x3_d.rearrange("(b p) d -> p b d", p=P)).then_inc(x_back, 16)
                sp.wait_ge(x_back, 16)

            @block.scalar
            def _(act):
                with act.If(is_far(act) > 0):
                    with act.Fori(0, NG) as g:
                        for b in range(GB):
                            r = g * GB + b
                            act.wait_ge(far_done, r + 1)
                            m = mask_v[:, bass.ds(g, 1), :, b * P:(b + 1) * P].rearrange("p o j i -> p (o j) i")
                            act.activation(far_m.rearrange("p (j i) -> p j i", j=NB), m, ACT.Relu).then_inc(
                                far_mask, 1)
                            act.wait_ge(far_max, r + 1)
                            act.activation(score, score, ACT.Exp, bias=dn[:, 0, 0:1]).then_inc(far_exp, 1)
                            act.wait_ge(far_pT_psum, r + 1)
                            act.activation(prob_T, ps_all, ACT.Copy).then_inc(far_pT, 1)

            @block.tensor
            def _(pe):
                with pe.If(is_far(pe) > 0):
                    pe.wait_ge(far_ident, 1)
                    pe.wait_ge(far_in, 32)
                    with pe.Fori(0, NB) as r:
                        pe.wait_ge(far_mask, r + 1)
                        for j in range(NB):
                            last = pe.matmul(ps_all[:, j * P:(j + 1) * P], far_m[:, j * P:(j + 1) * P],
                                             ident_bf[:, :], start=True, stop=True)
                        last.then_inc(far_turned, 1)
                        pe.wait_ge(far_exp, r + 1)
                        for j in range(NB):
                            last = pe.transpose(ps_all[:, j * P:(j + 1) * P], score[:, j * P:(j + 1) * P], ident[:, :])
                        last.then_inc(far_pT_psum, 1)
                        pe.wait_ge(far_pT, r + 1)
                        for j in range(NB):
                            last = pe.matmul(ps[:, 0, 0:D], prob_T[:, j * P:(j + 1) * P], h_all[:, j, :],
                                             start=(j == 0), stop=(j == NB - 1))
                        last.then_inc(far_sum, 1)

            @block.vector
            def _(dve):
                with dve.If(is_far(dve) > 0):
                    dve.tensor_copy(ident_bf[:, :], ident[:, :]).then_inc(far_ident, 1)
                    dve.memset(marks[:, 12:13], 0.0).then_inc(far_done, 1)
                    dve.wait_ge(far_in, 32)
                    with dve.Fori(0, NB) as r:
                        lk = Chain(dve, far_chain, r * FC)
                        dve.wait_ge(far_done, r + 1)
                        lk.link(dve.tensor_scalar(score, b_bc, ab[:, 0, bass.ds(r, 1)], None, ALU.add))
                        lk.link(dve.scalar_tensor_tensor(score, score, SLOPE1, score, ALU.mult, ALU.max))
                        dve.wait_ge(far_turned, r + 1)
                        lk.link(dve.tensor_scalar(pen, ps_all, BIG, -BIG, ALU.mult, ALU.add))
                        lk.link(dve.tensor_tensor(score, score, pen, ALU.add))
                        lk.link(dve.tensor_reduce(dn[:, 1, 0:1], score, AX_X, ALU.max))
                        dve.tensor_scalar(dn[:, 0, 0:1], dn[:, 1, 0:1], -1.0, None, ALU.mult).then_inc(far_max, 1)
                        dve.wait_ge(far_exp, r + 1)
                        lk.link(dve.tensor_reduce(dn[:, 2, 0:1], score, AX_X, ALU.add))
                        lk.link(dve.reciprocal(dn[:, 3, 0:1], dn[:, 2, 0:1]))
                        dve.wait_ge(far_sum, r + 1)
                        lk.link(dve.tensor_scalar(num[:, 1, 0:D], ps[:, 0, 0:D], dn[:, 3, 0:1], None, ALU.mult))
                        dve.wait_ge(far_x_in, (r + 1) * 16)
                        dve.tensor_tensor(num[:, 1, 0:D], num[:, 1, 0:D], num[:, 0, 0:D],
                                          ALU.add).then_inc(far_rows, 1)
                        assert lk.n == FC, lk.n
                        dve.wait_ge(far_rows, r + 1)
                        dve.bn_stats(st6[:, bass.ds(r, 1), :].rearrange("p o k -> p (o k)"), num[:, 1, 0:D])
                        dve.wait_ge(far_x_out, (r + 1) * 16)
                        dve.memset(marks[:, 13:14], 0.0).then_inc(far_done, 1)

        NE = 16
        HID = 256
        K = 2
        KB = K * NB
        TILES = K * N // P + NE
        RING = 16
        ROUNDS = TILES // RING
        at = [0]

        def m(shape, dt, size):
            n = size
            for x_ in shape:
                n *= x_
            v_ = view(mask, at[0], shape, dt, size)
            at[0] += (n + 63) // 64 * 64
            assert at[0] <= mask_bytes
            return v_

        w12 = m([NE, 2 * HID], F32, 4)
        w3_s = m([NE, 2, D], F32, 4)
        rows_k = view(work, 0, [K, NB, DW], F32, 4)
        Y = rows_k[:, 0, :, 0:D]
        NRES = 4
        result = m([NRES, K, GB, D], F32, 4)
        yT = m([2, GR], F32, 4)
        gw = m([NE], F32, 4)
        gb = m([NE], F32, 4)
        logit = m([NB, NE], F32, 4)
        top = m([NB, 8], F32, 4)
        top_i = m([NB, 8], U32, 4)
        idx = m([K, NB], F32, 4)
        pw = m([K, NB], F32, 4)
        iota_e = m([NE], F32, 4)
        iota_t = m([TILES], F32, 4)
        before = m([P], BF16, 2)
        hot = m([K, NB, NE], BF16, 2)
        tot = m([NE, KB], F32, 4)
        cum = m([NE, KB], F32, 4)
        one_row = m([NE * KB], F32, 4)
        n_e = m([NE], F32, 4)
        n_i = m([NE], I32, 4)
        t_e = m([NE], F32, 4)
        t_s = m([NE], F32, 4)
        off_e = m([NE], F32, 4)
        place = m([K, NB, NE], F32, 4)
        slot_f = m([K, NB], F32, 4)
        slot = m([KB], U32, 4)
        cmp_t = m([TILES, NE], F32, 4)
        eid_f = m([TILES], F32, 4)
        LATE = 3
        eid = m([LATE + TILES], I32, 4)
        xs = view(work, 33280, [RING // 2, 2, DW], F32, 4)
        xT_s = m([2, P], F32, 4)
        sil = m([2, HID], F32, 4)
        hid = m([2, HID], F32, 4)
        hidT = m([2, 2, P], F32, 4)
        o_s = view(work, 41600, [RING, D], F32, 4)
        with ExitStack() as c6:
            def sem6(name):
                return c6.enter_context(nc.semaphore(name))

            dchain = sem6("e_dchain")
            gate_in = sem6("gate_in")
            pchain = sem6("pchain")
            before_ok = sem6("before_ok")
            iota_ok = sem6("iota_ok")
            y_ready = sem6("y_ready")
            yT_psum = sem6("yT_psum")
            yT_ready = sem6("yT_ready")
            logit_psum = sem6("logit_psum")
            logit_taken = sem6("logit_taken")
            gap_ready = sem6("gap_ready")
            ratio = sem6("ratio")
            hot_ready = sem6("hot_ready")
            rank_psum = sem6("rank_psum")
            slot_ready = sem6("slot_ready")
            twin = sem6("twin")
            scattered = sem6("scattered")
            w_in6 = sem6("w_in6")
            block = c6.enter_context(nc.Block())

            @block.sync
            def _(sp):
                sp.dma_start(gw, gate_w).then_inc(gate_in, 16)
                sp.dma_start(gb, gate_b.partition_broadcast(P)).then_inc(gate_in, 16)
                sp.dma_start(w12[:, :, 0:HID], w1.rearrange("e d h -> d e h")).then_inc(w_in6, 16)
                sp.dma_start(w12[:, :, HID:2 * HID], w2.rearrange("e d h -> d e h")).then_inc(w_in6, 16)
                sp.dma_start(w3_s, w3.rearrange("e (c p) o -> p e c o", p=P)).then_inc(w_in6, 16)
                sp.wait_ge(w_in6, 48)

            @block.gpsimd
            def _(pool):
                pool.iota(iota_e, pattern=[[1, NE]], base=0, channel_multiplier=0,
                          allow_small_or_imprecise_dtypes=True).then_inc(iota_ok, 1)
                pool.iota(iota_t, pattern=[[1, TILES]], base=0, channel_multiplier=0,
                          allow_small_or_imprecise_dtypes=True).then_inc(iota_ok, 1)
                pool.memset(before, 1.0).then_inc(pchain, 1)
                pool.wait_ge(pchain, 1)
                pool.affine_select(out=before, in_=before, compare_op=ALU.is_gt, fill=0.0, base=0,
                                   pattern=[[1, P]], channel_multiplier=-1).then_inc(before_ok, 1)
                for k in range(K):
                    pool.iota(rows_k[:, k, :, D:D + 1].bitcast(U32), pattern=[[P, NB]], base=k * N,
                              channel_multiplier=1).then_inc(pchain, 1)
                for g in range(NG):
                    pool.wait_ge(y_ready, g + 1)
                    pool.tensor_copy(rows_k[:, 1, g * GB:(g + 1) * GB, 0:D],
                                     rows_k[:, 0, g * GB:(g + 1) * GB, 0:D]).then_inc(twin, 1)
                pool.wait_ge(pchain, 1 + K)
                pool.wait_ge(twin, NG)
                pool.wait_ge(slot_ready, 1)
                for k in range(K):
                    for b in range(NB):
                        pool.indirect_dma_start(
                            out=xs_d, out_offset=bass.IndirectOffsetOnAxis(
                                ap=slot[:, k * NB + b:k * NB + b + 1], axis=0),
                            in_=rows_k[:, k, b, :], in_offset=None).then_inc(scattered, 16)
                pool.wait_ge(scattered, KB * 16)

            @block.tensor
            def _(pe):
                pe.wait_ge(gate_in, 32)
                for g in range(NG + 1):
                    if g < NG:
                        pe.wait_ge(y_ready, g + 1)
                        if g >= 2:
                            pe.wait_ge(yT_ready, g - 1)
                        for b in range(GB):
                            last = pe.transpose(ps[:, g % 2, b * P:(b + 1) * P], Y[:, g * GB + b, :], ident[:, :])
                        last.then_inc(yT_psum, 1)
                    if g >= 1:
                        pe.wait_ge(yT_ready, g)
                        if g >= 3:
                            pe.wait_ge(logit_taken, g - 2)
                        for b in range(GB):
                            k = (g - 1) * GB + b
                            last = pe.matmul(ps[:, 2 + (g - 1) % 2, k * NE:(k + 1) * NE],
                                             yT[:, (g - 1) % 2, b * P:(b + 1) * P], gw,
                                             start=True, stop=True)
                        last.then_inc(logit_psum, 1)
                pe.wait_ge(before_ok, 1)
                for k in range(K):
                    pe.wait_ge(hot_ready, k + 1)
                    h_k = hot[:, k, :, :].rearrange("p b e -> p (b e)")
                    pe.matmul(ps[:, 4 + k, :], before, h_k, start=True, stop=True)
                    pe.matmul(ps[:, 6 + k, :], ones_bf[:, :], h_k, start=True, stop=True).then_inc(rank_psum, 1)

            @block.scalar
            def _(act):
                for g in range(NG):
                    act.wait_ge(yT_psum, g + 1)
                    if g >= 2:
                        act.wait_ge(logit_psum, g - 1)
                    act.activation(yT[:, g % 2, :], ps[:, g % 2, :], ACT.Copy).then_inc(yT_ready, 1)
                act.wait_ge(gap_ready, 1)
                act.activation(pw[:, 1, :], pw[:, 1, :], ACT.Exp).then_inc(ratio, 1)

            @block.vector
            def _(dve):
                ch = Chain(dve, dchain)
                ch.add(dve.memset(one_row, 1.0))
                ch.add(dve.memset(eid[:, 0:LATE], 0))
                ch.done()
                for b in range(NB):
                    ch.add(dve.bn_aggr(mv[:, b, :], st6[:, b, :]))
                ch.done()
                ch.link(dve.tensor_scalar(v_col, mv[:, :, 1], EPS, None, ALU.add))
                emit_rsqrt(dve, ch.link, v_col, y_col, t_col, u_col, 2)
                for b in range(NB):
                    ins = dve.tensor_scalar(Y[:, b, :], X[:, b, :], mv[:, b, 0:1], y_col[:, b:b + 1],
                                            ALU.subtract, ALU.mult)
                    if b % GB == GB - 1:
                        ins.then_inc(y_ready, 1)
                for g in range(NG):
                    dve.wait_ge(logit_psum, g + 1)
                    dve.tensor_tensor(logit[:, g * GB:(g + 1) * GB, :],
                                      ps[:, 2 + g % 2, g * GB * NE:(g + 1) * GB * NE].rearrange(
                                          "p (b e) -> p b e", e=NE),
                                      gb.unsqueeze(1).broadcast_to([P, GB, NE]), ALU.add).then_inc(logit_taken, 1)
                    dve.wait_ge(logit_taken, g + 1)
                    for b in range(g * GB, (g + 1) * GB):
                        ch.add(dve.max(top[:, b, :], logit[:, b, :]))
                    ch.done()
                    for b in range(g * GB, (g + 1) * GB):
                        ch.add(dve.max_index(top_i[:, b, :], top[:, b, :], logit[:, b, :]))
                ch.done()
                dve.tensor_tensor(pw[:, 1, :], top[:, :, 1], top[:, :, 0], ALU.subtract).then_inc(gap_ready, 1)
                ch.done()
                ch.link(dve.tensor_copy(idx, top_i[:, :, 0:K].rearrange("p b k -> p k b")))
                dve.wait_ge(iota_ok, 2)
                for k in range(K):
                    dve.tensor_tensor(hot[:, k, :, :], idx[:, k, :].unsqueeze(2).broadcast_to([P, NB, NE]),
                                      iota_e.unsqueeze(1).broadcast_to([P, NB, NE]), ALU.is_equal).then_inc(hot_ready, 1)
                dve.wait_ge(ratio, 1)
                ch.link(dve.tensor_scalar(v_col, pw[:, 1, :], 1.0, None, ALU.add))
                ch.link(dve.reciprocal(pw[:, 0, :], v_col))
                ch.link(dve.tensor_tensor(pw[:, 1, :], pw[:, 1, :], pw[:, 0, :], ALU.mult))
                ch.add(dve.tensor_copy(rows_k[:, :, :, D + 1], pw[:, :, :]))
                dve.wait_ge(rank_psum, K)
                for k in range(K):
                    ch.add(dve.tensor_copy(tot[:, :, k * NB:(k + 1) * NB],
                                           ps[:, 6 + k, :].rearrange("p (b e) -> p e b", e=NE)))
                ch.done()
                ch.link(dve.tensor_reduce(n_e, tot, AX_X, ALU.add))
                ch.link(dve.tensor_scalar(n_i, n_e, float(P - 1), None, ALU.add))
                ch.link(dve.tensor_scalar(n_i, n_i, 7, None, ALU.logical_shift_right))
                ch.link(dve.tensor_copy(t_e, n_i))
                ch.link(dve.tensor_tensor_scan(t_s, one_row[:, 0:NE], t_e, 0.0, ALU.mult, ALU.add))
                ch.link(dve.tensor_tensor(t_s, t_s, t_e, ALU.subtract))
                flat = lambda v_: v_.rearrange("p e k -> p (e k)")
                ch.link(dve.tensor_tensor_scan(flat(cum), one_row, flat(tot), 0.0, ALU.mult, ALU.add))
                ch.link(dve.tensor_tensor(cum, cum, tot, ALU.subtract))
                ch.link(dve.scalar_tensor_tensor(off_e, t_s, float(P), cum[:, :, 0], ALU.mult, ALU.subtract))
                ch.link(dve.tensor_tensor(cum, cum, off_e.unsqueeze(2).broadcast_to([P, NE, KB]), ALU.add))
                for k in range(K):
                    ch.add(dve.tensor_tensor(place[:, k, :, :], ps[:, 4 + k, :].rearrange("p (b e) -> p b e", e=NE),
                                             cum[:, :, k * NB:(k + 1) * NB].rearrange("p e b -> p b e"), ALU.add))
                ch.done()
                ch.link(dve.tensor_tensor(place, place, hot, ALU.mult))
                ch.link(dve.tensor_reduce(slot_f, place, AX_X, ALU.add))
                dve.tensor_copy(slot, slot_f.rearrange("p k b -> p (k b)")).then_inc(slot_ready, 1)
                ch.link(dve.tensor_tensor(cmp_t, t_s.unsqueeze(1).broadcast_to([P, TILES, NE]),
                                          iota_t.unsqueeze(2).broadcast_to([P, TILES, NE]), ALU.is_le))
                ch.link(dve.tensor_reduce(eid_f, cmp_t, AX_X, ALU.add))
                ch.link(dve.tensor_scalar(eid[:, LATE:LATE + TILES], eid_f, -1.0, None, ALU.add))

        with ExitStack() as c7:
            def sem7(name):
                return c7.enter_context(nc.semaphore(name))

            xs_in = [sem7(f"xs_in{i}") for i in range(RING // 2)]
            y_out = [sem7(f"y_out{i}") for i in range(RING)]
            xsT_psum = sem7("xsT_psum")
            xsT_ready = sem7("xsT_ready")
            up_psum = sem7("up_psum")
            sil_ready = sem7("sil_ready")
            hid_ready = sem7("hid_ready")
            hidT_psum = sem7("hidT_psum")
            hidT_ready = sem7("hidT_ready")
            o_psum = sem7("o_psum")
            o_ready = sem7("o_ready")
            block = c7.enter_context(nc.Block())

            @block.sync
            def _(sp):
                for c in range(TILES // 2):
                    for t in (2 * c - RING, 2 * c + 1 - RING):
                        if t >= 0:
                            sp.wait_ge(y_out[t % RING], (t // RING + 1) * 16)
                    sp.dma_start(xs[:, c % (RING // 2), :, :], xs_d[c * 2 * P:(c + 1) * 2 * P, :].rearrange(
                        "(t p) d -> p t d", p=P)).then_inc(xs_in[c % (RING // 2)], 16)

            @block.gpsimd
            def _(pool):
                for t in range(TILES):
                    pool.wait_ge(o_ready, t + 1)
                    pool.indirect_dma_start(
                        out=y_d, out_offset=bass.IndirectOffsetOnAxis(
                            ap=xs[:, t % RING // 2, t % 2, D:D + 1].bitcast(U32), axis=0),
                        in_=o_s[:, t % RING, :], in_offset=None).then_inc(y_out[t % RING], 16)
                for i in range(RING):
                    pool.wait_ge(y_out[i], TILES // RING * 16)

            @block.tensor
            def _(pe):
                experts = []

                def load_experts(it, last):
                    n = LATE if last else LATE + RING
                    src = eid[0:1, it * RING:it * RING + n] if isinstance(it, int) else eid[0:1, bass.ds(it * RING, n)]
                    _, values = nc.values_load_multi_w_load_instructions(
                        src, engines=(pe.engine,), min_val=0, max_val=NE - 1,
                        skip_runtime_bounds_check_because="they are counts of at most NE starts, less one")
                    experts[:] = values

                def turn(it, t):
                    pe.wait_ge(xs_in[t // 2], it * 16 + 16)
                    wait_use(pe, xsT_ready, it, t, 2, per=RING)
                    pe.transpose(ps[:, t % 2, 0:P], xs[:, t // 2, t % 2, 0:D], ident[:, :]).then_inc(xsT_psum, 1)

                def up(it, t, e):
                    pe.wait_ge(xsT_ready, it * RING + t + 1)
                    wait_use(pe, hid_ready, it, t, 2, per=RING)
                    pe.matmul(ps[:, 2 + t % 2, :], xT_s[:, t % 2, :],
                              w12[:, bass.ds(e, 1), :].rearrange("p o n -> p (o n)"),
                              start=True, stop=True).then_inc(up_psum, 1)

                def turn_hidden(it, t):
                    pe.wait_ge(hid_ready, it * RING + t + 1)
                    wait_use(pe, hidT_ready, it, t, 2, per=RING)
                    for c in range(2):
                        last = pe.transpose(ps[:, 4 + t % 2, c * P:(c + 1) * P], hid[:, t % 2, c * P:(c + 1) * P],
                                            ident[:, :])
                    last.then_inc(hidT_psum, 1)

                def down(it, t, e):
                    pe.wait_ge(hidT_ready, it * RING + t + 1)
                    wait_use(pe, o_ready, it, t, 2, per=RING)
                    for c in range(2):
                        last = pe.matmul(ps[:, 6 + t % 2, 0:D], hidT[:, t % 2, c, :],
                                         w3_s[:, bass.ds(e, 1), c, :].rearrange("p o n -> p (o n)"),
                                         start=(c == 0), stop=(c == 1))
                    last.then_inc(o_psum, 1)

                def step(it, t, first=False, last=False):
                    if t == 0:
                        load_experts(it, last)
                    if not last:
                        turn(it, t)
                    if not (first and t < 1) and not (last and t >= 1):
                        up(*back(it, t, 1, RING), experts[LATE + t - 1])
                    if not (first and t < 2) and not (last and t >= 2):
                        turn_hidden(*back(it, t, 2, RING))
                    if not (first and t < 3):
                        down(*back(it, t, 3, RING), experts[LATE + t - 3])

                run(pe, step, ROUNDS, per=RING)

            @block.scalar
            def _(act):
                def take_x(it, t):
                    act.wait_ge(xsT_psum, it * RING + t + 1)
                    wait_use(act, up_psum, it, t, 2, per=RING)
                    act.activation(xT_s[:, t % 2, :], ps[:, t % 2, 0:P], ACT.Copy).then_inc(xsT_ready, 1)

                def silu(it, t):
                    act.wait_ge(up_psum, it * RING + t + 1)
                    wait_use(act, hid_ready, it, t, 2, per=RING)
                    act.activation(sil[:, t % 2, :], ps[:, 2 + t % 2, 0:HID], ACT.Silu).then_inc(sil_ready, 1)

                def take_out(it, t):
                    act.wait_ge(o_psum, it * RING + t + 1)
                    if not (isinstance(it, int) and it == 0):
                        act.wait_ge(y_out[t], it * 16)
                    act.activation(o_s[:, t, :], ps[:, 6 + t % 2, 0:D], ACT.Copy,
                                   scale=xs[:, t // 2, t % 2, D + 1:D + 2]).then_inc(o_ready, 1)

                def step(it, t, first=False, last=False):
                    if not last:
                        take_x(it, t)
                    if not (first and t < 1) and not (last and t >= 1):
                        silu(*back(it, t, 1, RING))
                    if not (first and t < 3):
                        take_out(*back(it, t, 3, RING))

                run(act, step, ROUNDS, per=RING)

            @block.vector
            def _(dve):
                def gate(it, t):
                    dve.wait_ge(sil_ready, it * RING + t + 1)
                    wait_use(dve, hidT_psum, it, t, 2, per=RING)
                    dve.tensor_tensor(hid[:, t % 2, :], sil[:, t % 2, :], ps[:, 2 + t % 2, HID:2 * HID],
                                      ALU.mult).then_inc(hid_ready, 1)

                def take_hidden(it, t):
                    dve.wait_ge(hidT_psum, it * RING + t + 1)
                    wait_use(dve, o_psum, it, t, 2, per=RING)
                    dve.tensor_copy(hidT[:, t % 2, :, :], ps[:, 4 + t % 2, 0:HID].rearrange(
                        "p (c i) -> p c i", c=2)).then_inc(hidT_ready, 1)

                def step(it, t, first=False, last=False):
                    if not (first and t < 1) and not (last and t >= 1):
                        gate(*back(it, t, 1, RING))
                    if not (first and t < 2) and not (last and t >= 2):
                        take_hidden(*back(it, t, 2, RING))

                run(dve, step, ROUNDS, per=RING)

        with ExitStack() as c8:
            def sem8(name):
                return c8.enter_context(nc.semaphore(name))

            y_in = [sem8(f"y_in{i}") for i in range(NRES)]
            taken = sem8("taken")
            summed = sem8("summed")
            out_done = sem8("out_done")
            block = c8.enter_context(nc.Block())

            @block.scalar
            def _(act):
                for g in range(NG):
                    if g >= NRES:
                        act.wait_ge(summed, g - NRES + 1)
                    for k in range(K):
                        at_row = k * N + g * GR
                        act.dma_start(result[:, g % NRES, k, :, :], y_d[at_row:at_row + GR, :].rearrange(
                            "(b p) d -> p b d", p=P)).then_inc(y_in[g % NRES], 16)

            @block.vector
            def _(dve):
                for g in range(NG):
                    dve.wait_ge(y_in[g % NRES], (g // NRES + 1) * 16 * K)
                    xg = X[:, g * GB:(g + 1) * GB, :]
                    dve.tensor_tensor(xg, xg, result[:, g % NRES, 0, :, :], ALU.add).then_inc(taken, 1)
                    dve.wait_ge(taken, g + 1)
                    dve.tensor_tensor(xg, xg, result[:, g % NRES, 1, :, :], ALU.add).then_inc(summed, 1)

            @block.sync
            def _(sp):
                for g in range(NG):
                    sp.wait_ge(summed, g + 1)
                    sp.dma_start(out[g * GR:(g + 1) * GR, :].rearrange("(b p) d -> p b d", p=P),
                                 X[:, g * GB:(g + 1) * GB, :]).then_inc(out_done, 16)
                sp.wait_ge(out_done, 16 * NG)

_INS = ["x", "adj", "L0_gnn_Wq", "L0_gnn_Wk", "L0_gnn_Wv", "L0_gnn_a", "L0_ffn_ln_w", "L0_ffn_ln_b", "L0_ffn_W",
        "L0_ffn_b", "L1_gnn_a", "L1_ffn_gate_w", "L1_ffn_gate_b", "L1_ffn_w1", "L1_ffn_w2", "L1_ffn_w3"]


def build(nc, inputs):
    import numpy as _np
    from concourse import mybir as _mybir

    arrays, args = {}, []
    for name in _INS:
        a = _np.asarray(inputs[name])
        if name == "adj":
            a = a.reshape(NG, GR, NT, JT, P).transpose(0, 2, 4, 3, 1).reshape(NG, NT, P, JT * GR)
        if name in ("L0_gnn_a", "L1_gnn_a"):
            a = a.reshape(2, D).T
        a = _np.ascontiguousarray(a)
        arrays[f"in_{name}_dram"] = a
        args.append(nc.dram_tensor(f"in_{name}_dram", a.shape, _mybir.dt.from_np(a.dtype), kind="ExternalInput").ap())
    out = nc.dram_tensor("out_0_dram", (N, D), _mybir.dt.float32, kind="ExternalOutput").ap()
    network(nc, *args, out)
    return arrays


def kernel(**inputs):
    import concourse.bacc as _bacc
    from concourse.bass_utils import run_bass_kernel_spmd as _run

    nc = _bacc.Bacc("TRN2", target_bir_lowering=False, num_devices=1)
    arrays = build(nc, inputs)
    r = _run(nc, [arrays], core_ids=[0])
    return r.results[0]["out_0_dram"]
```
